# Optimizing a Trainium2 kernel written in Bass

```python
import numpy as np
import jax
import jax.numpy as jnp

def _softmax(x, axis=-1):
    return jax.nn.softmax(x, axis=axis)

def _gelu(x):
    return jax.nn.gelu(x, approximate=True)

def _silu(x):
    return jax.nn.silu(x)

def _sigmoid(x):
    return jax.nn.sigmoid(x)

def _layernorm(x, axis=-1, eps=1e-05):
    m = jnp.mean(x, axis=axis, keepdims=True)
    v = jnp.var(x, axis=axis, keepdims=True)
    return (x - m) / jnp.sqrt(v + eps)

def _scatter_add(tgt, idx, src, axis=0):
    return tgt.at[idx].add(src)

def _segment_sum(src, seg, n):
    return jax.ops.segment_sum(src, seg, n)
kernel_name = 'mk_adaln_d1_jaxref_r4_873f2f'

def setup_inputs(seed: int=0):
    np.random.seed(seed)
    _w = jnp.asarray

    def _L0_attn_setup():
        import jax, jax.numpy as jnp
        import numpy as np
        B, L, D, H = (2, 1024, 256, 4)
        DK = D // H
        DV = D // H
        CHUNK, FIRS, FIRL, CONV, GROUP = (32, 3, 31, 4, 2)
        EPS_ID, R_EPS = (0.06, 0.025)
        R_HID = 2 * D
        R_IN = D + H * 6

        def _l2norm(x, eps=1e-06):
            return x * jax.lax.rsqrt(jnp.sum(x * x, -1, keepdims=True) + eps)

        def _causal_dwconv(x, w):
            c = x.shape[-1]
            k = w.shape[-1]
            lhs = jnp.swapaxes(x, 1, 2)
            rhs = w[:, None, :]
            y = jax.lax.conv_general_dilated(lhs, rhs, window_strides=(1,), padding=[(k - 1, 0)], dimension_numbers=('NCH', 'OIH', 'NCH'), feature_group_count=c)
            return jnp.swapaxes(y, 1, 2)

        def _fir(x, filt):
            b, l, h, d = x.shape
            y = _causal_dwconv(x.reshape(b, l, h * d), filt.reshape(h * d, -1))
            return y.reshape(b, l, h, d)

        def _delta_rule_chunkwise(q, k, v, beta, chunk=CHUNK):
            b, h, Ls, dk = q.shape
            dv = v.shape[-1]
            n = Ls // chunk
            q = _l2norm(q)
            k = _l2norm(k)
            v = v * beta[..., None]
            kb = k * beta[..., None]
            rs = lambda t: t.reshape(b, h, n, chunk, -1)
            q, k, v, kb = map(rs, (q, k, v, kb))
            tri = jnp.triu(jnp.ones((chunk, chunk), bool), 0)
            T = jnp.where(tri, 0.0, -(kb @ jnp.swapaxes(k, -1, -2)))
            for i in range(1, chunk):
                T = T.at[..., i, :].add(jnp.einsum('...j,...jl->...l', T[..., i, :], T))
            T = T + jnp.eye(chunk, dtype=T.dtype)
            u = T @ v
            w = T @ kb
            fmask = jnp.triu(jnp.ones((chunk, chunk), bool), 1)
            mv = lambda t: jnp.moveaxis(t, 2, 0)

            def step(S, xs):
                qi, ki, ui, wi = xs
                attn = jnp.where(fmask, 0.0, qi @ jnp.swapaxes(ki, -1, -2))
                u2 = ui - wi @ S
                oi = qi @ S + attn @ u2
                return (S + jnp.swapaxes(ki, -1, -2) @ u2, oi)
            S0 = jnp.zeros((b, h, dk, dv), q.dtype)
            S, o = jax.lax.scan(step, S0, (mv(q), mv(k), mv(u), mv(w)))
            return (jnp.moveaxis(o, 0, 2).reshape(b, h, Ls, dv), S)
        key = jax.random.key(seed)
        ks = jax.random.split(key, 20)
        lin = lambda kk, i, o: 0.02 * jax.random.normal(kk, (i, o), jnp.float32)

        def fir(kk, kern):
            base = jnp.zeros((H, DV, kern), jnp.float32).at[:, :, -1].set(1.0)
            return base + 0.01 * jax.random.normal(kk, (H, DV, kern), jnp.float32)
        return {'hidden_states': jax.random.normal(ks[0], (B, L, D), jnp.float32), 'Wq': lin(ks[1], D, H * DK), 'Wk': lin(ks[2], D, H * DK), 'Wv': lin(ks[3], D, H * DV), 'Wb': lin(ks[4], D, H), 'conv_q': 0.3 * jax.random.normal(ks[5], (H * DK, CONV), jnp.float32), 'conv_k': 0.3 * jax.random.normal(ks[6], (H * DK, CONV), jnp.float32), 'conv_v': 0.3 * jax.random.normal(ks[7], (H * DV, CONV), jnp.float32), 'fir_short': fir(ks[8], FIRS), 'fir_long': fir(ks[9], FIRL), 'alpha_id': jnp.zeros((H,), jnp.float32), 'Wid': lin(ks[10], D, H), 'bid': jnp.zeros((H,), jnp.float32), 'Wr1': lin(ks[11], R_IN, R_HID), 'br1': jnp.zeros((R_HID,), jnp.float32), 'Wr2': lin(ks[12], R_HID, H * 3), 'br2': jnp.zeros((H * 3,), jnp.float32), 'log_tau_group': jnp.zeros(((H + GROUP - 1) // GROUP,), jnp.float32), 'log_tau_head': jnp.zeros((H,), jnp.float32), 'o_norm_w': jnp.ones((DV,), jnp.float32), 'Wo': lin(ks[13], H * DV, D)}
    _L0_attn_in = _L0_attn_setup()

    def _L0_ffn_setup():
        import jax, jax.numpy as jnp
        import numpy as np
        TOP_K = 4
        N_GROUP = 4
        TOPK_GROUP = 2
        ROUTED_SCALING = 2.5

        def _route(x, gate_weight):
            scores = jax.nn.sigmoid(x @ gate_weight.T)
            T, E = scores.shape
            gs = E // N_GROUP
            top2, _ = jax.lax.top_k(scores.reshape(T, N_GROUP, gs), 2)
            group_scores = top2.sum(-1)
            _, gidx = jax.lax.top_k(group_scores, TOPK_GROUP)
            gmask = jax.nn.one_hot(gidx, N_GROUP, dtype=jnp.float32).sum(1)
            smask = jnp.repeat(gmask, gs, axis=1) > 0.5
            masked = jnp.where(smask, scores, 0.0)
            topk_idx = jax.lax.top_k(masked, TOP_K)[1]
            topk_w = jnp.take_along_axis(scores, topk_idx, axis=1)
            topk_w = topk_w / (topk_w.sum(-1, keepdims=True) + 1e-20)
            topk_w = topk_w * ROUTED_SCALING
            combine = jnp.zeros((T, E), jnp.float32).at[jnp.arange(T)[:, None], topk_idx].add(topk_w)
            return combine
        key = jax.random.key(seed)
        ks = jax.random.split(key, 6)
        B, S, H = (2, 256, 256)
        E, I, Is = (16, 128, 512)
        g = lambda k, shape, scale: jax.random.normal(k, shape, dtype=jnp.float32) * scale
        return {'hidden_states': g(ks[0], (B, S, H), 1.0), 'gate_weight': g(ks[1], (E, H), 0.02), 'expert_up': g(ks[2], (E, H, I), 0.02), 'expert_down': g(ks[3], (E, I, H), 0.02), 'shared_up': g(ks[4], (H, Is), 0.02), 'shared_down': g(ks[5], (Is, H), 0.02)}
    _L0_ffn_in = _L0_ffn_setup()
    _L0_c = _w((lambda *s: np.random.randn(*s).astype(np.float32) * 0.05)(4, 256))
    _L0_wmod = _w((lambda *s: np.random.randn(*s).astype(np.float32) * 0.05)(256, 6 * 256) * 256 ** (-0.5))
    _d = {'L0_attn_hidden_states': _L0_attn_in['hidden_states'], 'L0_attn_Wq': _L0_attn_in['Wq'], 'L0_attn_Wk': _L0_attn_in['Wk'], 'L0_attn_Wv': _L0_attn_in['Wv'], 'L0_attn_Wb': _L0_attn_in['Wb'], 'L0_attn_conv_q': _L0_attn_in['conv_q'], 'L0_attn_conv_k': _L0_attn_in['conv_k'], 'L0_attn_conv_v': _L0_attn_in['conv_v'], 'L0_attn_fir_short': _L0_attn_in['fir_short'], 'L0_attn_fir_long': _L0_attn_in['fir_long'], 'L0_attn_alpha_id': _L0_attn_in['alpha_id'], 'L0_attn_Wid': _L0_attn_in['Wid'], 'L0_attn_bid': _L0_attn_in['bid'], 'L0_attn_Wr1': _L0_attn_in['Wr1'], 'L0_attn_br1': _L0_attn_in['br1'], 'L0_attn_Wr2': _L0_attn_in['Wr2'], 'L0_attn_br2': _L0_attn_in['br2'], 'L0_attn_log_tau_group': _L0_attn_in['log_tau_group'], 'L0_attn_log_tau_head': _L0_attn_in['log_tau_head'], 'L0_attn_o_norm_w': _L0_attn_in['o_norm_w'], 'L0_attn_Wo': _L0_attn_in['Wo'], 'L0_ffn_gate_weight': _L0_ffn_in['gate_weight'], 'L0_ffn_expert_up': _L0_ffn_in['expert_up'], 'L0_ffn_expert_down': _L0_ffn_in['expert_down'], 'L0_ffn_shared_up': _L0_ffn_in['shared_up'], 'L0_ffn_shared_down': _L0_ffn_in['shared_down'], 'L0_c': _L0_c, 'L0_wmod': _L0_wmod}
    _x0 = _d['L0_attn_hidden_states']
    _d['L0_attn_hidden_states'] = jax.random.normal(jax.random.fold_in(jax.random.key(seed), 1), (4, 2048, 256), dtype=_x0.dtype)
    del _x0
    return _d

def reference(L0_attn_hidden_states, L0_attn_Wq, L0_attn_Wk, L0_attn_Wv, L0_attn_Wb, L0_attn_conv_q, L0_attn_conv_k, L0_attn_conv_v, L0_attn_fir_short, L0_attn_fir_long, L0_attn_alpha_id, L0_attn_Wid, L0_attn_bid, L0_attn_Wr1, L0_attn_br1, L0_attn_Wr2, L0_attn_br2, L0_attn_log_tau_group, L0_attn_log_tau_head, L0_attn_o_norm_w, L0_attn_Wo, L0_ffn_gate_weight, L0_ffn_expert_up, L0_ffn_expert_down, L0_ffn_shared_up, L0_ffn_shared_down, L0_c, L0_wmod):

    def _L0_attn_ref(hidden_states, Wq, Wk, Wv, Wb, conv_q, conv_k, conv_v, fir_short, fir_long, alpha_id, Wid, bid, Wr1, br1, Wr2, br2, log_tau_group, log_tau_head, o_norm_w, Wo):
        import jax, jax.numpy as jnp
        import numpy as np
        B, L, D, H = (2, 1024, 256, 4)
        DK = D // H
        DV = D // H
        CHUNK, FIRS, FIRL, CONV, GROUP = (32, 3, 31, 4, 2)
        EPS_ID, R_EPS = (0.06, 0.025)
        R_HID = 2 * D
        R_IN = D + H * 6

        def _l2norm(x, eps=1e-06):
            return x * jax.lax.rsqrt(jnp.sum(x * x, -1, keepdims=True) + eps)

        def _causal_dwconv(x, w):
            c = x.shape[-1]
            k = w.shape[-1]
            lhs = jnp.swapaxes(x, 1, 2)
            rhs = w[:, None, :]
            y = jax.lax.conv_general_dilated(lhs, rhs, window_strides=(1,), padding=[(k - 1, 0)], dimension_numbers=('NCH', 'OIH', 'NCH'), feature_group_count=c)
            return jnp.swapaxes(y, 1, 2)

        def _fir(x, filt):
            b, l, h, d = x.shape
            y = _causal_dwconv(x.reshape(b, l, h * d), filt.reshape(h * d, -1))
            return y.reshape(b, l, h, d)

        def _delta_rule_chunkwise(q, k, v, beta, chunk=CHUNK):
            b, h, Ls, dk = q.shape
            dv = v.shape[-1]
            n = Ls // chunk
            q = _l2norm(q)
            k = _l2norm(k)
            v = v * beta[..., None]
            kb = k * beta[..., None]
            rs = lambda t: t.reshape(b, h, n, chunk, -1)
            q, k, v, kb = map(rs, (q, k, v, kb))
            tri = jnp.triu(jnp.ones((chunk, chunk), bool), 0)
            T = jnp.where(tri, 0.0, -(kb @ jnp.swapaxes(k, -1, -2)))
            for i in range(1, chunk):
                T = T.at[..., i, :].add(jnp.einsum('...j,...jl->...l', T[..., i, :], T))
            T = T + jnp.eye(chunk, dtype=T.dtype)
            u = T @ v
            w = T @ kb
            fmask = jnp.triu(jnp.ones((chunk, chunk), bool), 1)
            mv = lambda t: jnp.moveaxis(t, 2, 0)

            def step(S, xs):
                qi, ki, ui, wi = xs
                attn = jnp.where(fmask, 0.0, qi @ jnp.swapaxes(ki, -1, -2))
                u2 = ui - wi @ S
                oi = qi @ S + attn @ u2
                return (S + jnp.swapaxes(ki, -1, -2) @ u2, oi)
            S0 = jnp.zeros((b, h, dk, dv), q.dtype)
            S, o = jax.lax.scan(step, S0, (mv(q), mv(k), mv(u), mv(w)))
            return (jnp.moveaxis(o, 0, 2).reshape(b, h, Ls, dv), S)
        x = hidden_states
        b, l = x.shape[:2]
        q = jax.nn.silu(_causal_dwconv(x @ Wq, conv_q))
        k = jax.nn.silu(_causal_dwconv(x @ Wk, conv_k))
        v = jax.nn.silu(_causal_dwconv(x @ Wv, conv_v))
        qh = q.reshape(b, l, H, DK)
        kh = k.reshape(b, l, H, DK)
        vh = v.reshape(b, l, H, DV)
        beta = jax.nn.sigmoid(x @ Wb)
        bhld = lambda t: jnp.transpose(t, (0, 2, 1, 3))
        delta, _S = _delta_rule_chunkwise(bhld(qh), bhld(kh), bhld(vh), jnp.transpose(beta, (0, 2, 1)))
        delta = jnp.transpose(delta, (0, 2, 1, 3))
        fs = _fir(vh, fir_short)
        fl = _fir(vh, fir_long)
        stats = jnp.concatenate([fs.mean(-1), fs.std(-1), fl.mean(-1), fl.std(-1), delta.mean(-1), delta.std(-1)], -1)
        router_in = jnp.concatenate([x, stats], -1)
        hmid = jax.nn.gelu(router_in @ Wr1 + br1, approximate=False)
        logits = (hmid @ Wr2 + br2).reshape(b, l, H, 3)
        group_idx = jnp.arange(H) // GROUP
        tau = jnp.exp(log_tau_group)[group_idx] + 0.0 * jnp.exp(log_tau_head)
        p = jax.nn.softmax(logits / tau[None, None, :, None], -1)
        p = p * (1.0 - 3.0 * R_EPS) + R_EPS
        o = p[..., 0:1] * fs + p[..., 1:2] * fl + p[..., 2:3] * delta
        id_scale = EPS_ID + jax.nn.sigmoid(alpha_id)[None, None, :] * jax.nn.sigmoid(x @ Wid + bid)
        o = o + id_scale[..., None] * vh
        o = o * jax.lax.rsqrt(jnp.mean(o * o, -1, keepdims=True) + 1e-05) * o_norm_w
        return o.reshape(b, l, H * DV) @ Wo

    def _L0_ffn_ref(hidden_states, gate_weight, expert_up, expert_down, shared_up, shared_down):
        import jax, jax.numpy as jnp
        import numpy as np
        TOP_K = 4
        N_GROUP = 4
        TOPK_GROUP = 2
        ROUTED_SCALING = 2.5

        def _route(x, gate_weight):
            scores = jax.nn.sigmoid(x @ gate_weight.T)
            T, E = scores.shape
            gs = E // N_GROUP
            top2, _ = jax.lax.top_k(scores.reshape(T, N_GROUP, gs), 2)
            group_scores = top2.sum(-1)
            _, gidx = jax.lax.top_k(group_scores, TOPK_GROUP)
            gmask = jax.nn.one_hot(gidx, N_GROUP, dtype=jnp.float32).sum(1)
            smask = jnp.repeat(gmask, gs, axis=1) > 0.5
            masked = jnp.where(smask, scores, 0.0)
            topk_idx = jax.lax.top_k(masked, TOP_K)[1]
            topk_w = jnp.take_along_axis(scores, topk_idx, axis=1)
            topk_w = topk_w / (topk_w.sum(-1, keepdims=True) + 1e-20)
            topk_w = topk_w * ROUTED_SCALING
            combine = jnp.zeros((T, E), jnp.float32).at[jnp.arange(T)[:, None], topk_idx].add(topk_w)
            return combine
        B, S, H = hidden_states.shape
        x = hidden_states.reshape(-1, H)
        combine = _route(x.astype(jnp.float32), gate_weight)
        up = jnp.einsum('th,ehi->eti', x, expert_up)
        down = jnp.einsum('eti,eih->eth', jax.nn.silu(up), expert_down)
        moe_out = jnp.einsum('te,eth->th', combine, down)
        shared = jax.nn.silu(x @ shared_up) @ shared_down
        return (moe_out + shared).reshape(B, S, H)
    x = L0_attn_hidden_states
    mod = (_silu(L0_c) @ L0_wmod).reshape(L0_c.shape[0], 6, 1, -1)
    sa, ca, ga, sb, cb, gb = (mod[:, 0], mod[:, 1], mod[:, 2], mod[:, 3], mod[:, 4], mod[:, 5])
    ga = (2 * (ga >= 0) - 1) * jnp.maximum(jnp.abs(ga), 0.25)
    gb = (2 * (gb >= 0) - 1) * jnp.maximum(jnp.abs(gb), 0.25)
    h = _layernorm(x, axis=-1) * (1 + ca) + sa
    x = x + ga * _L0_attn_ref(h, L0_attn_Wq, L0_attn_Wk, L0_attn_Wv, L0_attn_Wb, L0_attn_conv_q, L0_attn_conv_k, L0_attn_conv_v, L0_attn_fir_short, L0_attn_fir_long, L0_attn_alpha_id, L0_attn_Wid, L0_attn_bid, L0_attn_Wr1, L0_attn_br1, L0_attn_Wr2, L0_attn_br2, L0_attn_log_tau_group, L0_attn_log_tau_head, L0_attn_o_norm_w, L0_attn_Wo)
    h = _layernorm(x, axis=-1) * (1 + cb) + sb
    x = x + gb * _L0_ffn_ref(h, L0_ffn_gate_weight, L0_ffn_expert_up, L0_ffn_expert_down, L0_ffn_shared_up, L0_ffn_shared_down)
    return x

_drawn_inputs = setup_inputs


def setup_inputs(seed=0):
    import zlib

    import numpy as np

    out = dict(_drawn_inputs(seed))
    spreads = {'L0_attn_alpha_id': (0.0, 2.0),
     'L0_attn_bid': (0.0, 2.0),
     'L0_attn_br1': (0.0, 0.8),
     'L0_attn_br2': (0.0, 0.8),
     'L0_attn_log_tau_group': (0.0, 0.8),
     'L0_attn_log_tau_head': (0.0, 0.1),
     'L0_attn_o_norm_w': (1.0, 0.6)}
    factors = {'L0_attn_Wq': 3.198,
     'L0_attn_Wk': 3.179,
     'L0_attn_Wb': 8.0,
     'L0_attn_conv_q': 3.191,
     'L0_attn_conv_k': 3.128,
     'L0_attn_Wid': 21.493,
     'L0_attn_Wr1': 8.0,
     'L0_attn_Wr2': 8.0,
     'L0_ffn_gate_weight': 5.632,
     'L0_ffn_expert_up': 4.887,
     'L0_ffn_expert_down': 4.841,
     'L0_ffn_shared_up': 3.055,
     'L0_ffn_shared_down': 3.024}
    for name, (base, spread) in spreads.items():
        noise = np.random.default_rng([zlib.crc32(name.encode()), seed]).standard_normal(out[name].shape)
        drawn = base * np.exp(spread * noise) if base else spread * noise
        out[name] = jnp.asarray(drawn.astype(out[name].dtype))
    for name, factor in factors.items():
        out[name] = (out[name] * factor).astype(out[name].dtype)
    return out
```

```python
from contextlib import ExitStack

import concourse.bass as bass
from concourse import mybir

ALU = mybir.AluOpType
ACT = mybir.ActivationFunctionType
F32 = mybir.dt.float32
AX_X = mybir.AxisListType.X

P = 128
B, L, D, H = 4, 2048, 256, 4
DK = D // H
KD = D // P
UT = 512
J = UT // P
UB = L // UT
NU = B * UB
TB = L // P
NT = B * TB
CONV, FIRS, FIRL = 4, 3, 31
E, EI, SI = 16, 128, 512
NG, TOPK, SCALING = 4, 4, 2.5
RH = 2 * D
LN_EPS, L2_EPS, RMS_EPS = 1e-5, 1e-6, 1e-5
EPS_ID, R_EPS = 0.06, 0.025
TOEP = P + 32
TAPROW = P + TOEP

SCRATCH = ["hT_d", "vf_d", "kq_d", "kqT_d", "taps_d", "toep_d", "fl_d", "o_d", "x2_d", "h2T_d", "gates_d", "comb_d"]


class Bag:
    pass


def setup(nc, m, w):
    with ExitStack() as ctx:
        def sb(name, shape):
            return ctx.enter_context(nc.sbuf_tensor(name, shape, F32))

        def sem(name):
            return ctx.enter_context(nc.semaphore(name))

        cT = sb("cT", [P, KD, B])
        scT = sb("scT", [P, KD, B])
        scB = sb("scB", [P, KD, B, P])
        zeros = sb("zeros", [P, P])
        wmod = sb("wmod", [P, KD, 6 * D])
        gatesB = sb("gatesB", [P, 2, B, D])
        gsign = sb("gsign", [P, 2, B, D])
        taus = sb("taus", [P, 8])
        fs_w = sb("fs_w", [P, KD, FIRS])
        fl_w = sb("fl_w", [P, KD, FIRL])
        onw = sb("onw", [P, 1])
        wo = sb("wo", [P, KD, D])
        taps = sb("taps", [P, KD, TAPROW])
        ps = ctx.enter_context(nc.psum_tensor("ps_setup", [P, 8, 512], F32))
        modt_ps = ps[:, 0, 0:48].rearrange("p (a b) -> p a b", b=B)

        c_in = sem("c_in")
        w_in = sem("w_in")
        small_in = sem("small_in")
        rest_in = sem("rest_in")
        taps_out = sem("taps_out")
        taps_placed = sem("taps_placed")
        zero_done = sem("zero_done")
        pool_step = sem("pool_step")
        silu_done = sem("silu_done")
        bcast_done = sem("bcast_done")
        mm_done = sem("mm_done")
        act_step = sem("act_step")
        vec_step = sem("vec_step")

        ctx.enter_context(nc.allow_non_contiguous_dma(reason="small vectors and weights, loaded once"))
        block = ctx.enter_context(nc.Block("setup"))

        @block.sync
        def _(sp):
            for b in range(B):
                for k in range(KD):
                    sp.dma_start(cT[:, k, b:b + 1], w.c[b, k * P:(k + 1) * P].unsqueeze(1)).then_inc(c_in, 16)
            sp.dma_start(wmod[:], w.wmod.rearrange("(k p) n -> p k n", p=P)).then_inc(w_in, 16)
            col = lambda a, k: a[k * P:(k + 1) * P, :]
            for k in range(KD):
                for i, a in enumerate((w.conv_v, w.conv_k, w.conv_q)):
                    sp.dma_start(m.conv_w[:, 2 * i + k, :], col(a, k)).then_inc(small_in, 16)
                sp.dma_start(fs_w[:, k, :], w.fir_short.rearrange("h d t -> (h d) t")[k * P:(k + 1) * P, :])\
                    .then_inc(small_in, 16)
            for i in range(2):
                sp.dma_start(onw[i * DK:(i + 1) * DK, :], w.o_norm_w.unsqueeze(1)).then_inc(small_in, 16)
            sp.dma_start(taus[:, 0:2], w.log_tau_group.partition_broadcast(P)).then_inc(small_in, 16)
            sp.dma_start(taus[:, 4:8], w.log_tau_head.partition_broadcast(P)).then_inc(small_in, 16)
            sp.dma_start(m.alpha[:], w.alpha_id.partition_broadcast(P)).then_inc(small_in, 16)
            sp.dma_start(wo[:], w.Wo.rearrange("(k p) n -> p k n", p=P)).then_inc(small_in, 16)
            for i, a in enumerate((w.Wv, w.Wk, w.Wq)):
                sp.dma_start(m.wqkv[:, :, i * D:(i + 1) * D], a.rearrange("(k p) n -> p k n", p=P))\
                    .then_inc(rest_in, 16)
            sp.dma_start(m.wgate[:, :, 0:H], w.Wb.rearrange("(k p) n -> p k n", p=P)).then_inc(rest_in, 16)
            sp.dma_start(m.wgate[:, :, H:2 * H], w.Wid.rearrange("(k p) n -> p k n", p=P)).then_inc(rest_in, 16)
            sp.dma_start(m.bid_row[0:1, H:2 * H], w.bid.unsqueeze(0)).then_inc(rest_in, 16)
            sp.dma_start(m.wr1[:], w.Wr1[0:D, :].rearrange("(k p) n -> p k n", p=P)).then_inc(rest_in, 16)
            sp.dma_start(m.wr1s[0:6 * H, :], w.Wr1[D:D + 6 * H, :]).then_inc(rest_in, 16)
            for i in range(RH // P):
                sp.dma_start(m.br1[:, i:i + 1], w.br1[i * P:(i + 1) * P].unsqueeze(1)).then_inc(rest_in, 16)
            sp.dma_start(m.wr2[:], w.Wr2.rearrange("(k p) n -> p k n", p=P)).then_inc(rest_in, 16)
            sp.dma_start(m.br2[0:1, :], w.br2.unsqueeze(0)).then_inc(rest_in, 16)
            for k in range(KD):
                sp.dma_start(m.wgT[:, k, :], w.gate_weight[:, k * P:(k + 1) * P].rearrange("e p -> p e"))\
                    .then_inc(rest_in, 16)
            n_rest = 16 * (3 + 3 + 2 + RH // P + 2 + KD)
            sp.wait_ge(zero_done, 1)
            for k in range(KD):
                sp.dma_start(fl_w[:, k, :], w.fir_long.rearrange("h d t -> (h d) t")[k * P:(k + 1) * P, :])\
                    .then_inc(taps_out, 16)
            sp.wait_ge(taps_placed, FIRL)
            sp.dma_start(m.taps_d.rearrange("(k p) n -> p k n", p=P), taps[:]).then_inc(taps_out, 16)
            sp.wait_ge(taps_out, 16 * KD + 16)
            sp.wait_ge(rest_in, n_rest)

        @block.gpsimd
        def _(pool):
            pool.memset(taps[:], 0.0).then_inc(pool_step, 1)
            pool.memset(zeros[:], 0.0).then_inc(pool_step, 1)
            pool.memset(m.ones[:], 1.0).then_inc(pool_step, 1)
            pool.memset(m.ident[:], 0.0).then_inc(pool_step, 1)
            pool.memset(m.flip[:], 0.0).then_inc(pool_step, 1)
            pool.memset(m.lower[:], 1.0).then_inc(pool_step, 1)
            pool.memset(m.upper[:], 1.0).then_inc(pool_step, 1)
            pool.memset(m.first_lower[:], 0.0).then_inc(pool_step, 1)
            for s in range(len(m.levels)):
                pool.memset(m.level_mask[s][:], 0.0).then_inc(pool_step, 1)
            pool.memset(m.zeros[:], 0.0).then_inc(pool_step, 1)
            pool.memset(m.half_pow[:], -0.5).then_inc(pool_step, 1)
            pool.memset(m.root_pow[:], 0.5).then_inc(pool_step, 1)
            pool.memset(m.l2_eps[:], L2_EPS).then_inc(pool_step, 1)
            pool.memset(m.bid_row[:, 0:H], 0.0).then_inc(pool_step, 1)
            n = 8 + len(m.levels) + 5
            pool.wait_ge(pool_step, n)
            pool.sem_inc(zero_done, 1)
            pool.affine_select(out=m.flip[:], in_=m.flip[:], compare_op=ALU.not_equal, fill=1.0, base=1 - P,
                               pattern=[[1, P]], channel_multiplier=1).then_inc(pool_step, 1)
            pool.affine_select(out=m.ident[:], in_=m.ident[:], compare_op=ALU.not_equal, fill=1.0, base=0,
                               pattern=[[-1, P]], channel_multiplier=1).then_inc(pool_step, 1)
            pool.affine_select(out=m.lower[:], in_=m.lower[:], compare_op=ALU.is_gt, fill=0.0, base=0,
                               pattern=[[-1, P]], channel_multiplier=1).then_inc(pool_step, 1)
            pool.affine_select(out=m.upper[:], in_=m.upper[:], compare_op=ALU.is_ge, fill=0.0, base=0,
                               pattern=[[0, H], [1, P]], channel_multiplier=-1).then_inc(pool_step, 1)
            v = m.first_lower.ap().rearrange("p h (n two) -> p h n two", two=2)[:, :, :, 0]
            pool.affine_select(out=v, in_=v, compare_op=ALU.not_equal, fill=1.0, base=-1,
                               pattern=[[0, H], [-2, P // 2]], channel_multiplier=1).then_inc(pool_step, 1)
            n += 5
            for i, s in enumerate(m.levels):
                v = m.level_mask[i].ap().rearrange("p h (n two s) -> p h n two s", two=2, s=s)
                nb = P // (2 * s)
                for h in range(H):
                    vh = v[:, h, :, 1, :]
                    pool.memset(vh, 1.0).then_inc(pool_step, 1)
                    n += 1
                    pool.wait_ge(pool_step, n)
                    pool.affine_select(out=vh, in_=vh, compare_op=ALU.is_ge, fill=0.0, base=0,
                                       pattern=[[-2 * s, nb], [0, s]], channel_multiplier=1).then_inc(pool_step, 1)
                    n += 1
                    pool.wait_ge(pool_step, n)
                    pool.affine_select(out=vh, in_=vh, compare_op=ALU.is_ge, fill=0.0, base=s - 1,
                                       pattern=[[2 * s, nb], [0, s]], channel_multiplier=-1).then_inc(pool_step, 1)
                    n += 1

            pool.wait_ge(pool_step, n)
            pool.sem_inc(zero_done, 1)

        @block.scalar
        def _(act):
            act.wait_ge(c_in, 16 * KD * B)
            act.activation(scT[:], cT[:], ACT.Silu).then_inc(silu_done, 1)
            act.wait_ge(mm_done, 1)
            act.activation(m.mod[:], modt_ps, ACT.Copy).then_inc(act_step, 1)
            act.wait_ge(mm_done, 2)
            act.activation(gatesB.ap().rearrange("p g b d -> p (g b d)"), ps[:, 1:5, :].rearrange("p a b -> p (a b)"), ACT.Copy).then_inc(act_step, 1)
            act.wait_ge(small_in, 16 * (4 * KD + 6))
            act.activation(taus[:, 0:2], taus[:, 0:2], ACT.Exp).then_inc(act_step, 1)
            act.activation(taus[:, 4:8], taus[:, 4:8], ACT.Exp).then_inc(act_step, 1)
            act.activation(m.alpha[:], m.alpha[:], ACT.Sigmoid).then_inc(act_step, 1)

        @block.tensor
        def _(pe):
            pe.wait_ge(w_in, 16)
            pe.wait_ge(silu_done, 1)
            for a in range(12):
                for k in range(KD):
                    mm = pe.matmul(modt_ps[:, a, :], wmod[:, k, a * P:(a + 1) * P], scT[:, k, :],
                                   start=(k == 0), stop=(k == KD - 1))
            mm.then_inc(mm_done, 1)
            pe.wait_ge(bcast_done, 1)
            for g in range(2):
                for b in range(B):
                    o = (g * B + b) * D
                    out = ps[:, 1 + o // 512, o % 512:o % 512 + D]
                    for k in range(KD):
                        mm = pe.matmul(out, scB[:, k, b, :], wmod[:, k, (2 + 3 * g) * D:(3 + 3 * g) * D],
                                       start=(k == 0), stop=(k == KD - 1))
            mm.then_inc(mm_done, 1)

        @block.vector
        def _(dve):
            dve.wait_ge(zero_done, 1)
            dve.wait_ge(taps_out, 16 * KD)
            for t in range(FIRL):
                c = P - 1 + FIRL - 1 - t
                dve.tensor_copy(taps[:, :, c:c + 1], fl_w[:, :, t:t + 1]).then_inc(taps_placed, 1)
            dve.wait_ge(silu_done, 1)
            dve.wait_ge(zero_done, 2)
            for k in range(KD):
                for b in range(B):
                    ins = dve.tensor_scalar(scB[:, k, b, :], zeros[:], scT[:, k, b:b + 1], None, ALU.add)
            ins.then_inc(bcast_done, 1)
            dve.wait_ge(act_step, 1)
            dve.tensor_scalar(m.mod[:, 2:4, :], m.mod[:, 2:4, :], 1.0, None, ALU.add).then_inc(vec_step, 1)
            dve.tensor_scalar(m.mod[:, 8:10, :], m.mod[:, 8:10, :], 1.0, None, ALU.add).then_inc(vec_step, 1)
            dve.wait_ge(act_step, 2)
            dve.tensor_scalar(gsign[:], gatesB[:], 0.0, 2.0, ALU.is_ge, ALU.mult).then_inc(vec_step, 1)
            dve.scalar_tensor_tensor(out=gatesB[:], in0=gatesB[:], scalar=-1.0, in1=gatesB[:], op0=ALU.mult,
                                     op1=ALU.max).then_inc(vec_step, 1)
            dve.wait_ge(vec_step, 4)
            dve.tensor_scalar(gatesB[:], gatesB[:], 0.25, None, ALU.max).then_inc(vec_step, 1)
            dve.tensor_scalar(gsign[:], gsign[:], -1.0, None, ALU.add).then_inc(vec_step, 1)
            dve.wait_ge(vec_step, 6)
            dve.tensor_tensor(gatesB[:], gatesB[:], gsign[:], ALU.mult).then_inc(vec_step, 1)
            dve.wait_ge(vec_step, 7)
            dve.tensor_copy(m.gbB[:], gatesB[:, 1]).then_inc(vec_step, 1)
            dve.wait_ge(small_in, 16 * (4 * KD + 6))
            for b in range(B):
                for k in range(KD):
                    dve.scalar_tensor_tensor(out=m.wog[:, b, k, :], in0=wo[:, k, :], scalar=onw[:, 0:1],
                                             in1=gatesB[:, 0, b, :], op0=ALU.mult, op1=ALU.mult)\
                        .then_inc(vec_step, 1)
            n = 8 + B * KD
            for k in range(KD):
                for t in range(FIRS):
                    dve.tensor_scalar(m.diag_fs[:, k, t, :], m.ident[:], fs_w[:, k, t:t + 1], None, ALU.mult)\
                        .then_inc(vec_step, 1)
            n += KD * FIRS
            dve.wait_ge(act_step, 4)
            for h in range(H):
                dve.scalar_tensor_tensor(out=m.rtau[:, h:h + 1], in0=taus[:, 4 + h:5 + h], scalar=0.0,
                                         in1=taus[:, h // 2:h // 2 + 1], op0=ALU.mult, op1=ALU.add)\
                    .then_inc(vec_step, 1)
            n += H
            dve.wait_ge(vec_step, n)
            dve.reciprocal(m.rtau[:], m.rtau[:]).then_inc(vec_step, 1)
            dve.wait_ge(vec_step, n + 1)


def norm_inputs(nc, m, w):
    with ExitStack() as ctx:
        def sb(name, shape):
            return ctx.enter_context(nc.sbuf_tensor(name, shape, F32))

        def sem(name):
            return ctx.enter_context(nc.semaphore(name))

        xin = [sb(f"xin{i}", [P, J, D]) for i in range(2)]
        xn = [sb(f"xn{i}", [P, J, D]) for i in range(2)]
        hT = [sb(f"hT{i}", [P, KD, UT]) for i in range(2)]
        stats = sb("ln_stats", [P, J, 6])
        mv = sb("ln_mv", [P, J, 2])
        rstd = sb("ln_rstd", [P, J])
        modb = sb("ln_modb", [P, 4])
        pad = sb("ln_pad", [P, 1])
        tp = [ctx.enter_context(nc.psum_tensor(f"ln_tp{i}", [P, KD, UT], F32)) for i in range(2)]
        gp = [ctx.enter_context(nc.psum_tensor(f"ln_gp{i}", [P, 512], F32)) for i in range(2)]

        x_in = [sem(f"ln_x_in{i}") for i in range(2)]
        store = [sem(f"ln_store{i}") for i in range(2)]
        ready = sem("ln_ready")
        vec_step = sem("ln_vec_step")
        mod_step = sem("ln_mod_step")
        xn_done = sem("ln_xn_done")
        rstd_done = sem("ln_rstd_done")
        var_done = sem("ln_var_done")
        tp_done = sem("ln_tp_done")
        h_done = sem("ln_h_done")
        g_done = sem("ln_g_done")
        gcopy_done = sem("ln_gcopy_done")
        block = ctx.enter_context(nc.Block("norm_inputs"))
        x_v = w.x.rearrange("b (g j p) d -> b g p j d", j=J, p=P)

        @block.sync
        def _(sp):
            sp.sem_inc(xn_done, 2)
            with sp.Fori(0, B) as b:
                for g in range(UB):
                    sp.wait_ge(xn_done, b * UB + (g + 1))
                    sp.dma_start(xin[g % 2][:], x_v[b, g]).then_inc(x_in[g % 2], 16)

        @block.vector
        def _(dve):
            per = 2 * J + 1
            with dve.Fori(0, B) as b:
                for g in range(UB):
                    i = g % 2
                    dve.wait_ge(x_in[i], b * (16 * UB // 2) + 16 * (g // 2 + 1))
                    for j in range(J):
                        dve.bn_stats(stats[:, j, :], xin[i][:, j, :]).then_inc(vec_step, 1)
                    dve.wait_ge(vec_step, b * (per * UB) + (g * per + J))
                    dve.memset(pad[:], 0.0)
                    for j in range(J):
                        dve.bn_aggr(mv[:, j, :], stats[:, j, :]).then_inc(vec_step, 1)
                    dve.wait_ge(vec_step, b * (per * UB) + (g * per + 2 * J))
                    dve.tensor_scalar(mv[:, :, 1], mv[:, :, 1], LN_EPS, None, ALU.add).then_inc(var_done, 1)
                    dve.wait_ge(rstd_done, b * UB + (g + 1))
                    dve.wait_ge(tp_done, b * UB + (g + 1))
                    for j in range(J):
                        ins = dve.tensor_scalar(xn[i][:, j, :], xin[i][:, j, :], mv[:, j, 0:1], rstd[:, j:j + 1],
                                                ALU.subtract, ALU.mult)
                    ins.then_inc(xn_done, 1)
                    dve.engine_nop().then_inc(vec_step, 1)

        @block.gpsimd
        def _(pool):
            pool.sem_inc(ready, 1)
            pool.sem_inc(h_done, 2)
            pool.sem_inc(tp_done, 2)
            pool.sem_inc(g_done, 2)
            pool.sem_inc(gcopy_done, 2)
            pool.sem_inc(store[0], 16)
            pool.sem_inc(store[1], 16)
            with pool.Fori(0, B) as b:
                for g in range(UB):
                    pool.wait_ge(var_done, b * UB + (g + 1))
                    pool.wait_ge(xn_done, b * UB + (g + 2))
                    pool.tensor_tensor(rstd[:], mv[:, :, 1], m.half_pow[:, 0:J], ALU.pow).then_inc(rstd_done, 1)

        @block.tensor
        def _(pe):
            with pe.Fori(0, B) as b:
                for g in range(UB):
                    i = g % 2
                    pe.wait_ge(xn_done, b * UB + (g + 3))
                    pe.wait_ge(h_done, b * UB + (g + 1))
                    for j in range(J):
                        for k in range(KD):
                            ins = pe.transpose(tp[i][:, k, j * P:(j + 1) * P], xn[i][:, j, k * P:(k + 1) * P],
                                               m.ident[:])
                    ins.then_inc(tp_done, 1)
                    pe.wait_ge(h_done, b * UB + (g + 3))
                    pe.wait_ge(gcopy_done, b * UB + (g + 1))
                    for j in range(J):
                        out = gp[i][:, j * 8:j * 8 + 8]
                        for k in range(KD):
                            pe.matmul(out, hT[i][:, k, j * P:(j + 1) * P], m.wgate[:, k, :],
                                      start=(k == 0), stop=False)
                        ins = pe.matmul(out, m.ones[0:1, :], m.bid_row[0:1, :], start=False, stop=True)
                    ins.then_inc(g_done, 1)

        @block.scalar
        def _(act):
            with act.Fori(0, B) as b:
                act.activation(modb[:].unsqueeze(2), m.mod[:, 0:4, bass.ds(b, 1)], ACT.Copy).then_inc(mod_step, 1)
                act.wait_ge(mod_step, b + 1)
                for g in range(UB):
                    i = g % 2
                    act.wait_ge(tp_done, b * UB + (g + 3))
                    act.wait_ge(store[i], b * (16 * UB // 2) + 16 * (g // 2 + 1))
                    act.wait_ge(g_done, b * UB + (g + 1))
                    for k in range(KD):
                        ins = act.activation(hT[i][:, k, :], tp[i][:, k, :], ACT.Identity,
                                             scale=modb[:, 2 + k:3 + k], bias=modb[:, k:k + 1])
                    ins.then_inc(h_done, 1)
                    act.wait_ge(h_done, b * UB + (g + 3))
                    act.dma_start(m.hT_d[bass.ds(b * UB + g, 1)].squeeze(0), hT[i][:]).then_inc(store[i], 16)
                    act.wait_ge(g_done, b * UB + (g + 3))
                    act.wait_ge(ready, 1)
                    act.activation(m.gates[:, bass.ds(b * (UB * J * 8) + g * J * 8, J * 8)],
                                   gp[i][:, 0:J * 8], ACT.Copy).then_inc(gcopy_done, 1)
            act.wait_ge(gcopy_done, 2 + NU)
            act.activation(m.gates[:], m.gates[:], ACT.Sigmoid).then_inc(gcopy_done, 1)
            for i in range(2):
                act.wait_ge(store[i], 16 + 16 * NU // 2)
            act.wait_ge(gcopy_done, 3 + NU)


def units_ahead(eng, front, body):
    front(0, 0)
    with eng.Fori(0, B - 1) as b:
        for g in range(UB):
            body(b * UB + g, g, b * UB + (g + 1))
    for g in range(UB):
        u = (B - 1) * UB + g
        body(u, g, u + 1 if g < UB - 1 else None)


def conv_heads(nc, m, w):
    NBLK = 3 * KD
    with ExitStack() as ctx:
        def sb(name, shape):
            return ctx.enter_context(nc.sbuf_tensor(name, shape, F32))

        def psum(name):
            return ctx.enter_context(nc.psum_tensor(name, [P, 512], F32))

        def sem(name):
            return ctx.enter_context(nc.semaphore(name))

        two = range(2)
        hT = [sb(f"cv_hT{i}", [P, KD, UT]) for i in two]
        pre = [sb(f"cv_pre{i}", [P, NBLK, CONV - 1 + UT]) for i in two]
        acc = [sb(f"cv_acc{i}", [P, UT]) for i in range(3)]
        vT = [sb(f"cv_vT{i}", [P, KD, FIRS - 1 + UT]) for i in two]
        kqc = [sb(f"cv_kqc{i}", [P, 2 * KD, UT]) for i in two]
        vf = [sb(f"cv_vf{i}", [P, J, 2 * D]) for i in two]
        kq = [sb(f"cv_kq{i}", [P, J, 2 * D]) for i in two]
        kqT = [sb(f"cv_kqT{i}", [P, J, 4 * P]) for i in two]
        sq = [sb(f"cv_sq{i}", [P, 2 * D]) for i in two]
        ss = [sb(f"cv_ss{i}", [P, 2 * H]) for i in two]
        rn = [sb(f"cv_rn{i}", [P, 2 * H]) for i in two]
        pj = [psum(f"cv_pj{i}") for i in two]
        vf_ps = [psum(f"cv_vfps{i}") for i in two]
        kq_ps = [psum(f"cv_kqps{i}") for i in two]
        kqT_ps = [psum(f"cv_kqTps{i}") for i in two]

        h_in = [sem(f"cv_h_in{i}") for i in two]
        store = [sem(f"cv_store{i}") for i in two]
        pj_done = sem("cv_pj_done")
        pre_done = sem("cv_pre_done")
        conv_step = sem("cv_conv_step")
        conv_done = sem("cv_conv_done")
        halo_done = sem("cv_halo_done")
        vhalo_done = sem("cv_vhalo_done")
        silu_done = sem("cv_silu_done")
        vf_done = sem("cv_vf_done")
        vfe_done = sem("cv_vfe_done")
        kq_done = sem("cv_kq_done")
        sq_done = sem("cv_sq_done")
        red_done = sem("cv_red_done")
        eps_done = sem("cv_eps_done")
        rn_done = sem("cv_rn_done")
        mult_done = sem("cv_mult_done")
        kqT_done = sem("cv_kqT_done")
        kqTe_done = sem("cv_kqTe_done")
        block = ctx.enter_context(nc.Block("conv_heads"))

        @block.sync
        def _(sp):
            sp.sem_inc(pj_done, 2 * NBLK)
            sp.sem_inc(vfe_done, 2)
            sp.sem_inc(kqTe_done, 2)
            sp.sem_inc(silu_done, 3)
            for i in two:
                sp.sem_inc(store[i], 48)
            with sp.Fori(0, B) as b:
                for g in range(UB):
                    sp.wait_ge(pj_done, b * (UB * NBLK) + (g + 1) * NBLK)
                    sp.dma_start(hT[g % 2][:], m.hT_d[bass.ds(b * UB + g, 1)].squeeze(0)).then_inc(h_in[g % 2], 16)

        @block.tensor
        def _(pe):
            pe.sem_inc(pre_done, 2)

            def project(u, g, o):
                i = g % 2
                if o == 0:
                    pe.wait_ge(h_in[i], 16 * ((u - i) // 2 + 1) if isinstance(u, int) else (u - i) * 8 + 16)
                pe.wait_ge(pre_done, u * NBLK + (o + 1))
                for k in range(KD):
                    ins = pe.matmul(pj[o % 2][:], m.wqkv[:, k, o * P:(o + 1) * P], hT[i][:, k, :],
                                    start=(k == 0), stop=(k == KD - 1))
                ins.then_inc(pj_done, 1)

            def turn_v(u, g, j):
                i = g % 2
                if j == 0:
                    pe.wait_ge(silu_done, u * NBLK + (KD + 3))
                    pe.wait_ge(vhalo_done, u + 1)
                pe.wait_ge(vfe_done, u * J + (j + 1))
                c0 = j * P
                for k in range(KD):
                    pe.transpose(vf_ps[j % 2][:, k * P:(k + 1) * P],
                                 vT[i][:, k, FIRS - 1 + c0:FIRS - 1 + c0 + P], m.ident[:])
                for k in range(KD):
                    for t in range(FIRS):
                        ins = pe.matmul(vf_ps[j % 2][:, D + k * P:D + (k + 1) * P], vT[i][:, k, c0 + t:c0 + t + P],
                                        m.diag_fs[:, k, t, :], start=(t == 0), stop=(t == FIRS - 1))
                ins.then_inc(vf_done, 1)

            def turn_kq(u, g, j):
                if j == 0:
                    pe.wait_ge(silu_done, u * NBLK + (NBLK + 3))
                pe.wait_ge(mult_done, u * J + (j + 1))
                for a in range(2 * KD):
                    ins = pe.transpose(kq_ps[j % 2][:, a * P:(a + 1) * P], kqc[g % 2][:, a, j * P:(j + 1) * P],
                                       m.ident[:])
                ins.then_inc(kq_done, 1)

            def turn_back(u, g, j):
                pe.wait_ge(mult_done, u * J + (j + 3))
                pe.wait_ge(kqTe_done, u * J + (j + 1))
                for a in range(2 * KD):
                    ins = pe.transpose(kqT_ps[j % 2][:, a * P:(a + 1) * P], kq[g % 2][:, j, a * P:(a + 1) * P],
                                       m.ident[:])
                ins.then_inc(kqT_done, 1)

            def front(u, g):
                for o in range(NBLK):
                    project(u, g, o)

            def body(u, g, nxt):
                for s in range(NBLK):
                    if s < J:
                        turn_kq(u, g, s)
                        turn_v(u, g, s)
                    if 2 <= s < J + 2:
                        turn_back(u, g, s - 2)
                    if nxt is not None:
                        project(nxt, g + 1, s)

            units_ahead(pe, front, body)

        @block.scalar
        def _(act):
            act.activation(pre[0][:, :, 0:CONV - 1], m.zeros[:, 0:NBLK * (CONV - 1)]
                           .rearrange("p (a b) -> p a b", a=NBLK), ACT.Copy).then_inc(halo_done, 1)
            act.activation(vT[0][:, :, 0:FIRS - 1], m.zeros[:, 0:KD * (FIRS - 1)]
                           .rearrange("p (a b) -> p a b", a=KD), ACT.Copy).then_inc(vhalo_done, 1)

            def evacuate(u, g, o):
                i = g % 2
                act.wait_ge(pj_done, u * NBLK + (o + 1 + 2 * NBLK))
                act.activation(pre[i][:, o, CONV - 1:], pj[o % 2][:], ACT.Copy)
                act.wait_ge(silu_done, u * NBLK + (o + 1))
                act.activation(acc[o % 3][:], pj[o % 2][:], ACT.Identity, scale=m.conv_w[:, o, CONV - 1:CONV])\
                    .then_inc(pre_done, 1)

            def halo(u, g):
                if g % UB == UB - 1:
                    src = m.zeros[:, 0:NBLK * (CONV - 1)].rearrange("p (a b) -> p a b", a=NBLK)
                else:
                    act.wait_ge(pre_done, u * NBLK + (NBLK + 2))
                    src = pre[g % 2][:, :, UT:UT + CONV - 1]
                act.activation(pre[(g + 1) % 2][:, :, 0:CONV - 1], src, ACT.Copy).then_inc(halo_done, 1)

            def vhalo(u, g):
                act.wait_ge(vf_done, u * J)  if not isinstance(u, int) or u > 0 else None
                if g % UB == UB - 1:
                    src = m.zeros[:, 0:KD * (FIRS - 1)].rearrange("p (a b) -> p a b", a=KD)
                else:
                    act.wait_ge(silu_done, u * NBLK + (KD + 3))
                    src = vT[g % 2][:, :, UT:UT + FIRS - 1]
                act.activation(vT[(g + 1) % 2][:, :, 0:FIRS - 1], src, ACT.Copy).then_inc(vhalo_done, 1)

            def silu(u, g, o):
                i = g % 2
                act.wait_ge(conv_done, u * NBLK + (o + 1))
                dst = vT[i][:, o, FIRS - 1:] if o < KD else kqc[i][:, o - KD, :]
                act.activation(dst, acc[o % 3][:], ACT.Silu).then_inc(silu_done, 1)

            def front_slot(u, g, s):
                evacuate(u, g, s)
                if s >= 1:
                    silu(u, g, s - 1)
                if s == NBLK - 1:
                    silu(u, g, s)
                    halo(u, g)
                    vhalo(u, g)

            def front(u, g):
                for s in range(NBLK):
                    front_slot(u, g, s)

            def body(u, g, nxt):
                i = g % 2
                if g >= 0:
                    act.wait_ge(store[i], (u - i) * 24 + 48)
                for s in range(NBLK):
                    if s < J:
                        act.wait_ge(kq_done, u * J + (s + 1))
                        act.wait_ge(red_done, u * J + (s + 1))
                        act.activation(sq[s % 2][:], kq_ps[s % 2][:], ACT.Square).then_inc(sq_done, 1)
                        act.wait_ge(vf_done, u * J + (s + 1))
                        act.activation(vf[i][:, s, :], vf_ps[s % 2][:], ACT.Copy).then_inc(vfe_done, 1)
                    if 2 <= s < J + 2:
                        act.wait_ge(kqT_done, u * J + (s - 1))
                        act.activation(kqT[i][:, s - 2, :], kqT_ps[s % 2][:], ACT.Copy).then_inc(kqTe_done, 1)
                    if nxt is not None:
                        front_slot(nxt, g + 1, s)
                rows = bass.ds(u * J, J)
                act.wait_ge(vfe_done, u * J + (J + 2))
                act.dma_start(m.vf_d[rows].rearrange("j p c -> p j c"), vf[i][:]).then_inc(store[i], 16)
                act.wait_ge(mult_done, u * J + (J + 2))
                act.dma_start(m.kq_d[rows].rearrange("j p c -> p j c"), kq[i][:]).then_inc(store[i], 16)
                act.wait_ge(kqTe_done, u * J + (J + 2))
                act.dma_start(m.kqT_d[rows].rearrange("j p c -> p j c"), kqT[i][:]).then_inc(store[i], 16)

            units_ahead(act, front, body)
            for i in two:
                act.wait_ge(store[i], 48 + 48 * NU // 2)

        @block.vector
        def _(dve):
            dve.sem_inc(red_done, 2)
            dve.sem_inc(rn_done, 2)
            dve.sem_inc(mult_done, 2)

            def conv(u, g, o):
                i = g % 2
                dve.wait_ge(pre_done, u * NBLK + (o + 3))
                if o == 0:
                    dve.wait_ge(halo_done, u + 1)
                for t in range(CONV - 1):
                    if t:
                        dve.wait_ge(conv_step, (u * NBLK + o) * 2 + t)
                    ins = dve.scalar_tensor_tensor(out=acc[o % 3][:], in0=pre[i][:, o, t:t + UT],
                                                   scalar=m.conv_w[:, o, t:t + 1], in1=acc[o % 3][:],
                                                   op0=ALU.mult, op1=ALU.add)
                    ins.then_inc(conv_done if t == CONV - 2 else conv_step, 1)

            def reduce_sq(u, j):
                dve.wait_ge(sq_done, u * J + (j + 1))
                dve.wait_ge(rn_done, u * J + (j + 1))
                dve.tensor_reduce(ss[j % 2][:], sq[j % 2][:].rearrange("p (h d) -> p h d", d=DK), AX_X, ALU.add)\
                    .then_inc(red_done, 1)

            def normalise(u, g, j):
                dve.wait_ge(rn_done, u * J + (j + 3))
                if j == 0:
                    dve.wait_ge(store[g % 2], (u - g % 2) * 24 + 48)
                v = lambda a: a.rearrange("p (h d) -> p h d", d=DK)
                dve.tensor_tensor(v(kq[g % 2][:, j, :]), v(kq_ps[j % 2][:]),
                                  rn[j % 2][:].unsqueeze(2).to_broadcast([P, 2 * H, DK]), ALU.mult)\
                    .then_inc(mult_done, 1)

            def front(u, g):
                for o in range(NBLK):
                    conv(u, g, o)

            def body(u, g, nxt):
                for s in range(NBLK):
                    if s < J:
                        reduce_sq(u, s)
                    if nxt is not None:
                        conv(nxt, g + 1, s)
                    if s < J:
                        normalise(u, g, s)

            units_ahead(dve, front, body)

        @block.gpsimd
        def _(pool):
            def body(u):
                for j in range(J):
                    pool.wait_ge(red_done, u * J + (j + 3))
                    pool.tensor_tensor(ss[j % 2][:], ss[j % 2][:], m.l2_eps[:, 0:2 * H], ALU.add)\
                        .then_inc(eps_done, 1)
                    pool.wait_ge(mult_done, u * J + (j + 1))
                    pool.wait_ge(eps_done, u * J + (j + 1))
                    pool.tensor_tensor(rn[j % 2][:], ss[j % 2][:], m.half_pow[:, 0:2 * H], ALU.pow)\
                        .then_inc(rn_done, 1)

            with pool.Fori(0, NU) as u:
                body(u)


def long_filter(nc, m, w):
    CB = 8
    RING = 4
    with ExitStack() as ctx:
        def sb(name, shape):
            return ctx.enter_context(nc.sbuf_tensor(name, shape, F32))

        def sem(name):
            return ctx.enter_context(nc.semaphore(name))

        NF = NT // 2
        v = sb("fl_v", [P, B, 1 + TB, D])
        fl = sb("fl_out", [P, B, TB, D])
        toep = [sb(f"fl_toep{i}", [P, CB, TOEP]) for i in range(RING)]
        v_in = [t[:].rearrange("p a b -> p (a b)")[:, 0:2 * D].rearrange("p (n c) -> p n c", c=D) for t in toep]
        ps = [ctx.enter_context(nc.psum_tensor(f"fl_ps{i}", [P, CB, B, TB], F32)) for i in range(RING)]
        fp = [ctx.enter_context(nc.psum_tensor(f"fl_fp{i}", [P, 2 * D], F32)) for i in range(RING)]
        loaded = [sem(f"fl_loaded{i}") for i in range(RING)]
        flip_done = sem("fl_flip_done")
        fev_done = [sem(f"fl_fev_done{i}") for i in range(2)]
        zero_done = sem("fl_zero_done")
        toep_in = [sem(f"fl_toep_in{i}") for i in range(RING)]
        mm_done = sem("fl_mm_done")
        ev_done = [sem(f"fl_ev_done{i}") for i in range(2)]
        store = sem("fl_store")
        block = ctx.enter_context(nc.Block("long_filter"))

        @block.sync
        def _(sp):
            sp.sem_inc(mm_done, RING)
            sp.sem_inc(flip_done, RING)
            sp.sem_inc(fev_done[0], 2)
            sp.sem_inc(fev_done[1], 2)
            with sp.Fori(0, NF // RING) as it:
                for q in range(RING):
                    sp.wait_ge(flip_done, it * RING + (q + 1))
                    sp.dma_start(v_in[q], m.vf_d[bass.ds(it * (2 * RING) + 2 * q, 2), :, 0:D]
                                 .rearrange("n p c -> p n c")).then_inc(loaded[q], 16)
            sp.wait_ge(flip_done, NF + RING)
            with sp.Fori(0, D // (CB * RING)) as it:
                for q in range(RING):
                    sp.wait_ge(mm_done, it * RING + (q + 1))
                    rows = bass.AP(tensor=m.taps_d.tensor, offset=(it * RING + q) * (CB * TAPROW),
                                   ap=[[1, P], [TAPROW, CB], [1, TOEP]])
                    sp.dma_start(toep[q][:], rows).then_inc(toep_in[q], 16)

        @block.gpsimd
        def _(pool):
            pool.sem_inc(ev_done[0], 2)
            pool.sem_inc(ev_done[1], 2)
            for b in range(B):
                pool.memset(v[:, b, 0, :], 0.0).then_inc(zero_done, 1)
            for half in range(2):
                for i in range(2):
                    pool.wait_ge(ev_done[i], 2 + (half + 1) * D // (CB * 4))
                for b in range(B):
                    c = slice(half * P, (half + 1) * P)
                    pool.dma_start(m.fl_d[b * TB:(b + 1) * TB, :, c].rearrange("n p c -> p n c"), fl[:, b, :, c])\
                        .then_inc(store, 16)
            pool.wait_ge(store, 16 * 2 * B)

        @block.tensor
        def _(pe):
            with pe.Fori(0, NF // RING) as it:
                for q in range(RING):
                    pe.wait_ge(loaded[q], it * 16 + 16)
                    pe.wait_ge(fev_done[q % 2], it * (RING // 2) + (q // 2 + 1))
                    pe.matmul(fp[q][:], m.flip[:], v_in[q].rearrange("p n c -> p (n c)"), start=True, stop=True)\
                        .then_inc(flip_done, 1)
            pe.wait_ge(fev_done[0], 2 + NF // 2)
            pe.wait_ge(fev_done[1], 2 + NF // 2)
            pe.wait_ge(zero_done, B)
            with pe.Fori(0, D // (CB * RING)) as it:
                for q in range(RING):
                    pe.wait_ge(toep_in[q], it * 16 + 16)
                    pe.wait_ge(ev_done[q % 2], it * (RING // 2) + (q // 2 + 1))
                    for c in range(CB):
                        ch = bass.ds(it * (RING * CB) + (q * CB + c), 1)
                        pe.matmul(ps[q][:, c], toep[q][:, c, 0:P], v[:, :, 1:, ch].squeeze(3), start=True, stop=True)
                        ins = pe.matmul(ps[q][0:TOEP - P, c], toep[q][:, c, P:], v[:, :, 0:TB, ch].squeeze(3),
                                        start=False, stop=True, skip_group_check=True)
                    ins.then_inc(mm_done, 1)

        def pair_of(it, q):
            n = it * (2 * RING) + 2 * q
            return v[:].rearrange("p b n c -> p (b n) c")[:, bass.ds(n + it // 2 + 1, 2), :]

        @block.scalar
        def _(act):
            with act.Fori(0, NF // RING) as it:
                for q in range(0, RING, 2):
                    act.wait_ge(flip_done, it * RING + (q + 1 + RING))
                    act.nop()
                    act.activation(pair_of(it, q), fp[q][:].rearrange("p (n c) -> p n c", c=D), ACT.Copy)\
                        .then_inc(fev_done[0], 1)
            with act.Fori(0, D // (CB * RING)) as it:
                for q in range(0, RING, 2):
                    act.wait_ge(mm_done, it * RING + (q + 1 + RING))
                    act.nop()
                    c0 = bass.ds(it * (RING * CB) + q * CB, CB)
                    act.activation(fl.ap().rearrange("p b n c -> p (b n) c")[:, :, c0],
                                   ps[q].ap().rearrange("p c b n -> p (b n) c"), ACT.Copy).then_inc(ev_done[0], 1)

        @block.vector
        def _(dve):
            with dve.Fori(0, NF // RING) as it:
                for q in range(1, RING, 2):
                    dve.wait_ge(flip_done, it * RING + (q + 1 + RING))
                    dve.tensor_scalar(pair_of(it, q), fp[q][:].rearrange("p (n c) -> p n c", c=D), 1.0, None,
                                      ALU.mult).then_inc(fev_done[1], 1)
            with dve.Fori(0, D // (CB * RING)) as it:
                for q in range(1, RING, 2):
                    dve.wait_ge(mm_done, it * RING + (q + 1 + RING))
                    c0 = bass.ds(it * (RING * CB) + q * CB, CB)
                    dve.tensor_scalar(fl.ap().rearrange("p b n c -> p (b n) c")[:, :, c0],
                                      ps[q].ap().rearrange("p c b n -> p (b n) c"), 1.0, None, ALU.mult)\
                        .then_inc(ev_done[1], 1)


def delta_rule(nc, m, w):
    NL = len(m.levels)
    with ExitStack() as ctx:
        def sb(name, shape):
            return ctx.enter_context(nc.sbuf_tensor(name, shape, F32))

        def psum(name):
            return ctx.enter_context(nc.psum_tensor(name, [P, H, P], F32))

        def sem(name):
            return ctx.enter_context(nc.semaphore(name))

        two = range(2)
        kqT = [[sb(f"dr_kqT{p}{i}", [P, 4, P]) for i in two] for p in two]
        kTz = [[sb(f"dr_kTz{p}{i}", [P, H, P]) for i in two] for p in two]
        k = [[sb(f"dr_k{p}{i}", [P, D]) for i in two] for p in two]
        v = [[sb(f"dr_v{p}{i}", [P, D]) for i in two] for p in two]
        DT = [[sb(f"dr_DT{p}{i}", [P, H, P]) for i in two] for p in two]
        att = [[sb(f"dr_att{p}{i}", [P, H, P]) for i in two] for p in two]
        o = [[sb(f"dr_o{p}{i}", [P, D]) for i in two] for p in two]
        A = [sb(f"dr_A{i}", [P, H, P]) for i in two]
        F = [sb(f"dr_F{i}", [P, H, P]) for i in two]
        Dm = [sb(f"dr_D{i}", [P, H, P]) for i in two]
        Ys = [sb(f"dr_Y{i}", [P, H, P]) for i in two]
        R = [sb(f"dr_R{i}", [P, D]) for i in two]
        U = [sb(f"dr_U{i}", [P, D]) for i in two]
        S = [sb(f"dr_S{b}", [P, H // 2, P]) for b in range(B)]
        y_ps = [psum(f"dr_yps{i}") for i in two]
        z_ps = [psum(f"dr_zps{i}") for i in two]
        t_ps = [psum(f"dr_tps{i}") for i in two]
        c_ps = [psum(f"dr_cps{i}") for i in two]

        loaded = [sem(f"dr_loaded{p}") for p in two]
        store = [sem(f"dr_store{p}") for p in two]
        zero_done = sem("dr_zero_done")
        gram_done = sem("dr_gram_done")
        attp_done = sem("dr_attp_done")
        A_done = sem("dr_A_done")
        att_done = sem("dr_att_done")
        F_done = sem("dr_F_done")
        D0_done = sem("dr_D0_done")
        DT0_done = sem("dr_DT0_done")
        y_done = sem("dr_y_done")
        Ys_done = sem("dr_Ys_done")
        z_done = sem("dr_z_done")
        DT_done = sem("dr_DT_done")
        t_done = sem("dr_t_done")
        D_done = sem("dr_D_done")
        kS_done = sem("dr_kS_done")
        R_step = sem("dr_R_step")
        R_done = sem("dr_R_done")
        u_done = sem("dr_u_done")
        U_done = sem("dr_U_done")
        so_done = sem("dr_so_done")
        o_done = sem("dr_o_done")
        S_done = sem("dr_S_done")
        block = ctx.enter_context(nc.Block("delta_rule"))

        def flat(a):
            return a[:].rearrange("p h c -> p (h c)")

        def heads(bank, half):
            return bank[:, 2 * half:2 * half + 2, :].rearrange("p a (e d) -> p (a e) d", e=2)

        @block.sync
        def _(sp):
            sp.sem_inc(so_done, 4)
            sp.sem_inc(o_done, 2)
            sp.sem_inc(S_done, 4)
            for p in two:
                sp.sem_inc(store[p], 32)
            sp.wait_ge(zero_done, B + 4)
            with sp.Fori(0, TB) as t:
                for p in two:
                    sp.wait_ge(so_done, t * 4 + (2 * p + 2))
                    for i in two:
                        n = bass.ds(t + (2 * p + i) * TB, 1)
                        sp.dma_start(flat(kqT[p][i]), m.kqT_d[n].squeeze(0)).then_inc(loaded[p], 16)
                        for e in two:
                            rows = slice(e * DK, (e + 1) * DK)
                            sp.dma_start(kTz[p][i][rows, e::2, :], m.kqT_d[n, rows, 0:2 * P].squeeze(0)
                                         .rearrange("p (a c) -> p a c", a=2)).then_inc(loaded[p], 16)
                        sp.dma_start(k[p][i][:], m.kq_d[n, :, 0:D].squeeze(0)).then_inc(loaded[p], 16)
                        sp.dma_start(v[p][i][:], m.vf_d[n, :, 0:D].squeeze(0)).then_inc(loaded[p], 16)

        @block.tensor
        def _(pe):
            def products(t, p):
                pe.wait_ge(loaded[p], t * 160 + 160)
                u2 = t * 4 + 2 * p
                for i in two:
                    for h in range(H):
                        ins = pe.matmul(y_ps[i][:, h, :], kqT[p][i][:, h // 2, :], kTz[p][i][:, h, :],
                                        start=True, stop=True)
                    ins.then_inc(gram_done, 1)
                for i in two:
                    for h in range(H):
                        ins = pe.matmul(t_ps[i][:, h, :], kTz[p][i][:, h, :], kqT[p][i][:, 2 + h // 2, :],
                                        start=True, stop=True)
                    ins.then_inc(attp_done, 1)

            def first_turn(t, p):
                u2 = t * 4 + 2 * p
                for i in two:
                    pe.wait_ge(D0_done, u2 + (i + 1))
                    pe.wait_ge(att_done, u2 + (i + 1))
                    for h in range(H):
                        ins = pe.transpose(t_ps[i][:, h, :], Dm[i][:, h, :], m.ident[:])
                    ins.then_inc(t_done, 1)

            def level(t, p, l, between):
                n = 2 * NL
                base = t * (2 * n) + (p * n + 2 * l)
                for i in two:
                    if l == 0:
                        pe.wait_ge(DT0_done, t * 4 + (2 * p + i + 1))
                    else:
                        pe.wait_ge(DT_done, base + (i - 1))
                    for h in range(H):
                        ins = pe.matmul(y_ps[i][:, h, :], A[i][:, h, :], DT[p][i][:, h, :], start=True, stop=True)
                    ins.then_inc(y_done, 1)
                between()
                for i in two:
                    pe.wait_ge(Ys_done, base + (i + 1))
                    if l > 0:
                        pe.wait_ge(D_done, t * (4 * (NL - 1)) + (p * 2 * (NL - 1) + 2 * (l - 1) + i + 1))
                    for h in range(H):
                        ins = pe.matmul(z_ps[i][:, h, :], Dm[i][:, h, :], Ys[i][:, h, :], start=True, stop=True)
                    ins.then_inc(z_done, 1)
                if l < NL - 1:
                    for i in two:
                        pe.wait_ge(DT_done, base + (i + 1))
                        for h in range(H):
                            ins = pe.transpose(t_ps[i][:, h, :], DT[p][i][:, h, :], m.ident[:])
                        ins.then_inc(t_done, 1)

            def scan(t, p, step, i):
                b = 2 * p + i
                u2 = t * 4 + (2 * p + i)
                if step == 0:
                    pe.wait_ge(S_done, u2 + 1)
                    pe.wait_ge(o_done, u2 + 1)
                    for a in range(H // 2):
                        ins = pe.matmul(c_ps[i][:, a, :], kqT[p][i][:, a, :], S[b][:, a, :], start=True, stop=True)
                    ins.then_inc(kS_done, 1)
                if step == 1:
                    pe.wait_ge(R_done, u2 + 1)
                    pe.wait_ge(S_done, u2 + 3)
                    pe.wait_ge(DT_done, (t * 4 + 2 * p) * NL + (2 * NL - 1 + i))
                    for h in range(H):
                        ins = pe.matmul(heads(c_ps[i], 1)[:, h, :], DT[p][i][:, h, :], R[i][:, h * DK:(h + 1) * DK],
                                        start=True, stop=True)
                    ins.then_inc(u_done, 1)
                if step == 2:
                    pe.wait_ge(U_done, u2 + 1)
                    for a in range(H // 2):
                        pe.matmul(c_ps[i][:, 2 + a, :], k[p][i][:, a * P:(a + 1) * P], U[i][:, a * P:(a + 1) * P],
                                  start=True, stop=True)
                    for a in range(H // 2):
                        pe.matmul(c_ps[i][:, a, :], kqT[p][i][:, 2 + a, :], S[b][:, a, :], start=True, stop=False,
                                  skip_group_check=True)
                        for h in (2 * a, 2 * a + 1):
                            ins = pe.matmul(heads(c_ps[i], 0)[:, h, :], att[p][i][:, h, :],
                                            U[i][:, h * DK:(h + 1) * DK], start=False, stop=(h % 2 == 1),
                                            skip_group_check=True)
                    ins.then_inc(so_done, 1)

            def stage(nxt, prev):
                if nxt is not None:
                    products(*nxt)
                for i in two:
                    if prev is not None:
                        scan(*prev, 0, i)
                if nxt is not None:
                    first_turn(*nxt)
                for l in range(NL):
                    def between():
                        if prev is not None and 1 <= l <= 4:
                            scan(*prev, 1 + (l - 1) // 2, (l - 1) % 2)
                    if nxt is not None:
                        level(*nxt, l, between)
                    else:
                        between()

            pe.wait_ge(zero_done, B)
            pairs_ahead(pe, stage)

        @block.vector
        def _(dve):
            def beta(t, b, h0, n):
                return m.gates[:, bass.ds(t * 8 + (b * TB * 8 + h0), n)]

            def products(t, p):
                u2 = t * 4 + 2 * p
                for i in two:
                    dve.wait_ge(gram_done, u2 + (i + 1))
                    for h in range(H):
                        ins = dve.scalar_tensor_tensor(out=A[i][:, h, :], in0=y_ps[i][:, h, :],
                                                       scalar=beta(t, 2 * p + i, h, 1), in1=m.lower[:],
                                                       op0=ALU.mult, op1=ALU.mult)
                    ins.then_inc(A_done, 1)
                for i in two:
                    dve.wait_ge(attp_done, u2 + (i + 1))
                    dve.tensor_tensor(att[p][i][:], t_ps[i][:], m.upper[:], ALU.mult).then_inc(att_done, 1)

            def level(t, p, l, between):
                n = 2 * NL
                base = t * (2 * n) + (p * n + 2 * l)
                for i in two:
                    dve.wait_ge(y_done, base + (i + 1))
                    dve.tensor_tensor(Ys[i][:], y_ps[i][:], m.level_mask[l][:], ALU.mult).then_inc(Ys_done, 1)
                between()
                for i in two:
                    dve.wait_ge(z_done, base + (i + 1))
                    dve.tensor_tensor(DT[p][i][:], DT[p][i][:], z_ps[i][:], ALU.subtract).then_inc(DT_done, 1)

            def scan(t, p, step, i):
                b = 2 * p + i
                u2 = t * 4 + (2 * p + i)
                if step == 0:
                    dve.wait_ge(kS_done, u2 + 1)
                    dve.tensor_tensor(R[i][:].rearrange("p (h d) -> p h d", d=DK), v[p][i][:]
                                      .rearrange("p (h d) -> p h d", d=DK), heads(c_ps[i], 0), ALU.subtract)\
                        .then_inc(R_step, 1)
                    dve.wait_ge(R_step, u2 + 1)
                    r = R[i][:].rearrange("p (h d) -> p h d", d=DK)
                    dve.tensor_tensor(r, r, beta(t, b, 0, H).unsqueeze(2).to_broadcast([P, H, DK]), ALU.mult)\
                        .then_inc(R_done, 1)
                if step == 2:
                    dve.wait_ge(so_done, u2 + 5)
                    for e in two:
                        r = slice(e * DK, (e + 1) * DK)
                        ins = dve.tensor_tensor(S[b][r, :, r], S[b][r, :, r], c_ps[i][r, H // 2:, r], ALU.add)
                    ins.then_inc(S_done, 1)

            def stage(nxt, prev):
                if nxt is not None:
                    products(*nxt)
                for i in two:
                    if prev is not None:
                        scan(*prev, 0, i)
                for l in range(NL):
                    def between():
                        if prev is not None and 1 <= l <= 4:
                            scan(*prev, 1 + (l - 1) // 2, (l - 1) % 2)
                    if nxt is not None:
                        level(*nxt, l, between)
                    else:
                        between()

            pairs_ahead(dve, stage)

        @block.gpsimd
        def _(pool):
            for b in range(B):
                pool.memset(S[b][:], 0.0).then_inc(zero_done, 1)
            for p in two:
                for i in two:
                    pool.memset(kTz[p][i][:], 0.0).then_inc(zero_done, 1)
            with pool.Fori(0, NT // 2) as u:
                for i in two:
                    pool.wait_ge(A_done, u * 2 + (i + 1))
                    pool.tensor_tensor(F[i][:], A[i][:], m.first_lower[:], ALU.mult).then_inc(F_done, 1)
                    pool.wait_ge(F_done, u * 2 + (i + 1))
                    pool.tensor_tensor(Dm[i][:], m.ident[:].unsqueeze(1).to_broadcast([P, H, P]), F[i][:],
                                       ALU.subtract).then_inc(D0_done, 1)

        @block.scalar
        def _(act):
            def first_turn(t, p):
                n = 2 * NL
                for i in two:
                    act.wait_ge(t_done, t * (2 * n) + (p * n + i + 1))
                    act.activation(flat(DT[p][i]), flat(t_ps[i]), ACT.Copy).then_inc(DT0_done, 1)

            def level(t, p, l):
                n = 2 * NL
                for i in two:
                    act.wait_ge(t_done, t * (2 * n) + (p * n + 2 * (l + 1) + i + 1))
                    act.activation(flat(Dm[i]), flat(t_ps[i]), ACT.Copy).then_inc(D_done, 1)

            def scan(t, p, step, i):
                b = 2 * p + i
                u2 = t * 4 + (2 * p + i)
                if step == 1:
                    act.wait_ge(u_done, u2 + 1)
                    act.activation(U[i][:].rearrange("p (h d) -> p h d", d=DK), heads(c_ps[i], 1), ACT.Copy)\
                        .then_inc(U_done, 1)
                if step == 2:
                    act.wait_ge(so_done, u2 + 5)
                    act.wait_ge(S_done, u2 + 5)
                    act.wait_ge(store[p], t * 32 + 32)
                    act.activation(o[p][i][:].rearrange("p (h d) -> p h d", d=DK), heads(c_ps[i], 0), ACT.Copy)\
                        .then_inc(o_done, 1)
                    act.wait_ge(o_done, u2 + 3)
                    act.dma_start(m.o_d[bass.ds(t + b * TB, 1)].squeeze(0), o[p][i][:]).then_inc(store[p], 16)

            def stage(nxt, prev):
                if nxt is not None:
                    first_turn(*nxt)
                for l in range(NL):
                    if prev is not None and 1 <= l <= 4:
                        scan(*prev, 1 + (l - 1) // 2, (l - 1) % 2)
                    if nxt is not None and l < NL - 1:
                        level(*nxt, l)

            pairs_ahead(act, stage)
            for p in two:
                act.wait_ge(store[p], 32 + 32 * TB)


def pairs_ahead(eng, stage):
    stage((0, 0), None)
    with eng.Fori(0, TB - 1) as t:
        stage((t, 1), (t, 0))
        stage((t + 1, 0), (t, 1))
    stage((TB - 1, 1), (TB - 1, 0))
    stage(None, (TB - 1, 1))


def mix_and_experts(nc, m, w):
    NX = SI // P + E
    NS = SI // P
    K3 = 3
    NH = J * H
    with ExitStack() as ctx:
        def sb(name, shape):
            return ctx.enter_context(nc.sbuf_tensor(name, shape, F32))

        def sem(name):
            return ctx.enter_context(nc.semaphore(name))

        two = range(2)
        eup = sb("mx_eup", [P, KD, E, EI])
        edn = sb("mx_edn", [P, E, D])
        sup = sb("mx_sup", [P, KD, SI])
        sdn = sb("mx_sdn", [P, NS, D])
        gsel = sb("mx_gsel", [P, J, NG, NG])
        esel = sb("mx_esel", [P, E, E])
        rms_eps = sb("mx_rms_eps", [P, NH])
        vf = [sb(f"mx_vf{i}", [P, J, 2 * D]) for i in two]
        fl = [sb(f"mx_fl{i}", [P, J, D]) for i in two]
        dl = [sb(f"mx_dl{i}", [P, J, D]) for i in two]
        xx = [sb(f"mx_x{i}", [P, J, D]) for i in two]
        hT = [sb(f"mx_hT{i}", [P, KD, UT]) for i in two]
        bs = sb("mx_bs", [P, J * K3 * H, 6])
        tmp = sb("mx_tmp", [P, 3, J * K3 * H])
        st = sb("mx_st", [P, J, K3 * 2 * H])
        stT = sb("mx_stT", [K3 * 2 * H, UT])
        hm = sb("mx_hm", [P, RH // P, UT])
        pr = sb("mx_pr", [P, NH, 3])
        red = sb("mx_red", [P, NH])
        ids = sb("mx_ids", [P, J, H])
        t0 = sb("mx_t0", [P, J, D])
        t1 = sb("mx_t1", [P, J, D])
        t2 = sb("mx_t2", [P, J, D])
        t3 = sb("mx_t3", [P, J, D])
        rms = sb("mx_rms", [P, NH])
        oT = sb("mx_oT", [P, KD, UT])
        x2 = [sb(f"mx_x2{i}", [P, J, D]) for i in two]
        st2 = sb("mx_st2", [P, J, 6])
        mv = sb("mx_mv", [P, J, 2])
        rstd = sb("mx_rstd", [P, J])
        modb = sb("mx_modb", [P, 4])
        h2T = [sb(f"mx_h2T{i}", [P, KD, UT]) for i in two]
        sc = sb("mx_sc", [P, J, E])
        hi = sb("mx_hi", [P, J * NG, 2])
        lo = sb("mx_lo", [P, J * NG, 2])
        gs = sb("mx_gs", [P, 4, J * NG])
        gq = sb("mx_gq", [P, 2, J, NG, NG])
        gm = sb("mx_gm", [P, J * NG])
        ms = sb("mx_ms", [P, J, E])
        rq = hm[:].rearrange("p f (g a b) -> p (f g a b)", a=E, b=E)\
            .rearrange("p (c j a b) -> p c j a b", c=2, j=J, a=E)
        rk = sb("mx_rk", [P, J, E])
        ws = sb("mx_ws", [P, J])
        comb = [sb(f"mx_comb{i}", [P, J, E]) for i in two]
        hs = [sb(f"mx_hs{r}", [P, UT]) for r in range(4)]
        acc = [sb(f"mx_acc{i}", [P, J, D]) for i in two]
        up_ps = [ctx.enter_context(nc.psum_tensor(f"mx_up{i}", [P, UT], F32)) for i in two]
        dn_ps = [ctx.enter_context(nc.psum_tensor(f"mx_dn{i}", [P, J, D], F32)) for i in two]
        M = [ctx.enter_context(nc.psum_tensor(f"mx_m{i}", [P, 512], F32)) for i in two]

        w_in = sem("mx_w_in")
        const_done = sem("mx_const_done")
        loaded = [sem(f"mx_loaded{i}") for i in two]
        stat_done = sem("mx_stat_done")
        var_step = sem("mx_var_step")
        var_done = sem("mx_var_done")
        std_done = sem("mx_std_done")
        stT_done = sem("mx_stT_done")
        stTe_done = sem("mx_stTe_done")
        hmid_done = sem("mx_hmid_done")
        gelu_done = sem("mx_gelu_done")
        logit_done = sem("mx_logit_done")
        lg_done = sem("mx_lg_done")
        soft_step = sem("mx_soft_step")
        shifted_done = sem("mx_shifted_done")
        exp_done = sem("mx_exp_done")
        prob_done = sem("mx_prob_done")
        pool_mix = sem("mx_pool_mix")
        mix_step = sem("mx_mix_step")
        mix_done = sem("mx_mix_done")
        sq_done = sem("mx_sq_done")
        ssum_done = sem("mx_ssum_done")
        rms_step = sem("mx_rms_step")
        rms_done = sem("mx_rms_done")
        on_done = sem("mx_on_done")
        oT_done = sem("mx_oT_done")
        oTe_done = sem("mx_oTe_done")
        wo_done = sem("mx_wo_done")
        x2_done = sem("mx_x2_done")
        ln_step = sem("mx_ln_step")
        ln_var_done = sem("mx_ln_var_done")
        rstd_done = sem("mx_rstd_done")
        xn_done = sem("mx_xn_done")
        hTp_done = sem("mx_hTp_done")
        modb_done = sem("mx_modb_done")
        h2T_done = sem("mx_h2T_done")
        gl_done = sem("mx_gl_done")
        gexp_done = sem("mx_gexp_done")
        route_step = sem("mx_route_step")
        comb_done = sem("mx_comb_done")
        sel_step = sem("mx_sel_step")
        up_done = sem("mx_up_done")
        silu_done = sem("mx_silu_done")
        dn_done = sem("mx_dn_done")
        sh_ev = sem("mx_sh_ev")
        dn_ev = sem("mx_dn_ev")
        fin_step = sem("mx_fin_step")
        fin_done = sem("mx_fin_done")
        store = [sem(f"mx_store{i}") for i in two]
        block = ctx.enter_context(nc.Block("mix_and_experts"))

        x_v = w.x.rearrange("b (g j p) d -> (b g) p j d", j=J, p=P)
        out_v = w.out.rearrange("b (g j p) d -> (b g) p j d", j=J, p=P)

        def by_head(a):
            return a.rearrange("p j (h d) -> p j h d", h=H)

        def spread(a):
            return a.unsqueeze(3).to_broadcast([P, J, H, DK])

        @block.sync
        def _(sp):
            sp.sem_inc(x2_done, 4)
            sp.sem_inc(fin_done, 2)
            sp.sem_inc(store[0], 16)
            sp.sem_inc(store[1], 16)
            sp.sem_inc(gexp_done, 1)
            sp.sem_inc(silu_done, 2)
            sp.sem_inc(dn_done, 4)
            sp.sem_inc(dn_ev, 2)

            def load(u, i):
                rows = bass.ds(u * J, J)
                sp.wait_ge(x2_done, u * 2 + 2)
                sp.dma_start(vf[i][:], m.vf_d[rows].rearrange("j p c -> p j c")).then_inc(loaded[i], 16)
                sp.dma_start(fl[i][:], m.fl_d[rows].rearrange("j p c -> p j c")).then_inc(loaded[i], 16)
                sp.dma_start(dl[i][:], m.o_d[rows].rearrange("j p c -> p j c")).then_inc(loaded[i], 16)
                sp.dma_start(xx[i][:], x_v[bass.ds(u, 1)].squeeze(0)).then_inc(loaded[i], 16)
                sp.dma_start(hT[i][:], m.hT_d[bass.ds(u, 1)].squeeze(0)).then_inc(loaded[i], 16)

            load(0, 0)
            sp.dma_start(sup[:], w.shared_up.rearrange("(k p) n -> p k n", p=P)).then_inc(w_in, 16)
            sp.dma_start(sdn[:], w.shared_down.rearrange("(k p) n -> p k n", p=P)).then_inc(w_in, 16)
            for k in range(KD):
                sp.dma_start(eup[:, k], w.expert_up[:, k * P:(k + 1) * P, :].rearrange("e p i -> p e i"))\
                    .then_inc(w_in, 16)
            sp.dma_start(edn[:], w.expert_down.rearrange("e i h -> i e h")).then_inc(w_in, 16)
            load(1, 1)

            def put(u, i):
                sp.wait_ge(fin_done, u + 3)
                sp.dma_start(out_v[bass.ds(u, 1)].squeeze(0), acc[i][:]).then_inc(store[i], 16)

            with sp.Fori(1, NU // 2) as t:
                for i in two:
                    load(t * 2 + i, i)
                    put(t * 2 + i - 2, i)
            for i in two:
                put(NU - 2 + i, i)
            sp.wait_ge(w_in, 16 * 5)
            for i in two:
                sp.wait_ge(store[i], 16 + 16 * NU // 2)

        @block.gpsimd
        def _(pool):
            n = 0
            pool.memset(gsel[:], 1.0).then_inc(const_done, 1)
            pool.memset(esel[:], 1.0).then_inc(const_done, 1)
            pool.wait_ge(const_done, 2)
            pool.affine_select(out=gsel[:], in_=gsel[:], compare_op=ALU.is_gt, fill=0.0, base=0,
                               pattern=[[0, J], [1, NG], [-1, NG]], channel_multiplier=0).then_inc(const_done, 1)
            pool.affine_select(out=esel[:], in_=esel[:], compare_op=ALU.is_gt, fill=0.0, base=0,
                               pattern=[[1, E], [-1, E]], channel_multiplier=0).then_inc(const_done, 1)

            def mix(u, i):
                pool.wait_ge(var_done, u + 1)
                pool.tensor_tensor(st[:].rearrange("p j (k s h) -> p j k s h", k=K3, s=2)[:, :, :, 1, :]
                                   .rearrange("p j k h -> p (j k) h"),
                                   tmp[:, 2, :].rearrange("p (a h) -> p a h", h=H),
                                   m.root_pow[:, 0:J * K3 * H].rearrange("p (a h) -> p a h", h=H), ALU.pow)\
                    .then_inc(std_done, 1)
                pool.wait_ge(prob_done, u + 1)
                pool.tensor_tensor(by_head(t0[:]), by_head(vf[i][:, :, 0:D]), spread(ids[:]), ALU.mult)\
                    .then_inc(pool_mix, 1)
                p0 = pr[:].rearrange("p (j h) c -> p j h c", h=H)[:, :, :, 0]
                pool.tensor_tensor(by_head(t1[:]), by_head(vf[i][:, :, D:]), spread(p0), ALU.mult)\
                    .then_inc(pool_mix, 1)
                pool.wait_ge(ssum_done, u + 1)
                pool.tensor_tensor(rms[:], rms[:], m.half_pow[:, 0:NH], ALU.pow).then_inc(rms_done, 1)
                pool.wait_ge(ln_var_done, u + 1)
                pool.tensor_tensor(rstd[:], mv[:, :, 1], m.half_pow[:, 0:J], ALU.pow).then_inc(rstd_done, 1)

            def finish(u, i):
                pool.wait_ge(dn_ev, u * E + (E + 2))
                pool.tensor_tensor(acc[i][:], acc[i][:], m.gbB[:, bass.ds(u // UB, 1), :].to_broadcast([P, J, D]),
                                   ALU.mult).then_inc(fin_step, 1)
                pool.wait_ge(fin_step, u + 1)
                pool.tensor_tensor(acc[i][:], acc[i][:], x2[i][:], ALU.add).then_inc(fin_done, 1)

            def front(u, g):
                mix(u, g % 2)

            def body(u, g, nxt):
                if nxt is not None:
                    mix(nxt, (g + 1) % 2)
                finish_b(u, g)

            def finish_b(u, g):
                finish(u, g % 2)

            units_ahead(pool, front, body)

        @block.tensor
        def _(pe):
            def mix(u, i, s):
                if s == 8:
                    pe.wait_ge(std_done, u + 1)
                    pe.wait_ge(gexp_done, u + 1)
                    for j in range(J):
                        ins = pe.transpose(M[0][0:K3 * 2 * H, j * P:(j + 1) * P], st[:, j, :], m.ident[:])
                    ins.then_inc(stT_done, 1)
                if 10 <= s < 14:
                    f = s - 10
                    if f == 0:
                        pe.wait_ge(loaded[i], (u - i) * 40 + 80)
                    pe.wait_ge(stTe_done, u + 1)
                    if f >= 2:
                        pe.wait_ge(gelu_done, u * 4 + (f - 1))
                    out = M[(f + 1) % 2]
                    for k in range(KD):
                        pe.matmul(out[:], m.wr1[:, k, f * P:(f + 1) * P], hT[i][:, k, :], start=(k == 0), stop=False)
                    pe.matmul(out[:], m.wr1s[:, f * P:(f + 1) * P], stT[:], start=False, stop=True)\
                        .then_inc(hmid_done, 1)
                if s == 15:
                    pe.wait_ge(gelu_done, u * 4 + 4)
                    for j in range(J):
                        out = M[1][:, j * 12:j * 12 + 12]
                        for f in range(RH // P):
                            pe.matmul(out, hm[:, f, j * P:(j + 1) * P], m.wr2[:, f, :], start=(f == 0), stop=False)
                        ins = pe.matmul(out, m.ones[0:1, :], m.br2[0:1, :], start=False, stop=True)
                    ins.then_inc(logit_done, 1)
                if s == 28:
                    pe.wait_ge(on_done, u + 1)
                    for k in range(KD):
                        for j in range(J):
                            ins = pe.transpose(M[k][:, j * P:(j + 1) * P], t3[:, j, k * P:(k + 1) * P], m.ident[:])
                        ins.then_inc(oT_done, 1)
                if s == 30:
                    pe.wait_ge(oTe_done, u * 2 + 2)
                    for jj in two:
                        for j in (2 * jj, 2 * jj + 1):
                            for k in range(KD):
                                ins = pe.matmul(M[jj][:, (j % 2) * D:(j % 2 + 1) * D], oT[:, k, j * P:(j + 1) * P],
                                                m.wog[:, bass.ds(u // UB, 1), k, :].squeeze(1),
                                                start=(k == 0), stop=(k == KD - 1))
                        ins.then_inc(wo_done, 1)
                if s == 35:
                    pe.wait_ge(xn_done, u + 1)
                    for k in range(KD):
                        for j in range(J):
                            ins = pe.transpose(M[k][:, j * P:(j + 1) * P], t3[:, j, k * P:(k + 1) * P], m.ident[:])
                        ins.then_inc(hTp_done, 1)
                if s == 38:
                    pe.wait_ge(h2T_done, u + 1)
                    for j in range(J):
                        for k in range(KD):
                            ins = pe.matmul(M[0][:, j * E:(j + 1) * E], h2T[i][:, k, j * P:(j + 1) * P],
                                            m.wgT[:, k, :], start=(k == 0), stop=(k == KD - 1))
                    ins.then_inc(gl_done, 1)

            def up(u, i, x):
                pe.wait_ge(silu_done, u * NX + (x + 1))
                for k in range(KD):
                    lhs = sup[:, k, x * P:(x + 1) * P] if x < NS else eup[:, k, x - NS, :]
                    ins = pe.matmul(up_ps[x % 2][:], lhs, h2T[i][:, k, :], start=(k == 0), stop=(k == KD - 1))
                ins.then_inc(up_done, 1)

            def down(u, i, x):
                n = max(x - NS + 1, 0)
                pe.wait_ge(silu_done, u * NX + (x + 3))
                if n == 2:
                    pe.wait_ge(sh_ev, u + 1)
                elif x == 0 or x >= NS:
                    pe.wait_ge(dn_ev, u * E + (n + 1 if n < 2 else n))
                rhs = sdn[:, x, :] if x < NS else edn[:, x - NS, :]
                for j in range(J):
                    ins = pe.matmul(dn_ps[(i + n) % 2][:, j, :], hs[x % 4][:, j * P:(j + 1) * P], rhs,
                                    start=(x == 0 and j % 2 == 0) or x >= NS, stop=(x >= NS - 1),
                                    skip_group_check=True)
                ins.then_inc(dn_done, 1)

            def front(u, g):
                for s in range(2 * NX):
                    mix(u, g % 2, s)

            def body(u, g, nxt):
                i = g % 2
                up(u, i, 0)
                for x in range(NX):
                    if x < NX - 1:
                        up(u, i, x + 1)
                    if nxt is not None:
                        mix(nxt, 1 - i, 2 * x)
                    down(u, i, x)
                    if nxt is not None:
                        mix(nxt, 1 - i, 2 * x + 1)

            pe.wait_ge(w_in, 16 * 5)
            units_ahead(pe, front, body)

        @block.scalar
        def _(act):
            def mix(u, i, s):
                if s == 9:
                    act.wait_ge(stT_done, u + 1)
                    act.activation(stT[:], M[0][0:K3 * 2 * H, :], ACT.Copy).then_inc(stTe_done, 1)
                if 11 <= s < 15:
                    f = s - 11
                    act.wait_ge(hmid_done, u * 4 + (f + 1))
                    if f == 0 and (not isinstance(u, int) or u > 0):
                        act.wait_ge(comb_done, u)
                    act.activation(hm[:, f, :], M[(f + 1) % 2][:], ACT.Gelu, bias=m.br1[:, f:f + 1])\
                        .then_inc(gelu_done, 1)
                if s == 17:
                    act.wait_ge(shifted_done, u + 1)
                    act.activation(pr[:], pr[:], ACT.Exp).then_inc(exp_done, 1)
                if s == 23:
                    act.wait_ge(mix_done, u + 1)
                    act.activation(t0[:], t2[:], ACT.Square).then_inc(sq_done, 1)
                if s == 29:
                    for k in range(KD):
                        act.wait_ge(oT_done, u * 2 + (k + 1))
                        act.activation(oT[:, k, :], M[k][:], ACT.Copy).then_inc(oTe_done, 1)
                if s == 28:
                    if not isinstance(u, int) or u > 0:
                        act.wait_ge(h2T_done, u)
                    act.activation(modb[:].unsqueeze(2), m.mod[:, 6:10, bass.ds(u // UB, 1)], ACT.Copy)\
                        .then_inc(modb_done, 1)
                if s == 36:
                    act.wait_ge(modb_done, u + 1)
                    for k in range(KD):
                        act.wait_ge(hTp_done, u * 2 + (k + 1))
                        ins = act.activation(h2T[i][:, k, :], M[k][:], ACT.Identity, scale=modb[:, 2 + k:3 + k],
                                             bias=modb[:, k:k + 1])
                    ins.then_inc(h2T_done, 1)
                if s == 39:
                    act.wait_ge(gl_done, u + 1)
                    act.activation(sc[:].rearrange("p j e -> p (j e)"), M[0][:, 0:J * E], ACT.Exp, scale=-1.0)\
                        .then_inc(gexp_done, 1)

            def silu(u, x):
                act.wait_ge(up_done, u * NX + (x + 1))
                act.wait_ge(dn_done, u * NX + (x + 1))
                act.activation(hs[x % 4][:], up_ps[x % 2][:], ACT.Silu).then_inc(silu_done, 1)

            def front(u, g):
                for s in range(2 * NX):
                    mix(u, g % 2, s)

            def body(u, g, nxt):
                i = g % 2
                silu(u, 0)
                for x in range(NX):
                    if x < NX - 1:
                        silu(u, x + 1)
                    if x == NS:
                        act.wait_ge(dn_done, u * NX + (NS + 4))
                        act.wait_ge(store[i], (u - i) * 8 + 16)
                        act.activation(acc[i][:], dn_ps[i][:], ACT.Copy).then_inc(sh_ev, 1)
                    if nxt is not None:
                        mix(nxt, 1 - i, 2 * x)
                        mix(nxt, 1 - i, 2 * x + 1)

            units_ahead(act, front, body)

        @block.vector
        def _(dve):
            def mix(u, i, s):
                if s < 2:
                    if s == 0:
                        dve.wait_ge(loaded[i], (u - i) * 40 + 80)
                    for r in range(s * 24, s * 24 + 24):
                        j, kind, h = r // (K3 * H), r // H % K3, r % H
                        src = (vf[i][:, j, D:], fl[i][:, j, :], dl[i][:, j, :])[kind][:, h * DK:(h + 1) * DK]
                        ins = dve.bn_stats(bs[:, r, :], src)
                    ins.then_inc(stat_done, 1)
                if s == 2:
                    dve.wait_ge(stat_done, u * 2 + 2)
                    dve.tensor_tensor(tmp[:, 0, :], bs[:, :, 1], bs[:, :, 4], ALU.add).then_inc(var_step, 1)
                    dve.tensor_tensor(tmp[:, 1, :], bs[:, :, 1], bs[:, :, 4], ALU.subtract).then_inc(var_step, 1)
                    dve.tensor_tensor(tmp[:, 2, :], bs[:, :, 2], bs[:, :, 5], ALU.add).then_inc(var_step, 1)
                    dve.wait_ge(var_step, u * 4 + 3)
                    mean = st[:].rearrange("p j (k s h) -> p (j k) s h", k=K3, s=2)[:, :, 0, :]
                    dve.tensor_scalar(mean, tmp[:, 0, :].rearrange("p (a h) -> p a h", h=H), 0.5, None, ALU.mult)
                    dve.scalar_tensor_tensor(out=tmp[:, 1, :], in0=tmp[:, 1, :], scalar=0.25, in1=tmp[:, 1, :],
                                             op0=ALU.mult, op1=ALU.mult).then_inc(var_step, 1)
                    dve.wait_ge(var_step, u * 4 + 4)
                    dve.scalar_tensor_tensor(out=tmp[:, 2, :], in0=tmp[:, 2, :], scalar=1.0 / DK, in1=tmp[:, 1, :],
                                             op0=ALU.mult, op1=ALU.add).then_inc(var_done, 1)
                if s == 16:
                    n = u * 5
                    dve.wait_ge(logit_done, u + 1)
                    dve.tensor_tensor(pr[:].rearrange("p (j h) c -> p j h c", h=H),
                                      M[1][:, 0:NH * 3].rearrange("p (j h c) -> p j h c", j=J, h=H),
                                      m.rtau[:].unsqueeze(1).unsqueeze(3).to_broadcast([P, J, H, 3]), ALU.mult)\
                        .then_inc(lg_done, 1)
                    dve.wait_ge(lg_done, u + 1)
                    dve.tensor_reduce(red[:], pr[:], AX_X, ALU.max).then_inc(soft_step, 1)
                    dve.wait_ge(soft_step, n + 1)
                    dve.tensor_tensor(pr[:], pr[:], red[:].unsqueeze(2).to_broadcast([P, NH, 3]), ALU.subtract)\
                        .then_inc(shifted_done, 1)
                    idg = m.gates[:, bass.ds(u * (J * 8), J * 8)].rearrange("p (j c) -> p j c", c=8)[:, :, H:]
                    dve.tensor_tensor(ids[:], idg, m.alpha[:].unsqueeze(1).to_broadcast([P, J, H]), ALU.mult)\
                        .then_inc(soft_step, 1)
                if s == 18:
                    n = u * 5
                    dve.wait_ge(exp_done, u + 1)
                    dve.tensor_reduce(red[:], pr[:], AX_X, ALU.add).then_inc(soft_step, 1)
                    dve.wait_ge(soft_step, n + 3)
                    dve.tensor_scalar(ids[:], ids[:], EPS_ID, None, ALU.add)
                    dve.reciprocal(red[:], red[:]).then_inc(soft_step, 1)
                    dve.wait_ge(soft_step, n + 4)
                    dve.tensor_tensor(pr[:], pr[:], red[:].unsqueeze(2).to_broadcast([P, NH, 3]), ALU.mult)\
                        .then_inc(soft_step, 1)
                    dve.wait_ge(soft_step, n + 5)
                    dve.tensor_scalar(pr[:], pr[:], 1.0 - 3.0 * R_EPS, R_EPS, ALU.mult, ALU.add)\
                        .then_inc(prob_done, 1)
                pc = pr[:].rearrange("p (j h) c -> p j h c", h=H)
                if s == 19:
                    dve.wait_ge(prob_done, u + 1)
                    dve.tensor_tensor(by_head(t2[:]), by_head(fl[i][:]), spread(pc[:, :, :, 1]), ALU.mult)\
                        .then_inc(mix_step, 1)
                    dve.tensor_tensor(by_head(t3[:]), by_head(dl[i][:]), spread(pc[:, :, :, 2]), ALU.mult)\
                        .then_inc(mix_step, 1)
                if s == 20:
                    dve.wait_ge(mix_step, u * 4 + 2)
                    dve.tensor_tensor(t2[:], t2[:], t3[:], ALU.add).then_inc(mix_step, 1)
                if s == 22:
                    dve.wait_ge(mix_step, u * 4 + 3)
                    dve.wait_ge(pool_mix, u * 2 + 2)
                    dve.tensor_tensor(t2[:], t2[:], t0[:], ALU.add).then_inc(mix_step, 1)
                    dve.wait_ge(mix_step, u * 4 + 4)
                    dve.tensor_tensor(t2[:], t2[:], t1[:], ALU.add).then_inc(mix_done, 1)
                if s == 24:
                    dve.wait_ge(sq_done, u + 1)
                    dve.tensor_reduce(rms[:], by_head(t0[:]).rearrange("p j h d -> p (j h) d"), AX_X, ALU.add)\
                        .then_inc(rms_step, 1)
                    dve.wait_ge(rms_step, u + 1)
                    dve.tensor_scalar(rms[:], rms[:], 1.0 / DK, RMS_EPS, ALU.mult, ALU.add).then_inc(ssum_done, 1)
                if s == 26:
                    dve.wait_ge(rms_done, u + 1)
                    dve.tensor_tensor(by_head(t3[:]), by_head(t2[:]),
                                      spread(rms[:].rearrange("p (j h) -> p j h", h=H)), ALU.mult)\
                        .then_inc(on_done, 1)
                if s == 30:
                    for jj in two:
                        dve.wait_ge(wo_done, u * 2 + (jj + 1))
                        if jj == 0:
                            dve.wait_ge(fin_done, u + 1)
                        dve.tensor_tensor(x2[i][:, 2 * jj:2 * jj + 2, :], xx[i][:, 2 * jj:2 * jj + 2, :],
                                          M[jj][:].rearrange("p (j d) -> p j d", d=D), ALU.add)\
                            .then_inc(x2_done, 1)
                if s == 31:
                    dve.wait_ge(x2_done, u * 2 + 6)
                    for j in range(J):
                        dve.bn_stats(st2[:, j, :], x2[i][:, j, :]).then_inc(ln_step, 1)
                    dve.wait_ge(ln_step, u * (2 * J) + J)
                    dve.memset(ws[:], 0.0)
                    for j in range(J):
                        dve.bn_aggr(mv[:, j, :], st2[:, j, :]).then_inc(ln_step, 1)
                    dve.wait_ge(ln_step, u * (2 * J) + 2 * J)
                    dve.tensor_scalar(mv[:, :, 1], mv[:, :, 1], LN_EPS, None, ALU.add).then_inc(ln_var_done, 1)
                if s == 33:
                    dve.wait_ge(rstd_done, u + 1)
                    for j in range(J):
                        ins = dve.tensor_scalar(t3[:, j, :], x2[i][:, j, :], mv[:, j, 0:1], rstd[:, j:j + 1],
                                                ALU.subtract, ALU.mult)
                    ins.then_inc(xn_done, 1)

            def route(u, i, s):
                n = u * 17
                flat = sc[:].rearrange("p j e -> p (j e)")
                quad = sc[:].rearrange("p j (g a b) -> p (j g) a b", g=NG, b=2)
                if s == 0:
                    dve.wait_ge(gexp_done, u + 2)
                    dve.tensor_scalar(flat, flat, 1.0, None, ALU.add).then_inc(route_step, 1)
                    dve.wait_ge(route_step, n + 1)
                    dve.reciprocal(flat, flat).then_inc(route_step, 1)
                    dve.wait_ge(route_step, n + 2)
                    dve.tensor_tensor(hi[:], quad[:, :, :, 0], quad[:, :, :, 1], ALU.max).then_inc(route_step, 1)
                    dve.tensor_tensor(lo[:], quad[:, :, :, 0], quad[:, :, :, 1], ALU.min).then_inc(route_step, 1)
                    dve.wait_ge(route_step, n + 4)
                    dve.tensor_tensor(gs[:, 0, :], hi[:, :, 0], hi[:, :, 1], ALU.max)
                    dve.tensor_tensor(gs[:, 1, :], hi[:, :, 0], hi[:, :, 1], ALU.min)
                    dve.tensor_tensor(gs[:, 2, :], lo[:, :, 0], lo[:, :, 1], ALU.max).then_inc(route_step, 1)
                    dve.wait_ge(route_step, n + 5)
                    dve.tensor_tensor(gs[:, 1, :], gs[:, 1, :], gs[:, 2, :], ALU.max).then_inc(route_step, 1)
                    dve.wait_ge(route_step, n + 6)
                    dve.tensor_tensor(gs[:, 3, :], gs[:, 0, :], gs[:, 1, :], ALU.add).then_inc(route_step, 1)
                if s == 1:
                    dve.wait_ge(route_step, n + 7)
                    g = gs[:, 3, :].rearrange("p (j g) -> p j g", g=NG)
                    other = g.unsqueeze(2).to_broadcast([P, J, NG, NG])
                    own = g.unsqueeze(3).to_broadcast([P, J, NG, NG])
                    dve.tensor_tensor(gq[:, 0], other, own, ALU.is_gt)
                    dve.tensor_tensor(gq[:, 1], other, own, ALU.is_equal).then_inc(route_step, 1)
                    dve.wait_ge(route_step, n + 8)
                    dve.tensor_tensor(gq[:, 1], gq[:, 1], gsel[:], ALU.mult).then_inc(route_step, 1)
                    dve.wait_ge(route_step, n + 9)
                    dve.tensor_tensor(gq[:, 0], gq[:, 0], gq[:, 1], ALU.add).then_inc(route_step, 1)
                    dve.wait_ge(route_step, n + 10)
                    dve.tensor_reduce(gm[:], gq[:, 0].rearrange("p j g h -> p (j g) h"), AX_X, ALU.add)\
                        .then_inc(route_step, 1)
                    dve.wait_ge(route_step, n + 11)
                    dve.tensor_scalar(gm[:], gm[:], 2.0, None, ALU.is_lt).then_inc(route_step, 1)
                    dve.wait_ge(route_step, n + 12)
                    dve.tensor_tensor(ms[:].rearrange("p j (g a) -> p (j g) a", g=NG),
                                      sc[:].rearrange("p j (g a) -> p (j g) a", g=NG),
                                      gm[:].unsqueeze(2).to_broadcast([P, J * NG, E // NG]), ALU.mult)\
                        .then_inc(route_step, 1)
                if s == 2:
                    dve.wait_ge(route_step, n + 13)
                    other = ms[:].unsqueeze(2).to_broadcast([P, J, E, E])
                    own = ms[:].unsqueeze(3).to_broadcast([P, J, E, E])
                    dve.tensor_tensor(rq[:, 0], other, own, ALU.is_gt)
                    dve.tensor_tensor(rq[:, 1], other, own, ALU.is_equal).then_inc(route_step, 1)
                    dve.wait_ge(route_step, n + 14)
                    dve.tensor_tensor(rq[:, 1], rq[:, 1], esel[:].unsqueeze(1).to_broadcast([P, J, E, E]), ALU.mult)\
                        .then_inc(route_step, 1)
                if s == 3:
                    dve.wait_ge(route_step, n + 15)
                    dve.tensor_tensor(rq[:, 0], rq[:, 0], rq[:, 1], ALU.add).then_inc(route_step, 1)
                    dve.wait_ge(route_step, n + 16)
                    dve.tensor_reduce(rk[:].rearrange("p j e -> p (j e)"), rq[:, 0].rearrange("p j a b -> p (j a) b"),
                                      AX_X, ALU.add).then_inc(route_step, 1)
                    dve.wait_ge(route_step, n + 17)
                    dve.scalar_tensor_tensor(out=ms[:].rearrange("p j e -> p (j e)"),
                                             in0=rk[:].rearrange("p j e -> p (j e)"), scalar=float(TOPK), in1=flat,
                                             op0=ALU.is_lt, op1=ALU.mult).then_inc(sel_step, 1)
                    dve.wait_ge(sel_step, u * 4 + 1)
                    dve.tensor_reduce(ws[:], ms[:], AX_X, ALU.add).then_inc(sel_step, 1)
                    dve.wait_ge(sel_step, u * 4 + 2)
                    dve.tensor_scalar(ws[:], ws[:], 1e-20, None, ALU.add).then_inc(sel_step, 1)
                    dve.wait_ge(sel_step, u * 4 + 3)
                    dve.reciprocal(ws[:], ws[:]).then_inc(sel_step, 1)
                    dve.wait_ge(sel_step, u * 4 + 4)
                    for j in range(J):
                        ins = dve.tensor_scalar(comb[i][:, j, :], ms[:, j, :], ws[:, j:j + 1], SCALING, ALU.mult,
                                                ALU.mult)
                    ins.then_inc(comb_done, 1)

            def expert(u, i, e):
                n = e + 1
                if e == 0:
                    dve.wait_ge(comb_done, u + 1)
                dve.wait_ge(dn_done, u * NX + (NS + e + 5))
                if e == 0:
                    dve.wait_ge(sh_ev, u + 1)
                else:
                    dve.wait_ge(dn_ev, u * E + (e + 2))
                for j in range(J):
                    ins = dve.scalar_tensor_tensor(out=acc[i][:, j, :], in0=dn_ps[(i + n) % 2][:, j, :],
                                                   scalar=comb[i][:, j, e:e + 1], in1=acc[i][:, j, :],
                                                   op0=ALU.mult, op1=ALU.add)
                ins.then_inc(dn_ev, 1)

            def front(u, g):
                for s in range(2 * NX):
                    mix(u, g % 2, s)

            def body(u, g, nxt):
                i = g % 2
                for x in range(NX):
                    if x >= NS:
                        expert(u, i, x - NS)
                    else:
                        route(u, i, x)
                    if nxt is not None:
                        mix(nxt, 1 - i, 2 * x)
                        mix(nxt, 1 - i, 2 * x + 1)

            dve.wait_ge(const_done, 4)
            units_ahead(dve, front, body)


def build(nc, x, Wq, Wk, Wv, Wb, conv_q, conv_k, conv_v, fir_short, fir_long, alpha_id, Wid, bid, Wr1, br1,
          Wr2, br2, log_tau_group, log_tau_head, o_norm_w, Wo, gate_weight, expert_up, expert_down, shared_up,
          shared_down, c, wmod, out, phases=None, debug_inputs=()):
    w = Bag()
    w.x, w.Wq, w.Wk, w.Wv = x, Wq, Wk, Wv
    w.Wb, w.conv_q, w.conv_k, w.conv_v = Wb, conv_q, conv_k, conv_v
    w.fir_short, w.fir_long, w.alpha_id, w.Wid = fir_short, fir_long, alpha_id, Wid
    w.bid, w.Wr1, w.br1, w.Wr2 = bid, Wr1, br1, Wr2
    w.br2, w.log_tau_group, w.log_tau_head, w.o_norm_w = br2, log_tau_group, log_tau_head, o_norm_w
    w.Wo, w.gate_weight, w.expert_up, w.expert_down = Wo, gate_weight, expert_up, expert_down
    w.shared_up, w.shared_down, w.c, w.wmod = shared_up, shared_down, c, wmod
    w.out = out
    m = Bag()

    def dram(name, shape):
        kind = {"kind": "ExternalInput"} if name in debug_inputs else {}
        return nc.dram_tensor(name, shape, F32, **kind).ap()

    m.hT_d = dram("hT_d", (NU, P, KD, UT))
    m.vf_d = dram("vf_d", (NT, P, 2 * D))
    m.kq_d = dram("kq_d", (NT, P, 2 * D))
    m.kqT_d = dram("kqT_d", (NT, P, 4 * P))
    m.fl_d = dram("fl_d", (NT, P, D))
    m.o_d = dram("o_d", (NT, P, D))
    m.taps_d = dram("taps_d", (D, TAPROW))
    with ExitStack() as ctx:
        def sb(name, shape):
            return ctx.enter_context(nc.sbuf_tensor(name, shape, F32))
        m.levels = [2, 4, 8, 16, 32, 64]
        m.ident = sb("ident", [P, P])
        m.flip = sb("flip", [P, P])
        m.ones = sb("ones", [P, P])
        m.lower = sb("lower", [P, P])
        m.upper = sb("upper", [P, H, P])
        m.first_lower = sb("first_lower", [P, H, P])
        m.level_mask = [sb(f"level_mask{s}", [P, H, P]) for s in m.levels]
        m.zeros = sb("zeros_small", [P, 32])
        m.half_pow = sb("half_pow", [P, 64])
        m.root_pow = sb("root_pow", [P, 64])
        m.l2_eps = sb("l2_eps", [P, 16])
        m.conv_w = sb("conv_w", [P, 6, CONV])
        m.alpha = sb("alpha", [P, H])
        m.rtau = sb("rtau", [P, H])
        m.mod = sb("mod", [P, 12, B])
        m.gbB = sb("gbB", [P, B, D])
        m.wog = sb("wog", [P, B, KD, D])
        m.diag_fs = sb("diag_fs", [P, KD, FIRS, P])
        m.wqkv = sb("wqkv", [P, KD, 3 * D])
        m.wgate = sb("wgate", [P, KD, 8])
        m.bid_row = sb("bid_row", [1, 8])
        m.wr1 = sb("wr1", [P, KD, RH])
        m.wr1s = sb("wr1s", [6 * H, RH])
        m.br1 = sb("br1", [P, RH // P])
        m.wr2 = sb("wr2", [P, RH // P, 3 * H])
        m.br2 = sb("br2", [1, 3 * H])
        m.wgT = sb("wgT", [P, KD, E])
        m.gates = sb("gates", [P, NT * 8])
        for name, stage in STAGES:
            if phases is None or name in phases:
                stage(nc, m, w)


STAGES = [("setup", setup), ("norm", norm_inputs), ("conv", conv_heads), ("long", long_filter), ("delta", delta_rule), ("mix", mix_and_experts)]

_INS = ['x', 'Wq', 'Wk', 'Wv', 'Wb', 'conv_q', 'conv_k', 'conv_v', 'fir_short', 'fir_long', 'alpha_id', 'Wid', 'bid',
        'Wr1', 'br1', 'Wr2', 'br2', 'log_tau_group', 'log_tau_head', 'o_norm_w', 'Wo', 'gate_weight', 'expert_up',
        'expert_down', 'shared_up', 'shared_down', 'c', 'wmod']
_INS = [("L0_attn_hidden_states" if n == 'x' else f"L0_{n}" if n in ('c', 'wmod') else
         f"L0_ffn_{n}" if n in ('gate_weight', 'expert_up', 'expert_down', 'shared_up', 'shared_down') else
         f"L0_attn_{n}") for n in _INS]
_OUTS = [((B, L, D), 'float32')]


def kernel(**inputs):
    import numpy as _np
    import concourse.bacc as _bacc
    from concourse import mybir as _mybir
    from concourse.bass_utils import run_bass_kernel_spmd as _run

    nc = _bacc.Bacc("TRN2", target_bir_lowering=False, num_devices=1)
    arrays, args = {}, []
    for name in _INS:
        a = _np.ascontiguousarray(inputs[name])
        arrays[f"in_{name}_dram"] = a
        args.append(nc.dram_tensor(f"in_{name}_dram", a.shape, _mybir.dt.from_np(a.dtype), kind="ExternalInput").ap())
    for i, (shape, dtype) in enumerate(_OUTS):
        dt = _mybir.dt.from_np(_np.dtype(dtype))
        args.append(nc.dram_tensor(f"out_{i}_dram", shape, dt, kind="ExternalOutput").ap())
    build(nc, *args)
    r = _run(nc, [arrays], core_ids=[0])
    got = tuple(r.results[0][f"out_{i}_dram"] for i in range(len(_OUTS)))
    return got[0]
```

```python
from contextlib import ExitStack

import concourse.bass as bass
from concourse import mybir

ALU = mybir.AluOpType
ACT = mybir.ActivationFunctionType
F32 = mybir.dt.float32
AX_X = mybir.AxisListType.X

P = 128
B, L, D, H = 4, 2048, 256, 4
DK = D // H
KD = D // P
UT = 512
J = UT // P
UB = L // UT
NU = B * UB
TB = L // P
NT = B * TB
CONV, FIRS, FIRL = 4, 3, 31
E, EI, SI = 16, 128, 512
NG, TOPK, SCALING = 4, 4, 2.5
RH = 2 * D
LN_EPS, L2_EPS, RMS_EPS = 1e-5, 1e-6, 1e-5
EPS_ID, R_EPS = 0.06, 0.025
TOEP = P + 32
TAPROW = P + TOEP


class Bag:
    pass


def setup(nc, m, w):
    with ExitStack() as ctx:
        def sb(name, shape):
            return ctx.enter_context(nc.sbuf_tensor(name, shape, F32))

        def sem(name):
            return ctx.enter_context(nc.semaphore(name))

        cT = sb("cT", [P, KD, B])
        scT = sb("scT", [P, KD, B])
        scB = sb("scB", [P, KD, B, P])
        zeros = sb("zeros", [P, P])
        wmod = sb("wmod", [P, KD, 6 * D])
        gatesB = sb("gatesB", [P, 2, B, D])
        gsign = sb("gsign", [P, 2, B, D])
        taus = sb("taus", [P, 8])
        fs_w = sb("fs_w", [P, KD, FIRS])
        fl_w = sb("fl_w", [P, KD, FIRL])
        onw = sb("onw", [P, 1])
        wo = sb("wo", [P, KD, D])
        taps = sb("taps", [P, KD, TAPROW])
        ps = ctx.enter_context(nc.psum_tensor("ps_setup", [P, 8, 512], F32))
        modt_ps = ps[:, 0, 0:48].rearrange("p (a b) -> p a b", b=B)

        c_in = sem("c_in")
        w_in = sem("w_in")
        small_in = sem("small_in")
        rest_in = sem("rest_in")
        taps_out = sem("taps_out")
        taps_placed = sem("taps_placed")
        zero_done = sem("zero_done")
        pool_step = sem("pool_step")
        silu_done = sem("silu_done")
        bcast_done = sem("bcast_done")
        mm_done = sem("mm_done")
        act_step = sem("act_step")
        vec_step = sem("vec_step")

        ctx.enter_context(nc.allow_non_contiguous_dma(reason="small vectors and weights, loaded once"))
        block = ctx.enter_context(nc.Block("setup"))

        @block.sync
        def _(sp):
            for b in range(B):
                for k in range(KD):
                    sp.dma_start(cT[:, k, b:b + 1], w.c[b, k * P:(k + 1) * P].unsqueeze(1)).then_inc(c_in, 16)
            sp.dma_start(wmod[:], w.wmod.rearrange("(k p) n -> p k n", p=P)).then_inc(w_in, 16)
            col = lambda a, k: a[k * P:(k + 1) * P, :]
            for k in range(KD):
                for i, a in enumerate((w.conv_v, w.conv_k, w.conv_q)):
                    sp.dma_start(m.conv_w[:, 2 * i + k, :], col(a, k)).then_inc(small_in, 16)
                sp.dma_start(fs_w[:, k, :], w.fir_short.rearrange("h d t -> (h d) t")[k * P:(k + 1) * P, :])\
                    .then_inc(small_in, 16)
            for i in range(2):
                sp.dma_start(onw[i * DK:(i + 1) * DK, :], w.o_norm_w.unsqueeze(1)).then_inc(small_in, 16)
            sp.dma_start(taus[:, 0:2], w.log_tau_group.partition_broadcast(P)).then_inc(small_in, 16)
            sp.dma_start(taus[:, 4:8], w.log_tau_head.partition_broadcast(P)).then_inc(small_in, 16)
            sp.dma_start(m.alpha[:], w.alpha_id.partition_broadcast(P)).then_inc(small_in, 16)
            sp.dma_start(wo[:], w.Wo.rearrange("(k p) n -> p k n", p=P)).then_inc(small_in, 16)
            for i, a in enumerate((w.Wv, w.Wk, w.Wq)):
                sp.dma_start(m.wqkv[:, :, i * D:(i + 1) * D], a.rearrange("(k p) n -> p k n", p=P))\
                    .then_inc(rest_in, 16)
            sp.dma_start(m.wgate[:, :, 0:H], w.Wb.rearrange("(k p) n -> p k n", p=P)).then_inc(rest_in, 16)
            sp.dma_start(m.wgate[:, :, H:2 * H], w.Wid.rearrange("(k p) n -> p k n", p=P)).then_inc(rest_in, 16)
            sp.dma_start(m.bid_row[0:1, H:2 * H], w.bid.unsqueeze(0)).then_inc(rest_in, 16)
            sp.dma_start(m.wr1[:], w.Wr1[0:D, :].rearrange("(k p) n -> p k n", p=P)).then_inc(rest_in, 16)
            sp.dma_start(m.wr1s[0:6 * H, :], w.Wr1[D:D + 6 * H, :]).then_inc(rest_in, 16)
            for i in range(RH // P):
                sp.dma_start(m.br1[:, i:i + 1], w.br1[i * P:(i + 1) * P].unsqueeze(1)).then_inc(rest_in, 16)
            sp.dma_start(m.wr2[:], w.Wr2.rearrange("(k p) n -> p k n", p=P)).then_inc(rest_in, 16)
            sp.dma_start(m.br2[0:1, :], w.br2.unsqueeze(0)).then_inc(rest_in, 16)
            for k in range(KD):
                sp.dma_start(m.wgT[:, k, :], w.gate_weight[:, k * P:(k + 1) * P].rearrange("e p -> p e"))\
                    .then_inc(rest_in, 16)
            n_rest = 16 * (3 + 3 + 2 + RH // P + 2 + KD)
            sp.wait_ge(zero_done, 1)
            for k in range(KD):
                sp.dma_start(fl_w[:, k, :], w.fir_long.rearrange("h d t -> (h d) t")[k * P:(k + 1) * P, :])\
                    .then_inc(taps_out, 16)
            sp.wait_ge(taps_placed, FIRL)
            sp.dma_start(m.taps_d.rearrange("(k p) n -> p k n", p=P), taps[:]).then_inc(taps_out, 16)
            sp.wait_ge(taps_out, 16 * KD + 16)
            sp.wait_ge(rest_in, n_rest)

        @block.gpsimd
        def _(pool):
            pool.memset(taps[:], 0.0).then_inc(pool_step, 1)
            pool.memset(zeros[:], 0.0).then_inc(pool_step, 1)
            pool.memset(m.ones[:], 1.0).then_inc(pool_step, 1)
            pool.memset(m.ident[:], 0.0).then_inc(pool_step, 1)
            pool.memset(m.flip[:], 0.0).then_inc(pool_step, 1)
            pool.memset(m.lower[:], 1.0).then_inc(pool_step, 1)
            pool.memset(m.upper[:], 1.0).then_inc(pool_step, 1)
            pool.memset(m.first_lower[:], 0.0).then_inc(pool_step, 1)
            for s in range(len(m.levels)):
                pool.memset(m.level_mask[s][:], 1.0).then_inc(pool_step, 1)
            pool.memset(m.zeros[:], 0.0).then_inc(pool_step, 1)
            pool.memset(m.half_pow[:], -0.5).then_inc(pool_step, 1)
            pool.memset(m.root_pow[:], 0.5).then_inc(pool_step, 1)
            pool.memset(m.l2_eps[:], L2_EPS).then_inc(pool_step, 1)
            pool.memset(m.bid_row[:, 0:H], 0.0).then_inc(pool_step, 1)
            n = 8 + len(m.levels) + 5
            pool.wait_ge(pool_step, n)
            pool.sem_inc(zero_done, 1)
            pool.affine_select(out=m.flip[:], in_=m.flip[:], compare_op=ALU.not_equal, fill=1.0, base=1 - P,
                               pattern=[[1, P]], channel_multiplier=1).then_inc(pool_step, 1)
            pool.affine_select(out=m.ident[:], in_=m.ident[:], compare_op=ALU.not_equal, fill=1.0, base=0,
                               pattern=[[-1, P]], channel_multiplier=1).then_inc(pool_step, 1)
            pool.affine_select(out=m.lower[:], in_=m.lower[:], compare_op=ALU.is_gt, fill=0.0, base=0,
                               pattern=[[-1, P]], channel_multiplier=1).then_inc(pool_step, 1)
            pool.affine_select(out=m.upper[:], in_=m.upper[:], compare_op=ALU.is_ge, fill=0.0, base=0,
                               pattern=[[0, H], [1, P]], channel_multiplier=-1).then_inc(pool_step, 1)
            v = m.first_lower.ap().rearrange("p h (n two) -> p h n two", two=2)[:, :, :, 0]
            pool.affine_select(out=v, in_=v, compare_op=ALU.not_equal, fill=1.0, base=-1,
                               pattern=[[0, H], [-2, P // 2]], channel_multiplier=1).then_inc(pool_step, 1)
            n += 5
            for i, s in enumerate(m.levels):
                v = m.level_mask[i].ap().rearrange("p h (n s) -> p h n s", s=s)
                nb = P // (2 * s)
                for h in range(H):
                    vh = v[:, h]
                    pool.wait_ge(pool_step, n)
                    pool.affine_select(out=vh, in_=vh, compare_op=ALU.is_ge, fill=0.0, base=-s,
                                       pattern=[[-2 * s, nb], [0, s]], channel_multiplier=1).then_inc(pool_step, 1)
                    n += 1
                    pool.wait_ge(pool_step, n)
                    pool.affine_select(out=vh, in_=vh, compare_op=ALU.is_ge, fill=0.0, base=2 * s - 1,
                                       pattern=[[2 * s, nb], [0, s]], channel_multiplier=-1).then_inc(pool_step, 1)
                    n += 1

            pool.wait_ge(pool_step, n)
            pool.sem_inc(zero_done, 1)

        @block.scalar
        def _(act):
            act.wait_ge(c_in, 16 * KD * B)
            act.activation(scT[:], cT[:], ACT.Silu).then_inc(silu_done, 1)
            act.wait_ge(mm_done, 1)
            act.activation(m.mod[:], modt_ps, ACT.Copy).then_inc(act_step, 1)
            act.wait_ge(mm_done, 2)
            act.activation(gatesB.ap().rearrange("p g b d -> p (g b d)"), ps[:, 1:5, :].rearrange("p a b -> p (a b)"), ACT.Copy).then_inc(act_step, 1)
            act.wait_ge(small_in, 16 * (4 * KD + 6))
            act.activation(taus[:, 0:2], taus[:, 0:2], ACT.Exp).then_inc(act_step, 1)
            act.activation(taus[:, 4:8], taus[:, 4:8], ACT.Exp).then_inc(act_step, 1)
            act.activation(m.alpha[:], m.alpha[:], ACT.Sigmoid).then_inc(act_step, 1)

        @block.tensor
        def _(pe):
            pe.wait_ge(w_in, 16)
            pe.wait_ge(silu_done, 1)
            for a in range(12):
                for k in range(KD):
                    mm = pe.matmul(modt_ps[:, a, :], wmod[:, k, a * P:(a + 1) * P], scT[:, k, :],
                                   start=(k == 0), stop=(k == KD - 1))
            mm.then_inc(mm_done, 1)
            pe.wait_ge(bcast_done, 1)
            for g in range(2):
                for b in range(B):
                    o = (g * B + b) * D
                    out = ps[:, 1 + o // 512, o % 512:o % 512 + D]
                    for k in range(KD):
                        mm = pe.matmul(out, scB[:, k, b, :], wmod[:, k, (2 + 3 * g) * D:(3 + 3 * g) * D],
                                       start=(k == 0), stop=(k == KD - 1))
            mm.then_inc(mm_done, 1)

        @block.vector
        def _(dve):
            dve.wait_ge(zero_done, 1)
            dve.wait_ge(taps_out, 16 * KD)
            for t in range(FIRL):
                c = P - 1 + FIRL - 1 - t
                dve.tensor_copy(taps[:, :, c:c + 1], fl_w[:, :, t:t + 1]).then_inc(taps_placed, 1)
            dve.wait_ge(silu_done, 1)
            dve.wait_ge(zero_done, 2)
            for k in range(KD):
                for b in range(B):
                    ins = dve.tensor_scalar(scB[:, k, b, :], zeros[:], scT[:, k, b:b + 1], None, ALU.add)
            ins.then_inc(bcast_done, 1)
            dve.wait_ge(act_step, 1)
            dve.tensor_scalar(m.mod[:, 2:4, :], m.mod[:, 2:4, :], 1.0, None, ALU.add).then_inc(vec_step, 1)
            dve.tensor_scalar(m.mod[:, 8:10, :], m.mod[:, 8:10, :], 1.0, None, ALU.add).then_inc(vec_step, 1)
            dve.wait_ge(act_step, 2)
            dve.tensor_scalar(gsign[:], gatesB[:], 0.0, 2.0, ALU.is_ge, ALU.mult).then_inc(vec_step, 1)
            dve.scalar_tensor_tensor(out=gatesB[:], in0=gatesB[:], scalar=-1.0, in1=gatesB[:], op0=ALU.mult,
                                     op1=ALU.max).then_inc(vec_step, 1)
            dve.wait_ge(vec_step, 4)
            dve.tensor_scalar(gatesB[:], gatesB[:], 0.25, None, ALU.max).then_inc(vec_step, 1)
            dve.tensor_scalar(gsign[:], gsign[:], -1.0, None, ALU.add).then_inc(vec_step, 1)
            dve.wait_ge(vec_step, 6)
            dve.tensor_tensor(gatesB[:], gatesB[:], gsign[:], ALU.mult).then_inc(vec_step, 1)
            dve.wait_ge(vec_step, 7)
            dve.tensor_copy(m.gbB[:], gatesB[:, 1]).then_inc(vec_step, 1)
            dve.wait_ge(small_in, 16 * (4 * KD + 6))
            for b in range(B):
                for k in range(KD):
                    dve.scalar_tensor_tensor(out=m.wog[:, b, k, :], in0=wo[:, k, :], scalar=onw[:, 0:1],
                                             in1=gatesB[:, 0, b, :], op0=ALU.mult, op1=ALU.mult)\
                        .then_inc(vec_step, 1)
            n = 8 + B * KD
            for k in range(KD):
                for t in range(FIRS):
                    dve.tensor_scalar(m.diag_fs[:, k, t, :], m.ident[:], fs_w[:, k, t:t + 1], None, ALU.mult)\
                        .then_inc(vec_step, 1)
            n += KD * FIRS
            dve.wait_ge(act_step, 4)
            for h in range(H):
                dve.scalar_tensor_tensor(out=m.rtau[:, h:h + 1], in0=taus[:, 4 + h:5 + h], scalar=0.0,
                                         in1=taus[:, h // 2:h // 2 + 1], op0=ALU.mult, op1=ALU.add)\
                    .then_inc(vec_step, 1)
            n += H
            dve.wait_ge(vec_step, n)
            dve.reciprocal(m.rtau[:], m.rtau[:]).then_inc(vec_step, 1)
            dve.wait_ge(vec_step, n + 1)


def units_ahead(eng, front, body):
    front(0, 0)
    with eng.Fori(0, B - 1) as b:
        for g in range(UB):
            body(b * UB + g, g, b * UB + (g + 1))
    for g in range(UB):
        u = (B - 1) * UB + g
        body(u, g, u + 1 if g < UB - 1 else None)


def norm_inputs(nc, m, w):
    with ExitStack() as ctx:
        def sb(name, shape):
            return ctx.enter_context(nc.sbuf_tensor(name, shape, F32))

        def sem(name):
            return ctx.enter_context(nc.semaphore(name))

        xin = [sb(f"xin{i}", [P, J, D]) for i in range(2)]
        xn = [sb(f"xn{i}", [P, J, D]) for i in range(2)]
        hT = [sb(f"hT{i}", [P, KD, UT]) for i in range(2)]
        stats = sb("ln_stats", [P, J, 6])
        mv = [sb(f"ln_mv{i}", [P, J, 2]) for i in range(2)]
        rstd = [sb(f"ln_rstd{i}", [P, J]) for i in range(2)]
        modb = sb("ln_modb", [P, 4])
        pad = sb("ln_pad", [P, 1])
        tp = [ctx.enter_context(nc.psum_tensor(f"ln_tp{i}", [P, KD, UT], F32)) for i in range(2)]
        gp = [ctx.enter_context(nc.psum_tensor(f"ln_gp{i}", [P, 512], F32)) for i in range(2)]

        x_in = [sem(f"ln_x_in{i}") for i in range(2)]
        store = [sem(f"ln_store{i}") for i in range(2)]
        ready = sem("ln_ready")
        vec_step = sem("ln_vec_step")
        mod_step = sem("ln_mod_step")
        xn_done = sem("ln_xn_done")
        rstd_done = sem("ln_rstd_done")
        var_done = sem("ln_var_done")
        tp_done = sem("ln_tp_done")
        h_done = sem("ln_h_done")
        g_done = sem("ln_g_done")
        gcopy_done = sem("ln_gcopy_done")
        block = ctx.enter_context(nc.Block("norm_inputs"))
        x_v = w.x.rearrange("b (g j p) d -> (b g) p j d", j=J, p=P)

        @block.sync
        def _(sp):
            sp.sem_inc(xn_done, 2)
            sp.sem_inc(store[0], 16)
            sp.sem_inc(store[1], 16)

            def load(u, i):
                sp.wait_ge(xn_done, u + 1)
                sp.dma_start(xin[i][:], x_v[bass.ds(u, 1)].squeeze(0)).then_inc(x_in[i], 16)

            def put(u, i):
                sp.wait_ge(h_done, u + 3)
                sp.dma_start(m.hT_d[bass.ds(u, 1)].squeeze(0), hT[i][:]).then_inc(store[i], 16)

            load(0, 0)
            load(1, 1)
            with sp.Fori(1, NU // 2) as t:
                for i in range(2):
                    load(t * 2 + i, i)
                    put(t * 2 + i - 2, i)
            for i in range(2):
                put(NU - 2 + i, i)
            for i in range(2):
                sp.wait_ge(store[i], 16 + 16 * NU // 2)

        @block.vector
        def _(dve):
            def front(u, g):
                i = g % 2
                dve.wait_ge(x_in[i], (u - i) * 8 + 16)
                for j in range(J):
                    dve.bn_stats(stats[:, j, :], xin[i][:, j, :]).then_inc(vec_step, 1)
                dve.wait_ge(vec_step, u * (2 * J) + J)
                dve.memset(pad[:], 0.0)
                for j in range(J):
                    dve.bn_aggr(mv[i][:, j, :], stats[:, j, :]).then_inc(vec_step, 1)
                dve.wait_ge(vec_step, u * (2 * J) + 2 * J)
                dve.tensor_scalar(mv[i][:, :, 1], mv[i][:, :, 1], LN_EPS, None, ALU.add).then_inc(var_done, 1)

            def body(u, g, nxt):
                i = g % 2
                if nxt is not None:
                    front(nxt, g + 1)
                dve.wait_ge(rstd_done, u + 1)
                dve.wait_ge(tp_done, u + 1)
                for j in range(J):
                    ins = dve.tensor_scalar(xn[i][:, j, :], xin[i][:, j, :], mv[i][:, j, 0:1], rstd[i][:, j:j + 1],
                                            ALU.subtract, ALU.mult)
                ins.then_inc(xn_done, 1)

            units_ahead(dve, front, body)

        @block.gpsimd
        def _(pool):
            pool.sem_inc(ready, 1)
            pool.sem_inc(h_done, 2)
            pool.sem_inc(tp_done, 2)
            pool.sem_inc(g_done, 2)
            pool.sem_inc(gcopy_done, 2)
            with pool.Fori(0, NU // 2) as t:
                for i in range(2):
                    pool.wait_ge(var_done, t * 2 + (i + 1))
                    pool.wait_ge(xn_done, t * 2 + (i + 1))
                    pool.tensor_tensor(rstd[i][:], mv[i][:, :, 1], m.half_pow[:, 0:J], ALU.pow).then_inc(rstd_done, 1)

        @block.tensor
        def _(pe):
            def front(u, g):
                i = g % 2
                pe.wait_ge(xn_done, u + 3)
                pe.wait_ge(h_done, u + 1)
                for j in range(J):
                    for k in range(KD):
                        ins = pe.transpose(tp[i][:, k, j * P:(j + 1) * P], xn[i][:, j, k * P:(k + 1) * P],
                                           m.ident[:])
                ins.then_inc(tp_done, 1)

            def body(u, g, nxt):
                i = g % 2
                if nxt is not None:
                    front(nxt, g + 1)
                pe.wait_ge(h_done, u + 3)
                pe.wait_ge(gcopy_done, u + 1)
                for j in range(J):
                    out = gp[i][:, j * 8:j * 8 + 8]
                    for k in range(KD):
                        pe.matmul(out, hT[i][:, k, j * P:(j + 1) * P], m.wgate[:, k, :],
                                  start=(k == 0), stop=False)
                    ins = pe.matmul(out, m.ones[0:1, :], m.bid_row[0:1, :], start=False, stop=True)
                ins.then_inc(g_done, 1)

            units_ahead(pe, front, body)

        @block.scalar
        def _(act):
            def front(u, g):
                i = g % 2
                if g % UB == 0:
                    act.wait_ge(h_done, u + 2)
                    act.wait_ge(ready, 1)
                    act.activation(modb[:].unsqueeze(2), m.mod[:, 0:4, bass.ds(u // UB, 1)], ACT.Copy)\
                        .then_inc(mod_step, UB)
                    act.wait_ge(mod_step, u + UB)
                act.wait_ge(tp_done, u + 3)
                act.wait_ge(store[i], (u - i) * 8 + 16)
                act.wait_ge(g_done, u + 1)
                for k in range(KD):
                    ins = act.activation(hT[i][:, k, :], tp[i][:, k, :], ACT.Identity,
                                         scale=modb[:, 2 + k:3 + k], bias=modb[:, k:k + 1])
                ins.then_inc(h_done, 1)

            def body(u, g, nxt):
                if nxt is not None:
                    front(nxt, g + 1)
                act.wait_ge(g_done, u + 3)
                act.wait_ge(ready, 1)
                act.activation(m.gates[:, bass.ds(u * (J * 8), J * 8)], gp[g % 2][:, 0:J * 8], ACT.Copy)\
                    .then_inc(gcopy_done, 1)

            units_ahead(act, front, body)
            act.wait_ge(gcopy_done, 2 + NU)
            act.activation(m.gates[:], m.gates[:], ACT.Sigmoid).then_inc(gcopy_done, 1)
            act.wait_ge(gcopy_done, 3 + NU)


def conv_heads(nc, m, w):
    NBLK = 3 * KD
    NKQ = 2 * KD
    with ExitStack() as ctx:
        def sb(name, shape):
            return ctx.enter_context(nc.sbuf_tensor(name, shape, F32))

        def psum(name):
            return ctx.enter_context(nc.psum_tensor(name, [P, 512], F32))

        def sem(name):
            return ctx.enter_context(nc.semaphore(name))

        two = range(2)

        def weight(o):
            return (o + KD) % NBLK

        hT = [sb(f"cv_hT{i}", [P, KD, UT]) for i in two]
        pre = [sb(f"cv_pre{i}", [P, NBLK, CONV - 1 + UT]) for i in two]
        acc = [sb(f"cv_acc{i}", [P, UT]) for i in range(3)]
        vT = [sb(f"cv_vT{i}", [P, KD, FIRS - 1 + UT]) for i in two]
        kqc = [sb(f"cv_kqc{i}", [P, 2 * KD, UT]) for i in two]
        vf = [sb(f"cv_vf{i}", [P, J, 2 * D]) for i in two]
        kq = [sb(f"cv_kq{i}", [P, J, 2 * D]) for i in two]
        kqT = [sb(f"cv_kqT{i}", [P, J, 4 * P]) for i in two]
        sq = [sb(f"cv_sq{i}", [P, 2 * D]) for i in two]
        ss = [sb(f"cv_ss{i}", [P, 2 * H]) for i in two]
        rn = [sb(f"cv_rn{i}", [P, 2 * H]) for i in two]
        pj = [psum(f"cv_pj{i}") for i in two]
        vf_ps = [psum(f"cv_vfps{i}") for i in two]
        kq_ps = [psum(f"cv_kqps{i}") for i in two]
        kqT_ps = [psum(f"cv_kqTps{i}") for i in two]

        h_in = [sem(f"cv_h_in{i}") for i in two]
        store = [sem(f"cv_store{i}") for i in two]
        pj_done = sem("cv_pj_done")
        pre_done = sem("cv_pre_done")
        conv_step = sem("cv_conv_step")
        conv_done = sem("cv_conv_done")
        halo_done = sem("cv_halo_done")
        vhalo_done = sem("cv_vhalo_done")
        silu_done = sem("cv_silu_done")
        vf_done = sem("cv_vf_done")
        vfe_done = sem("cv_vfe_done")
        kq_done = sem("cv_kq_done")
        sq_done = sem("cv_sq_done")
        red_done = sem("cv_red_done")
        eps_done = sem("cv_eps_done")
        rn_done = sem("cv_rn_done")
        mult_done = sem("cv_mult_done")
        kqT_done = sem("cv_kqT_done")
        kqTe_done = sem("cv_kqTe_done")
        block = ctx.enter_context(nc.Block("conv_heads"))

        @block.sync
        def _(sp):
            sp.sem_inc(pj_done, 2 * NBLK)
            sp.sem_inc(vfe_done, 2)
            sp.sem_inc(kqTe_done, 2)
            sp.sem_inc(silu_done, 3)
            for i in two:
                sp.sem_inc(store[i], 48)
            def load(u, i):
                sp.wait_ge(pj_done, u * NBLK + NBLK)
                sp.dma_start(hT[i][:], m.hT_d[bass.ds(u, 1)].squeeze(0)).then_inc(h_in[i], 16)

            def put(u, i):
                rows = bass.ds(u * J, J)
                sp.wait_ge(vfe_done, u * J + (J + 2))
                sp.dma_start(m.vf_d[rows].rearrange("j p c -> p j c"), vf[i][:]).then_inc(store[i], 16)
                sp.wait_ge(mult_done, u * J + (J + 2))
                sp.dma_start(m.kq_d[rows].rearrange("j p c -> p j c"), kq[i][:]).then_inc(store[i], 16)
                sp.wait_ge(kqTe_done, u * J + (J + 2))
                sp.dma_start(m.kqT_d[rows].rearrange("j p c -> p j c"), kqT[i][:]).then_inc(store[i], 16)

            load(0, 0)
            load(1, 1)
            with sp.Fori(1, NU // 2) as t:
                for i in two:
                    load(t * 2 + i, i)
                    put(t * 2 + i - 2, i)
            for i in two:
                put(NU - 2 + i, i)
            for i in two:
                sp.wait_ge(store[i], 48 + 48 * NU // 2)

        @block.tensor
        def _(pe):
            pe.sem_inc(pre_done, 2)

            def project(u, g, o):
                i = g % 2
                if o == 0:
                    pe.wait_ge(h_in[i], 16 * ((u - i) // 2 + 1) if isinstance(u, int) else (u - i) * 8 + 16)
                pe.wait_ge(pre_done, u * NBLK + (o + 1))
                for k in range(KD):
                    ins = pe.matmul(pj[o % 2][:], m.wqkv[:, k, weight(o) * P:(weight(o) + 1) * P], hT[i][:, k, :],
                                    start=(k == 0), stop=(k == KD - 1))
                ins.then_inc(pj_done, 1)

            def turn_v(u, g, j):
                i = g % 2
                if j == 0:
                    pe.wait_ge(silu_done, u * NBLK + (NBLK + 3))
                    pe.wait_ge(vhalo_done, u + 1)
                pe.wait_ge(vfe_done, u * J + (j + 1))
                c0 = j * P
                for k in range(KD):
                    pe.transpose(vf_ps[j % 2][:, k * P:(k + 1) * P],
                                 vT[i][:, k, FIRS - 1 + c0:FIRS - 1 + c0 + P], m.ident[:])
                for k in range(KD):
                    for t in range(FIRS):
                        ins = pe.matmul(vf_ps[j % 2][:, D + k * P:D + (k + 1) * P], vT[i][:, k, c0 + t:c0 + t + P],
                                        m.diag_fs[:, k, t, :], start=(t == 0), stop=(t == FIRS - 1))
                ins.then_inc(vf_done, 1)

            def turn_kq(u, g, j):
                if j == 0:
                    pe.wait_ge(silu_done, u * NBLK + (NKQ + 3))
                pe.wait_ge(mult_done, u * J + (j + 1))
                for a in range(2 * KD):
                    ins = pe.transpose(kq_ps[j % 2][:, a * P:(a + 1) * P], kqc[g % 2][:, a, j * P:(j + 1) * P],
                                       m.ident[:])
                ins.then_inc(kq_done, 1)

            def turn_back(u, g, j):
                pe.wait_ge(mult_done, u * J + (j + 3))
                pe.wait_ge(kqTe_done, u * J + (j + 1))
                for a in range(2 * KD):
                    ins = pe.transpose(kqT_ps[j % 2][:, a * P:(a + 1) * P], kq[g % 2][:, j, a * P:(a + 1) * P],
                                       m.ident[:])
                ins.then_inc(kqT_done, 1)

            def front(u, g):
                for o in range(NBLK):
                    project(u, g, o)

            def body(u, g, nxt):
                for s in range(NBLK):
                    if nxt is not None:
                        project(nxt, g + 1, s)
                    if s < J:
                        turn_kq(u, g, s)
                    if 2 <= s < J + 2:
                        turn_back(u, g, s - 2)
                    if 1 <= s < J + 1:
                        turn_v(u, g, s - 1)

            units_ahead(pe, front, body)

        @block.scalar
        def _(act):
            act.activation(pre[0][:, :, 0:CONV - 1], m.zeros[:, 0:NBLK * (CONV - 1)]
                           .rearrange("p (a b) -> p a b", a=NBLK), ACT.Copy).then_inc(halo_done, 1)
            act.activation(vT[0][:, :, 0:FIRS - 1], m.zeros[:, 0:KD * (FIRS - 1)]
                           .rearrange("p (a b) -> p a b", a=KD), ACT.Copy).then_inc(vhalo_done, 1)

            def evacuate(u, g, o):
                i = g % 2
                act.wait_ge(pj_done, u * NBLK + (o + 1 + 2 * NBLK))
                act.activation(pre[i][:, o, CONV - 1:], pj[o % 2][:], ACT.Copy)
                act.wait_ge(silu_done, u * NBLK + (o + 1))
                act.activation(acc[o % 3][:], pj[o % 2][:], ACT.Identity, scale=m.conv_w[:, weight(o), CONV - 1:CONV])\
                    .then_inc(pre_done, 1)

            def halo(u, g):
                if g % UB == UB - 1:
                    src = m.zeros[:, 0:NBLK * (CONV - 1)].rearrange("p (a b) -> p a b", a=NBLK)
                else:
                    act.wait_ge(pre_done, u * NBLK + (NBLK + 2))
                    src = pre[g % 2][:, :, UT:UT + CONV - 1]
                act.activation(pre[(g + 1) % 2][:, :, 0:CONV - 1], src, ACT.Copy).then_inc(halo_done, 1)

            def vhalo(u, g):
                if not isinstance(u, int) or u > 0:
                    act.wait_ge(vf_done, u * J)
                if g % UB == UB - 1:
                    src = m.zeros[:, 0:KD * (FIRS - 1)].rearrange("p (a b) -> p a b", a=KD)
                else:
                    act.wait_ge(silu_done, u * NBLK + (NBLK + 3))
                    src = vT[g % 2][:, :, UT:UT + FIRS - 1]
                act.activation(vT[(g + 1) % 2][:, :, 0:FIRS - 1], src, ACT.Copy).then_inc(vhalo_done, 1)

            def silu(u, g, o):
                i = g % 2
                act.wait_ge(conv_done, u * NBLK + (o + 1))
                dst = kqc[i][:, o, :] if o < NKQ else vT[i][:, o - NKQ, FIRS - 1:]
                act.activation(dst, acc[o % 3][:], ACT.Silu).then_inc(silu_done, 1)

            def front_slot(u, g, s):
                evacuate(u, g, s)
                if s >= 1:
                    silu(u, g, s - 1)
                if s == NBLK - 1:
                    silu(u, g, s)
                    halo(u, g)
                    vhalo(u, g)

            def front(u, g):
                for s in range(NBLK):
                    front_slot(u, g, s)

            def body(u, g, nxt):
                i = g % 2
                act.wait_ge(store[i], (u - i) * 24 + 48)
                for s in range(NBLK):
                    if s < J:
                        act.wait_ge(kq_done, u * J + (s + 1))
                        act.wait_ge(red_done, u * J + (s + 1))
                        act.activation(sq[s % 2][:], kq_ps[s % 2][:], ACT.Square).then_inc(sq_done, 1)
                    if nxt is not None:
                        front_slot(nxt, g + 1, s)
                    if 2 <= s < J + 2:
                        act.wait_ge(kqT_done, u * J + (s - 1))
                        act.activation(kqT[i][:, s - 2, :], kqT_ps[s % 2][:], ACT.Copy).then_inc(kqTe_done, 1)
                    if 1 <= s < J + 1:
                        act.wait_ge(vf_done, u * J + s)
                        act.activation(vf[i][:, s - 1, :], vf_ps[(s - 1) % 2][:], ACT.Copy).then_inc(vfe_done, 1)

            units_ahead(act, front, body)

        @block.vector
        def _(dve):
            dve.sem_inc(red_done, 2)
            dve.sem_inc(rn_done, 2)
            dve.sem_inc(mult_done, 2)

            def conv(u, g, o):
                i = g % 2
                dve.wait_ge(pre_done, u * NBLK + (o + 3))
                if o == 0:
                    dve.wait_ge(halo_done, u + 1)
                for t in range(CONV - 1):
                    if t:
                        dve.wait_ge(conv_step, (u * NBLK + o) * 2 + t)
                    ins = dve.scalar_tensor_tensor(out=acc[o % 3][:], in0=pre[i][:, o, t:t + UT],
                                                   scalar=m.conv_w[:, weight(o), t:t + 1], in1=acc[o % 3][:],
                                                   op0=ALU.mult, op1=ALU.add)
                    ins.then_inc(conv_done if t == CONV - 2 else conv_step, 1)

            def reduce_sq(u, j):
                dve.wait_ge(sq_done, u * J + (j + 1))
                dve.wait_ge(rn_done, u * J + (j + 1))
                dve.tensor_reduce(ss[j % 2][:], sq[j % 2][:].rearrange("p (h d) -> p h d", d=DK), AX_X, ALU.add)\
                    .then_inc(red_done, 1)

            def normalise(u, g, j):
                dve.wait_ge(rn_done, u * J + (j + 3))
                if j == 0:
                    dve.wait_ge(store[g % 2], (u - g % 2) * 24 + 48)
                v = lambda a: a.rearrange("p (h d) -> p h d", d=DK)
                dve.tensor_tensor(v(kq[g % 2][:, j, :]), v(kq_ps[j % 2][:]),
                                  rn[j % 2][:].unsqueeze(2).to_broadcast([P, 2 * H, DK]), ALU.mult)\
                    .then_inc(mult_done, 1)

            def front(u, g):
                for o in range(NBLK):
                    conv(u, g, o)

            def body(u, g, nxt):
                for s in range(NBLK):
                    if 1 <= s < J + 1:
                        normalise(u, g, s - 1)
                    if s < J:
                        reduce_sq(u, s)
                    if nxt is not None:
                        conv(nxt, g + 1, s)

            units_ahead(dve, front, body)

        @block.gpsimd
        def _(pool):
            def body(u):
                for j in range(J):
                    pool.wait_ge(red_done, u * J + (j + 3))
                    pool.tensor_tensor(ss[j % 2][:], ss[j % 2][:], m.l2_eps[:, 0:2 * H], ALU.add)\
                        .then_inc(eps_done, 1)
                    pool.wait_ge(mult_done, u * J + (j + 1))
                    pool.wait_ge(eps_done, u * J + (j + 1))
                    pool.tensor_tensor(rn[j % 2][:], ss[j % 2][:], m.half_pow[:, 0:2 * H], ALU.pow)\
                        .then_inc(rn_done, 1)

            with pool.Fori(0, NU) as u:
                body(u)


def long_filter(nc, m, w):
    CB = 8
    RING = 4
    with ExitStack() as ctx:
        def sb(name, shape):
            return ctx.enter_context(nc.sbuf_tensor(name, shape, F32))

        def sem(name):
            return ctx.enter_context(nc.semaphore(name))

        NF = NT // 2
        v = sb("fl_v", [P, B, 1 + TB, D])
        fl = sb("fl_out", [P, B, TB, D])
        toep = [sb(f"fl_toep{i}", [P, CB, TOEP]) for i in range(RING)]
        v_in = [t[:].rearrange("p a b -> p (a b)")[:, 0:2 * D].rearrange("p (n c) -> p n c", c=D) for t in toep]
        ps = [ctx.enter_context(nc.psum_tensor(f"fl_ps{i}", [P, CB, B, TB], F32)) for i in range(RING)]
        fp = [ctx.enter_context(nc.psum_tensor(f"fl_fp{i}", [P, 2 * D], F32)) for i in range(RING)]
        loaded = [sem(f"fl_loaded{i}") for i in range(RING)]
        flip_done = sem("fl_flip_done")
        fev_done = [sem(f"fl_fev_done{i}") for i in range(2)]
        zero_done = sem("fl_zero_done")
        toep_in = [sem(f"fl_toep_in{i}") for i in range(RING)]
        mm_done = sem("fl_mm_done")
        ev_done = [sem(f"fl_ev_done{i}") for i in range(2)]
        store = sem("fl_store")
        block = ctx.enter_context(nc.Block("long_filter"))

        @block.sync
        def _(sp):
            sp.sem_inc(mm_done, RING)
            sp.sem_inc(flip_done, RING)
            sp.sem_inc(fev_done[0], 2)
            sp.sem_inc(fev_done[1], 2)
            with sp.Fori(0, NF // RING) as it:
                for q in range(RING):
                    sp.wait_ge(flip_done, it * RING + (q + 1))
                    sp.dma_start(v_in[q], m.vf_d[bass.ds(it * (2 * RING) + 2 * q, 2), :, 0:D]
                                 .rearrange("n p c -> p n c")).then_inc(loaded[q], 16)
            sp.wait_ge(flip_done, NF + RING)
            with sp.Fori(0, D // (CB * RING)) as it:
                for q in range(RING):
                    sp.wait_ge(mm_done, it * RING + (q + 1))
                    rows = bass.AP(tensor=m.taps_d.tensor, offset=(it * RING + q) * (CB * TAPROW),
                                   ap=[[1, P], [TAPROW, CB], [1, TOEP]])
                    sp.dma_start(toep[q][:], rows).then_inc(toep_in[q], 16)

        @block.gpsimd
        def _(pool):
            pool.sem_inc(ev_done[0], 2)
            pool.sem_inc(ev_done[1], 2)
            for b in range(B):
                pool.memset(v[:, b, 0, :], 0.0).then_inc(zero_done, 1)
            for half in range(2):
                for i in range(2):
                    pool.wait_ge(ev_done[i], 2 + (half + 1) * D // (CB * 4))
                for b in range(B):
                    c = slice(half * P, (half + 1) * P)
                    pool.dma_start(m.fl_d[b * TB:(b + 1) * TB, :, c].rearrange("n p c -> p n c"), fl[:, b, :, c])\
                        .then_inc(store, 16)
            pool.wait_ge(store, 16 * 2 * B)

        @block.tensor
        def _(pe):
            with pe.Fori(0, NF // RING) as it:
                for q in range(RING):
                    pe.wait_ge(loaded[q], it * 16 + 16)
                    pe.wait_ge(fev_done[q % 2], it * (RING // 2) + (q // 2 + 1))
                    pe.matmul(fp[q][:], m.flip[:], v_in[q].rearrange("p n c -> p (n c)"), start=True, stop=True)\
                        .then_inc(flip_done, 1)
            pe.wait_ge(fev_done[0], 2 + NF // 2)
            pe.wait_ge(fev_done[1], 2 + NF // 2)
            pe.wait_ge(zero_done, B)
            with pe.Fori(0, D // (CB * RING)) as it:
                for q in range(RING):
                    pe.wait_ge(toep_in[q], it * 16 + 16)
                    pe.wait_ge(ev_done[q % 2], it * (RING // 2) + (q // 2 + 1))
                    for c in range(CB):
                        ch = bass.ds(it * (RING * CB) + (q * CB + c), 1)
                        pe.matmul(ps[q][:, c], toep[q][:, c, 0:P], v[:, :, 1:, ch].squeeze(3), start=True, stop=True)
                        ins = pe.matmul(ps[q][0:TOEP - P, c], toep[q][:, c, P:], v[:, :, 0:TB, ch].squeeze(3),
                                        start=False, stop=True, skip_group_check=True)
                    ins.then_inc(mm_done, 1)

        def pair_of(it, q):
            n = it * (2 * RING) + 2 * q
            return v[:].rearrange("p b n c -> p (b n) c")[:, bass.ds(n + it // 2 + 1, 2), :]

        @block.scalar
        def _(act):
            with act.Fori(0, NF // RING) as it:
                for q in range(0, RING, 2):
                    act.wait_ge(flip_done, it * RING + (q + 1 + RING))
                    act.nop()
                    act.activation(pair_of(it, q), fp[q][:].rearrange("p (n c) -> p n c", c=D), ACT.Copy)\
                        .then_inc(fev_done[0], 1)
            with act.Fori(0, D // (CB * RING)) as it:
                for q in range(0, RING, 2):
                    act.wait_ge(mm_done, it * RING + (q + 1 + RING))
                    act.nop()
                    c0 = bass.ds(it * (RING * CB) + q * CB, CB)
                    act.activation(fl.ap().rearrange("p b n c -> p (b n) c")[:, :, c0],
                                   ps[q].ap().rearrange("p c b n -> p (b n) c"), ACT.Copy).then_inc(ev_done[0], 1)

        @block.vector
        def _(dve):
            with dve.Fori(0, NF // RING) as it:
                for q in range(1, RING, 2):
                    dve.wait_ge(flip_done, it * RING + (q + 1 + RING))
                    dve.tensor_scalar(pair_of(it, q), fp[q][:].rearrange("p (n c) -> p n c", c=D), 1.0, None,
                                      ALU.mult).then_inc(fev_done[1], 1)
            with dve.Fori(0, D // (CB * RING)) as it:
                for q in range(1, RING, 2):
                    dve.wait_ge(mm_done, it * RING + (q + 1 + RING))
                    c0 = bass.ds(it * (RING * CB) + q * CB, CB)
                    dve.tensor_scalar(fl.ap().rearrange("p b n c -> p (b n) c")[:, :, c0],
                                      ps[q].ap().rearrange("p c b n -> p (b n) c"), 1.0, None, ALU.mult)\
                        .then_inc(ev_done[1], 1)


def delta_rule(nc, m, w):
    NL = len(m.levels)
    with ExitStack() as ctx:
        def sb(name, shape):
            return ctx.enter_context(nc.sbuf_tensor(name, shape, F32))

        def psum(name):
            return ctx.enter_context(nc.psum_tensor(name, [P, H, P], F32))

        def sem(name):
            return ctx.enter_context(nc.semaphore(name))

        two = range(2)
        kqT = [[sb(f"dr_kqT{p}{i}", [P, 4, P]) for i in two] for p in two]
        kTz = [[sb(f"dr_kTz{p}{i}", [P, H, P]) for i in two] for p in two]
        k = [[sb(f"dr_k{p}{i}", [P, D]) for i in two] for p in two]
        v = [[sb(f"dr_v{p}{i}", [P, D]) for i in two] for p in two]
        DT = [[sb(f"dr_DT{i}{z}", [P, 2, H, P // 2]) for z in two] for i in two]
        Tt = [sb(f"dr_Tt{i}", [P, H, P]) for i in two]
        att = [[sb(f"dr_att{p}{i}", [P, H, P]) for i in two] for p in two]
        o = [[sb(f"dr_o{p}{i}", [P, D]) for i in two] for p in two]
        A = [sb(f"dr_A{i}", [P, H, P]) for i in two]
        C = [[sb(f"dr_C{i}{s}", [P, H, P // 2]) for s in m.levels] for i in two]
        ident4 = sb("dr_ident4", [P, H, P])
        F = [sb(f"dr_F{i}", [P, H, P]) for i in two]
        Dm = [sb(f"dr_D{i}", [P // 2, H, P]) for i in two]
        Ys = [sb(f"dr_Y{i}", [P // 2, H, P // 2]) for i in two]
        R = [sb(f"dr_R{i}", [P, D]) for i in two]
        U = [sb(f"dr_U{i}", [P, D]) for i in two]
        S = [sb(f"dr_S{b}", [P, H // 2, P]) for b in range(B)]
        y_ps = [psum(f"dr_yps{i}") for i in two]
        z_ps = [psum(f"dr_zps{i}") for i in two]
        t_ps = [psum(f"dr_tps{i}") for i in two]
        c_ps = [psum(f"dr_cps{i}") for i in two]

        loaded = [sem(f"dr_loaded{p}") for p in two]
        store = [sem(f"dr_store{p}") for p in two]
        zero_done = sem("dr_zero_done")
        gram_done = sem("dr_gram_done")
        attp_done = sem("dr_attp_done")
        A_done = sem("dr_A_done")
        att_done = sem("dr_att_done")
        F_done = sem("dr_F_done")
        DT0_done = sem("dr_DT0_done")
        y_done = sem("dr_y_done")
        Ys_done = sem("dr_Ys_done")
        z_done = sem("dr_z_done")
        C_done = sem("dr_C_done")
        DT_done = sem("dr_DT_done")
        even_done = sem("dr_even_done")
        Ft_done = sem("dr_Ft_done")
        t_done = sem("dr_t_done")
        D_done = sem("dr_D_done")
        kS_done = sem("dr_kS_done")
        R_step = sem("dr_R_step")
        R_done = sem("dr_R_done")
        u_done = sem("dr_u_done")
        U_done = sem("dr_U_done")
        so_done = sem("dr_so_done")
        o_done = sem("dr_o_done")
        S_done = sem("dr_S_done")
        block = ctx.enter_context(nc.Block("delta_rule"))

        def flat(a):
            return a[:].rearrange("p h c -> p (h c)")

        def moved(i, l, which):
            s = m.levels[l]
            if l == NL - 1:
                return Tt[i][:, :, which * s:(which + 1) * s]
            d = DT[i][(l + 1) % 2][:].rearrange("p b h (n two s) -> p (h n) b two s", two=2, s=s)
            return d[:, :, :, which, :]

        def kept(a, l):
            s = m.levels[l]
            if l == NL - 1:
                return a
            return a.rearrange("p h (n b s) -> p (h n) b s", b=2, s=s)

        def half(bank):
            return bank[0:P // 2, 0:H // 2, :].rearrange("p a (e d) -> p (a e) d", e=2)

        def heads(bank, half):
            return bank[:, 2 * half:2 * half + 2, :].rearrange("p a (e d) -> p (a e) d", e=2)

        @block.sync
        def _(sp):
            sp.sem_inc(so_done, 4)
            sp.sem_inc(o_done, 2)
            sp.sem_inc(S_done, 4)
            for p in two:
                sp.sem_inc(store[p], 32)
            sp.wait_ge(zero_done, B + 4 + H)
            with sp.Fori(0, TB) as t:
                for p in two:
                    sp.wait_ge(so_done, t * 4 + (2 * p + 2))
                    for i in two:
                        n = bass.ds(t + (2 * p + i) * TB, 1)
                        sp.dma_start(flat(kqT[p][i]), m.kqT_d[n].squeeze(0)).then_inc(loaded[p], 16)
                        for e in two:
                            rows = slice(e * DK, (e + 1) * DK)
                            sp.dma_start(kTz[p][i][rows, e::2, :], m.kqT_d[n, rows, 0:2 * P].squeeze(0)
                                         .rearrange("p (a c) -> p a c", a=2)).then_inc(loaded[p], 16)
                        sp.dma_start(k[p][i][:], m.kq_d[n, :, 0:D].squeeze(0)).then_inc(loaded[p], 16)
                        sp.dma_start(v[p][i][:], m.vf_d[n, :, 0:D].squeeze(0)).then_inc(loaded[p], 16)

        def ahead(t, p):
            return t * (4 * NL) + 2 * p * NL

        @block.tensor
        def _(pe):
            def products(t, p, first=False):
                pe.wait_ge(loaded[p], t * 160 + 160)
                for i in two:
                    for h in range(H):
                        ins = pe.matmul(t_ps[i][:, h, :], kqT[p][i][:, h // 2, :], kTz[p][i][:, h, :],
                                        start=True, stop=True)
                    ins.then_inc(gram_done, 1)
                for i in two:
                    if not first:
                        pe.wait_ge(DT_done, ahead(t, p) + (i - 1))
                    for h in range(H):
                        ins = pe.matmul(z_ps[i][:, h, :], kTz[p][i][:, h, :], kqT[p][i][:, 2 + h // 2, :],
                                        start=True, stop=True)
                    ins.then_inc(attp_done, 1)

            def first_turn(t, p):
                u2 = t * 4 + 2 * p
                for i in two:
                    pe.wait_ge(F_done, u2 + (i + 1))
                    for h in range(H):
                        ins = pe.transpose(t_ps[i][:, h, :], F[i][:, h, :], m.ident[:])
                    ins.then_inc(Ft_done, 1)

            def level(t, p, l, between, behind):
                base = ahead(t, p) + 2 * l
                for i in two:
                    if l == 0:
                        pe.wait_ge(DT0_done, t * 4 + (2 * p + i + 1))
                    else:
                        pe.wait_ge(DT_done, base + (i - 1))
                        pe.wait_ge(even_done, base + (i - 1))
                    for a in range(H // 2):
                        ins = pe.transpose(t_ps[i][:, a, :], DT[i][l % 2][:, 0, 2 * a:2 * a + 2, :]
                                           .rearrange("p h c -> p (h c)"), m.ident[:])
                    ins.then_inc(t_done, 1)
                for i in two:
                    pe.wait_ge(C_done, base + (i + 1))
                    for h in range(H):
                        ins = pe.matmul(half(y_ps[i])[:, h, :], C[i][l][:, h, :], DT[i][l % 2][:, 1, h, :],
                                        start=True, stop=True)
                    ins.then_inc(y_done, 1)
                between()
                for i in two:
                    pe.wait_ge(Ys_done, base + (i + 1))
                    pe.wait_ge(D_done, base + (i + 1))
                    if l == 0:
                        pe.wait_ge(att_done, t * 4 + (2 * p + i + 1))
                    for h in range(H):
                        ins = pe.matmul(heads(z_ps[i], 0)[:, h, :], Dm[i][:, h, :], Ys[i][:, h, :], start=True,
                                        stop=True)
                    ins.then_inc(z_done, 1)
                behind()

            def scan(t, p, step, i):
                b = 2 * p + i
                u2 = t * 4 + (2 * p + i)
                if step == 0:
                    pe.wait_ge(S_done, u2 + 1)
                    pe.wait_ge(o_done, u2 + 1)
                    for a in range(H // 2):
                        ins = pe.matmul(c_ps[i][:, a, :], kqT[p][i][:, a, :], S[b][:, a, :], start=True, stop=True)
                    ins.then_inc(kS_done, 1)
                if step == 1:
                    pe.wait_ge(R_done, u2 + 1)
                    pe.wait_ge(S_done, u2 + 3)
                    for h in range(H):
                        ins = pe.matmul(heads(c_ps[i], 1)[:, h, :], Tt[i][:, h, :], R[i][:, h * DK:(h + 1) * DK],
                                        start=True, stop=True)
                    ins.then_inc(u_done, 1)
                if step == 2:
                    pe.wait_ge(U_done, u2 + 1)
                    for a in range(H // 2):
                        pe.matmul(c_ps[i][:, 2 + a, :], k[p][i][:, a * P:(a + 1) * P], U[i][:, a * P:(a + 1) * P],
                                  start=True, stop=True)
                if step >= 3:
                    a = step - 3
                    pe.matmul(c_ps[i][:, a, :], kqT[p][i][:, 2 + a, :], S[b][:, a, :], start=True, stop=False,
                              skip_group_check=True)
                    for h in (2 * a, 2 * a + 1):
                        ins = pe.matmul(heads(c_ps[i], 0)[:, h, :], att[p][i][:, h, :],
                                        U[i][:, h * DK:(h + 1) * DK], start=False, stop=(h % 2 == 1),
                                        skip_group_check=True)
                    if a == H // 2 - 1:
                        ins.then_inc(so_done, 1)

            fill = [([(1, 0), (1, 1)], []), ([(2, 0)], [(3, 0), (4, 0)]), ([(2, 1)], [(3, 1), (4, 1)])]

            def stage(cur, prev, after):
                for i in two:
                    if prev is not None:
                        pe.wait_ge(DT_done, ahead(*prev) + (2 * NL - 1 + i))
                        pe.wait_ge(even_done, ahead(*prev) + (2 * NL - 1 + i))
                        scan(*prev, 0, i)
                if cur is not None:
                    first_turn(*cur)
                for l in range(NL):
                    def between():
                        if prev is not None and l < len(fill):
                            for step, i in fill[l][0]:
                                scan(*prev, step, i)

                    def behind():
                        if prev is not None and l < len(fill):
                            for step, i in fill[l][1]:
                                scan(*prev, step, i)
                    if cur is not None:
                        level(*cur, l, between, behind)
                    else:
                        between()
                        behind()
                if after is not None:
                    products(*after)

            pe.wait_ge(zero_done, B + 4 + H)
            products(0, 0, first=True)
            pairs_ahead(pe, stage)

        @block.vector
        def _(dve):
            def beta(t, b, h0, n):
                return m.gates[:, bass.ds(t * 8 + (b * TB * 8 + h0), n)]

            def products(t, p, first=False):
                u2 = t * 4 + 2 * p
                for i in two:
                    dve.wait_ge(gram_done, u2 + (i + 1))
                    if not first:
                        dve.wait_ge(C_done, ahead(t, p) + (i - 1))
                    for h in range(H):
                        ins = dve.scalar_tensor_tensor(out=A[i][:, h, :], in0=t_ps[i][:, h, :],
                                                       scalar=beta(t, 2 * p + i, h, 1), in1=m.lower[:],
                                                       op0=ALU.mult, op1=ALU.mult)
                    ins.then_inc(A_done, 1)
            def keep_att(t, p):
                u2 = t * 4 + 2 * p
                for i in two:
                    dve.wait_ge(attp_done, u2 + (i + 1))
                    dve.tensor_tensor(att[p][i][:], z_ps[i][:], m.upper[:], ALU.mult).then_inc(att_done, 1)

            def level(t, p, l, between):
                base = ahead(t, p) + 2 * l
                for i in two:
                    dve.wait_ge(y_done, base + (i + 1))
                    dve.tensor_scalar(Ys[i][:], half(y_ps[i]), -1.0, None, ALU.mult).then_inc(Ys_done, 1)
                if l == 0:
                    keep_att(t, p)
                between()
                for i in two:
                    dve.wait_ge(z_done, base + (i + 1))
                    dve.tensor_tensor(moved(i, l, 1), kept(DT[i][l % 2][:, 1], l), kept(heads(z_ps[i], 0), l),
                                      ALU.add).then_inc(DT_done, 1)

            def scan(t, p, step, i):
                b = 2 * p + i
                u2 = t * 4 + (2 * p + i)
                if step == 0:
                    dve.wait_ge(kS_done, u2 + 1)
                    dve.tensor_tensor(R[i][:].rearrange("p (h d) -> p h d", d=DK), v[p][i][:]
                                      .rearrange("p (h d) -> p h d", d=DK), heads(c_ps[i], 0), ALU.subtract)\
                        .then_inc(R_step, 1)
                    dve.wait_ge(R_step, u2 + 1)
                    r = R[i][:].rearrange("p (h d) -> p h d", d=DK)
                    dve.tensor_tensor(r, r, beta(t, b, 0, H).unsqueeze(2).to_broadcast([P, H, DK]), ALU.mult)\
                        .then_inc(R_done, 1)
                if step == 2:
                    dve.wait_ge(so_done, u2 + 5)
                    for e in two:
                        r = slice(e * DK, (e + 1) * DK)
                        ins = dve.tensor_tensor(S[b][r, :, r], S[b][r, :, r], c_ps[i][r, H // 2:, r], ALU.add)
                    ins.then_inc(S_done, 1)

            def first_turn(t, p):
                for i in two:
                    dve.wait_ge(Ft_done, t * 4 + (2 * p + i + 1))
                    s = m.levels[0]
                    dve.tensor_tensor(DT[i][0][:].rearrange("p b h (n s) -> p (h n) b s", s=s),
                                      kept(ident4[:], 0), kept(t_ps[i][:], 0), ALU.subtract).then_inc(DT0_done, 1)

            def stage(cur, prev, after):
                for i in two:
                    if prev is not None:
                        scan(*prev, 0, i)
                if cur is not None:
                    first_turn(*cur)
                for l in range(NL):
                    def between():
                        if prev is not None and 2 <= l <= 3:
                            scan(*prev, 2, l - 2)
                    if cur is not None:
                        level(*cur, l, between)
                    else:
                        between()
                if after is not None:
                    products(*after)

            products(0, 0, first=True)
            pairs_ahead(dve, stage)

        @block.gpsimd
        def _(pool):
            for b in range(B):
                pool.memset(S[b][:], 0.0).then_inc(zero_done, 1)
            for p in two:
                for i in two:
                    pool.memset(kTz[p][i][:], 0.0).then_inc(zero_done, 1)
            for h in range(H):
                pool.tensor_copy(ident4[:, h, :], m.ident[:]).then_inc(zero_done, 1)
            with pool.Fori(0, TB) as t:
                for p in two:
                    for i in two:
                        pool.wait_ge(A_done, t * 4 + (2 * p + i + 1))
                        pool.tensor_tensor(F[i][:], A[i][:], m.first_lower[:], ALU.mult).then_inc(F_done, 1)
                    for l, s in enumerate(m.levels):
                        for i in two:
                            even = A[i][:].rearrange("p h (n two s) -> p (h n) two s", two=2, s=s)[:, :, 0, :]
                            pool.tensor_tensor(C[i][l][:].rearrange("p h (n s) -> p (h n) s", s=s), even,
                                               m.level_mask[l][:].rearrange("p h (n s) -> p (h n) s", s=s),
                                               ALU.mult).then_inc(C_done, 1)

        @block.scalar
        def _(act):
            def level(t, p, l):
                for i in two:
                    act.wait_ge(t_done, ahead(t, p) + (2 * l + i + 1))
                    for e in two:
                        ins = act.activation(Dm[i][:, e::2, :], t_ps[i][e * DK:(e + 1) * DK, 0:H // 2, :], ACT.Copy)
                    ins.then_inc(D_done, 1)
                for i in two:
                    act.activation(moved(i, l, 0), kept(DT[i][l % 2][:, 0], l), ACT.Copy).then_inc(even_done, 1)

            def scan(t, p, step, i):
                b = 2 * p + i
                u2 = t * 4 + (2 * p + i)
                if step == 1:
                    act.wait_ge(u_done, u2 + 1)
                    act.activation(U[i][:].rearrange("p (h d) -> p h d", d=DK), heads(c_ps[i], 1), ACT.Copy)\
                        .then_inc(U_done, 1)
                if step == 2:
                    act.wait_ge(so_done, u2 + 5)
                    act.wait_ge(S_done, u2 + 5)
                    act.wait_ge(store[p], t * 32 + 32)
                    act.activation(o[p][i][:].rearrange("p (h d) -> p h d", d=DK), heads(c_ps[i], 0), ACT.Copy)\
                        .then_inc(o_done, 1)
                    act.wait_ge(o_done, u2 + 3)
                    act.dma_start(m.o_d[bass.ds(t + b * TB, 1)].squeeze(0), o[p][i][:]).then_inc(store[p], 16)

            def stage(cur, prev, after):
                for l in range(NL):
                    if cur is not None:
                        level(*cur, l)
                    if prev is not None and l == 0:
                        scan(*prev, 1, 0)
                        scan(*prev, 1, 1)
                    if prev is not None and 2 <= l <= 3:
                        scan(*prev, 2, l - 2)

            pairs_ahead(act, stage)
            for p in two:
                act.wait_ge(store[p], 32 + 32 * TB)


def pairs_ahead(eng, stage):
    stage((0, 0), None, (0, 1))
    with eng.Fori(0, TB - 1) as t:
        stage((t, 1), (t, 0), (t + 1, 0))
        stage((t + 1, 0), (t, 1), (t + 1, 1))
    stage((TB - 1, 1), (TB - 1, 0), None)
    stage(None, (TB - 1, 1), None)


def mix_and_experts(nc, m, w):
    NX = SI // P + E
    NS = SI // P
    K3 = 3
    NH = J * H
    NR = J * K3 * H
    with ExitStack() as ctx:
        def sb(name, shape):
            return ctx.enter_context(nc.sbuf_tensor(name, shape, F32))

        def sem(name):
            return ctx.enter_context(nc.semaphore(name))

        two = range(2)
        eup = sb("mx_eup", [P, KD, E, EI])
        edn = sb("mx_edn", [P, E, D])
        sup = sb("mx_sup", [P, KD, SI])
        sdn = sb("mx_sdn", [P, NS, D])
        gsel = sb("mx_gsel", [P, J, NG, NG])
        esel = sb("mx_esel", [P, E, E])
        rms_eps = sb("mx_rms_eps", [P, NH])
        vf = [sb(f"mx_vf{i}", [P, J, 2 * D]) for i in two]
        fl = [sb(f"mx_fl{i}", [P, J, D]) for i in two]
        dl = [sb(f"mx_dl{i}", [P, J, D]) for i in two]
        xx = [sb(f"mx_x{i}", [P, J, D]) for i in two]
        hT = [sb(f"mx_hT{i}", [P, KD, UT]) for i in two]
        bs = sb("mx_bs", [P, J * K3 * H, 6])
        tmp = sb("mx_tmp", [P, 3, J * K3 * H])
        st = sb("mx_st", [P, J, K3 * 2 * H])
        stT = sb("mx_stT", [K3 * 2 * H, UT])
        hm = sb("mx_hm", [P, RH // P, UT])
        pr = sb("mx_pr", [P, NH, 3])
        red = sb("mx_red", [P, NH])
        ids = sb("mx_ids", [P, J, H])
        t0 = sb("mx_t0", [P, J, D])
        t1 = sb("mx_t1", [P, J, D])
        t2 = sb("mx_t2", [P, J, D])
        t3 = sb("mx_t3", [P, J, D])
        rms = sb("mx_rms", [P, NH])
        oT = sb("mx_oT", [P, KD, UT])
        x2 = [sb(f"mx_x2{i}", [P, J, D]) for i in two]
        st2 = sb("mx_st2", [P, J, 6])
        mv = sb("mx_mv", [P, J, 2])
        rstd = sb("mx_rstd", [P, J])
        modb = sb("mx_modb", [P, 4])
        h2T = [sb(f"mx_h2T{i}", [P, KD, UT]) for i in two]
        sc = sb("mx_sc", [P, J, E])
        hi = sb("mx_hi", [P, J * NG, 2])
        lo = sb("mx_lo", [P, J * NG, 2])
        gs = sb("mx_gs", [P, 4, J * NG])
        gq = sb("mx_gq", [P, 2, J, NG, NG])
        gm = sb("mx_gm", [P, J * NG])
        ms = sb("mx_ms", [P, J, E])
        rq = hm[:].rearrange("p f (g a b) -> p (f g a b)", a=E, b=E)\
            .rearrange("p (c j a b) -> p c j a b", c=2, j=J, a=E)
        rk = sb("mx_rk", [P, J, E])
        ws = sb("mx_ws", [P, J])
        comb = [sb(f"mx_comb{i}", [P, J, E]) for i in two]
        hs = [sb(f"mx_hs{r}", [P, UT]) for r in range(4)]
        acc = [sb(f"mx_acc{i}", [P, J, D]) for i in two]
        up_ps = [ctx.enter_context(nc.psum_tensor(f"mx_up{i}", [P, UT], F32)) for i in two]
        dn_ps = [ctx.enter_context(nc.psum_tensor(f"mx_dn{i}", [P, J, D], F32)) for i in two]
        M = [ctx.enter_context(nc.psum_tensor(f"mx_m{i}", [P, 512], F32)) for i in two]

        w_in = sem("mx_w_in")
        const_done = sem("mx_const_done")
        loaded = [sem(f"mx_loaded{i}") for i in two]
        stat_done = sem("mx_stat_done")
        var_step = sem("mx_var_step")
        var_done = sem("mx_var_done")
        std_done = sem("mx_std_done")
        stT_done = sem("mx_stT_done")
        stTe_done = sem("mx_stTe_done")
        hmid_done = sem("mx_hmid_done")
        gelu_done = sem("mx_gelu_done")
        logit_done = sem("mx_logit_done")
        lg_done = sem("mx_lg_done")
        soft_step = sem("mx_soft_step")
        shifted_done = sem("mx_shifted_done")
        exp_done = sem("mx_exp_done")
        prob_done = sem("mx_prob_done")
        pool_mix = sem("mx_pool_mix")
        mix_step = sem("mx_mix_step")
        mix_done = sem("mx_mix_done")
        sq_done = sem("mx_sq_done")
        ssum_done = sem("mx_ssum_done")
        rms_step = sem("mx_rms_step")
        rms_done = sem("mx_rms_done")
        on_done = sem("mx_on_done")
        oT_done = sem("mx_oT_done")
        oTe_done = sem("mx_oTe_done")
        wo_done = sem("mx_wo_done")
        x2_done = sem("mx_x2_done")
        ln_step = sem("mx_ln_step")
        ln_var_done = sem("mx_ln_var_done")
        rstd_done = sem("mx_rstd_done")
        xn_done = sem("mx_xn_done")
        hTp_done = sem("mx_hTp_done")
        modb_done = sem("mx_modb_done")
        h2T_done = sem("mx_h2T_done")
        gl_done = sem("mx_gl_done")
        gexp_done = sem("mx_gexp_done")
        route_step = sem("mx_route_step")
        comb_done = sem("mx_comb_done")
        sel_step = sem("mx_sel_step")
        up_done = sem("mx_up_done")
        silu_done = sem("mx_silu_done")
        dn_done = sem("mx_dn_done")
        sh_ev = sem("mx_sh_ev")
        dn_ev = sem("mx_dn_ev")
        fin_step = sem("mx_fin_step")
        fin_done = sem("mx_fin_done")
        store = [sem(f"mx_store{i}") for i in two]
        block = ctx.enter_context(nc.Block("mix_and_experts"))

        x_v = w.x.rearrange("b (g j p) d -> (b g) p j d", j=J, p=P)
        out_v = w.out.rearrange("b (g j p) d -> (b g) p j d", j=J, p=P)

        def by_head(a):
            return a.rearrange("p j (h d) -> p j h d", h=H)

        def spread(a):
            return a.unsqueeze(3).to_broadcast([P, J, H, DK])

        @block.sync
        def _(sp):
            sp.sem_inc(x2_done, 4)
            sp.sem_inc(fin_done, 2)
            sp.sem_inc(store[0], 16)
            sp.sem_inc(store[1], 16)
            sp.sem_inc(gexp_done, 1)
            sp.sem_inc(silu_done, 2)
            sp.sem_inc(dn_done, 4)
            sp.sem_inc(dn_ev, 2)

            def load(u, i):
                rows = bass.ds(u * J, J)
                sp.wait_ge(x2_done, u * 2 + 2)
                sp.dma_start(vf[i][:], m.vf_d[rows].rearrange("j p c -> p j c")).then_inc(loaded[i], 16)
                sp.dma_start(fl[i][:], m.fl_d[rows].rearrange("j p c -> p j c")).then_inc(loaded[i], 16)
                sp.dma_start(dl[i][:], m.o_d[rows].rearrange("j p c -> p j c")).then_inc(loaded[i], 16)
                sp.dma_start(xx[i][:], x_v[bass.ds(u, 1)].squeeze(0)).then_inc(loaded[i], 16)
                sp.dma_start(hT[i][:], m.hT_d[bass.ds(u, 1)].squeeze(0)).then_inc(loaded[i], 16)

            load(0, 0)
            sp.dma_start(sup[:], w.shared_up.rearrange("(k p) n -> p k n", p=P)).then_inc(w_in, 16)
            sp.dma_start(sdn[:], w.shared_down.rearrange("(k p) n -> p k n", p=P)).then_inc(w_in, 16)
            for k in range(KD):
                sp.dma_start(eup[:, k], w.expert_up[:, k * P:(k + 1) * P, :].rearrange("e p i -> p e i"))\
                    .then_inc(w_in, 16)
            sp.dma_start(edn[:], w.expert_down.rearrange("e i h -> i e h")).then_inc(w_in, 16)
            load(1, 1)

            def put(u, i):
                sp.wait_ge(fin_done, u + 3)
                sp.dma_start(out_v[bass.ds(u, 1)].squeeze(0), acc[i][:]).then_inc(store[i], 16)

            with sp.Fori(1, NU // 2) as t:
                for i in two:
                    load(t * 2 + i, i)
                    put(t * 2 + i - 2, i)
            for i in two:
                put(NU - 2 + i, i)
            sp.wait_ge(w_in, 16 * 5)
            for i in two:
                sp.wait_ge(store[i], 16 + 16 * NU // 2)

        @block.gpsimd
        def _(pool):
            n = 0
            pool.memset(gsel[:], 1.0).then_inc(const_done, 1)
            pool.memset(esel[:], 1.0).then_inc(const_done, 1)
            pool.wait_ge(const_done, 2)
            pool.affine_select(out=gsel[:], in_=gsel[:], compare_op=ALU.is_gt, fill=0.0, base=0,
                               pattern=[[0, J], [1, NG], [-1, NG]], channel_multiplier=0).then_inc(const_done, 1)
            pool.affine_select(out=esel[:], in_=esel[:], compare_op=ALU.is_gt, fill=0.0, base=0,
                               pattern=[[1, E], [-1, E]], channel_multiplier=0).then_inc(const_done, 1)

            def mix(u, i):
                for half in two:
                    n = NR // 2
                    part = slice(half * n, (half + 1) * n)
                    pool.wait_ge(var_done, u * 2 + (half + 1))
                    std = st[:, half * J // 2:(half + 1) * J // 2].rearrange("p j (k s h) -> p (j k) s h", k=K3, s=2)
                    pool.tensor_tensor(std[:, :, 1, :], tmp[:, 2, part].rearrange("p (a h) -> p a h", h=H),
                                       m.root_pow[:, part].rearrange("p (a h) -> p a h", h=H), ALU.pow)\
                        .then_inc(std_done, 1)
                pool.wait_ge(prob_done, u + 1)
                pool.tensor_tensor(by_head(t0[:]), by_head(vf[i][:, :, 0:D]), spread(ids[:]), ALU.mult)\
                    .then_inc(pool_mix, 1)
                p0 = pr[:].rearrange("p (j h) c -> p j h c", h=H)[:, :, :, 0]
                pool.tensor_tensor(by_head(t1[:]), by_head(vf[i][:, :, D:]), spread(p0), ALU.mult)\
                    .then_inc(pool_mix, 1)
                pool.wait_ge(ssum_done, u + 1)
                pool.tensor_tensor(rms[:], rms[:], m.half_pow[:, 0:NH], ALU.pow).then_inc(rms_done, 1)
                pool.wait_ge(ln_var_done, u + 1)
                pool.tensor_tensor(rstd[:], mv[:, :, 1], m.half_pow[:, 0:J], ALU.pow).then_inc(rstd_done, 1)

            def finish(u, i):
                pool.wait_ge(dn_ev, u * E + (E + 2))
                pool.tensor_tensor(acc[i][:], acc[i][:], m.gbB[:, bass.ds(u // UB, 1), :].to_broadcast([P, J, D]),
                                   ALU.mult).then_inc(fin_step, 1)
                pool.wait_ge(fin_step, u + 1)
                pool.tensor_tensor(acc[i][:], acc[i][:], x2[i][:], ALU.add).then_inc(fin_done, 1)

            def front(u, g):
                mix(u, g % 2)

            def body(u, g, nxt):
                if nxt is not None:
                    mix(nxt, (g + 1) % 2)
                finish(u, g % 2)

            units_ahead(pool, front, body)

        @block.tensor
        def _(pe):
            def mix(u, i, s):
                if s == 7:
                    pe.wait_ge(std_done, u * 2 + 2)
                    pe.wait_ge(gexp_done, u + 1)
                    for j in range(J):
                        ins = pe.transpose(M[0][0:K3 * 2 * H, j * P:(j + 1) * P], st[:, j, :], m.ident[:])
                    ins.then_inc(stT_done, 1)
                if 8 <= s < 12:
                    f = s - 8
                    if f == 0:
                        pe.wait_ge(loaded[i], (u - i) * 40 + 80)
                    pe.wait_ge(stTe_done, u + 1)
                    if f >= 2:
                        pe.wait_ge(gelu_done, u * 4 + (f - 1))
                    out = M[(f + 1) % 2]
                    for k in range(KD):
                        pe.matmul(out[:], m.wr1[:, k, f * P:(f + 1) * P], hT[i][:, k, :], start=(k == 0), stop=False)
                    pe.matmul(out[:], m.wr1s[:, f * P:(f + 1) * P], stT[:], start=False, stop=True)\
                        .then_inc(hmid_done, 1)
                if 14 <= s < 16:
                    if s == 14:
                        pe.wait_ge(gelu_done, u * 4 + 4)
                    for j in (2 * (s - 14), 2 * (s - 14) + 1):
                        out = M[1][:, j * 12:j * 12 + 12]
                        for f in range(RH // P):
                            pe.matmul(out, hm[:, f, j * P:(j + 1) * P], m.wr2[:, f, :], start=(f == 0), stop=False)
                        ins = pe.matmul(out, m.ones[0:1, :], m.br2[0:1, :], start=False, stop=True)
                    if s == 15:
                        ins.then_inc(logit_done, 1)
                if s == 29:
                    pe.wait_ge(on_done, u + 1)
                    for k in range(KD):
                        for j in range(J):
                            ins = pe.transpose(M[k][:, j * P:(j + 1) * P], t3[:, j, k * P:(k + 1) * P], m.ident[:])
                        ins.then_inc(oT_done, 1)
                if s == 30:
                    pe.wait_ge(oTe_done, u * 2 + 2)
                    for jj in two:
                        for j in (2 * jj, 2 * jj + 1):
                            for k in range(KD):
                                ins = pe.matmul(M[jj][:, (j % 2) * D:(j % 2 + 1) * D], oT[:, k, j * P:(j + 1) * P],
                                                m.wog[:, bass.ds(u // UB, 1), k, :].squeeze(1),
                                                start=(k == 0), stop=(k == KD - 1))
                        ins.then_inc(wo_done, 1)
                if s == 35:
                    pe.wait_ge(xn_done, u + 1)
                    for k in range(KD):
                        for j in range(J):
                            ins = pe.transpose(M[k][:, j * P:(j + 1) * P], t3[:, j, k * P:(k + 1) * P], m.ident[:])
                        ins.then_inc(hTp_done, 1)
                if s == 38:
                    pe.wait_ge(h2T_done, u + 1)
                    for j in range(J):
                        for k in range(KD):
                            ins = pe.matmul(M[0][:, j * E:(j + 1) * E], h2T[i][:, k, j * P:(j + 1) * P],
                                            m.wgT[:, k, :], start=(k == 0), stop=(k == KD - 1))
                    ins.then_inc(gl_done, 1)

            def up(u, i, x):
                pe.wait_ge(silu_done, u * NX + (x + 1))
                for k in range(KD):
                    lhs = sup[:, k, x * P:(x + 1) * P] if x < NS else eup[:, k, x - NS, :]
                    ins = pe.matmul(up_ps[x % 2][:], lhs, h2T[i][:, k, :], start=(k == 0), stop=(k == KD - 1))
                ins.then_inc(up_done, 1)

            def down(u, i, x):
                n = max(x - NS + 1, 0)
                pe.wait_ge(silu_done, u * NX + (x + 3))
                if n == 2:
                    pe.wait_ge(sh_ev, u + 1)
                elif x == 0 or x >= NS:
                    pe.wait_ge(dn_ev, u * E + (n + 1 if n < 2 else n))
                rhs = sdn[:, x, :] if x < NS else edn[:, x - NS, :]
                for j in range(J):
                    ins = pe.matmul(dn_ps[(i + n) % 2][:, j, :], hs[x % 4][:, j * P:(j + 1) * P], rhs,
                                    start=(x == 0 and j % 2 == 0) or x >= NS, stop=(x >= NS - 1),
                                    skip_group_check=True)
                ins.then_inc(dn_done, 1)

            def front(u, g):
                for s in range(2 * NX):
                    mix(u, g % 2, s)

            def body(u, g, nxt):
                i = g % 2
                up(u, i, 0)
                for x in range(NX):
                    if x < NX - 1:
                        up(u, i, x + 1)
                    if nxt is not None:
                        mix(nxt, 1 - i, 2 * x)
                    down(u, i, x)
                    if nxt is not None:
                        mix(nxt, 1 - i, 2 * x + 1)

            pe.wait_ge(w_in, 16 * 5)
            units_ahead(pe, front, body)

        @block.scalar
        def _(act):
            def mix(u, i, s):
                if s == 7:
                    act.wait_ge(stT_done, u + 1)
                    act.activation(stT[:], M[0][0:K3 * 2 * H, :], ACT.Copy).then_inc(stTe_done, 1)
                if 9 <= s < 13:
                    f = s - 9
                    act.wait_ge(hmid_done, u * 4 + (f + 1))
                    if f == 0 and (not isinstance(u, int) or u > 0):
                        act.wait_ge(comb_done, u)
                    act.activation(hm[:, f, :], M[(f + 1) % 2][:], ACT.Gelu, bias=m.br1[:, f:f + 1])\
                        .then_inc(gelu_done, 1)
                if s == 16:
                    act.wait_ge(shifted_done, u + 1)
                    act.activation(pr[:], pr[:], ACT.Exp).then_inc(exp_done, 1)
                if s == 22:
                    act.wait_ge(mix_done, u + 1)
                    act.activation(t0[:], t2[:], ACT.Square).then_inc(sq_done, 1)
                if s == 29:
                    for k in range(KD):
                        act.wait_ge(oT_done, u * 2 + (k + 1))
                        act.activation(oT[:, k, :], M[k][:], ACT.Copy).then_inc(oTe_done, 1)
                if s == 28:
                    if not isinstance(u, int) or u > 0:
                        act.wait_ge(h2T_done, u)
                    act.activation(modb[:].unsqueeze(2), m.mod[:, 6:10, bass.ds(u // UB, 1)], ACT.Copy)\
                        .then_inc(modb_done, 1)
                if s == 35:
                    act.wait_ge(modb_done, u + 1)
                    for k in range(KD):
                        act.wait_ge(hTp_done, u * 2 + (k + 1))
                        ins = act.activation(h2T[i][:, k, :], M[k][:], ACT.Identity, scale=modb[:, 2 + k:3 + k],
                                             bias=modb[:, k:k + 1])
                    ins.then_inc(h2T_done, 1)
                if s == 39:
                    act.wait_ge(gl_done, u + 1)
                    act.activation(sc[:].rearrange("p j e -> p (j e)"), M[0][:, 0:J * E], ACT.Exp, scale=-1.0)\
                        .then_inc(gexp_done, 1)

            def silu(u, x):
                act.wait_ge(up_done, u * NX + (x + 1))
                act.wait_ge(dn_done, u * NX + (x + 1))
                act.activation(hs[x % 4][:], up_ps[x % 2][:], ACT.Silu).then_inc(silu_done, 1)

            def front(u, g):
                for s in range(2 * NX):
                    mix(u, g % 2, s)

            def body(u, g, nxt):
                i = g % 2
                silu(u, 0)
                for x in range(NX):
                    if x < NX - 1:
                        silu(u, x + 1)
                    if x == NS:
                        act.wait_ge(dn_done, u * NX + (NS + 4))
                        act.wait_ge(store[i], (u - i) * 8 + 16)
                        act.activation(acc[i][:], dn_ps[i][:], ACT.Copy).then_inc(sh_ev, 1)
                    if nxt is not None:
                        mix(nxt, 1 - i, 2 * x)
                        mix(nxt, 1 - i, 2 * x + 1)

            units_ahead(act, front, body)

        @block.vector
        def _(dve):
            def mix(u, i, s):
                if s < 2:
                    n = NR // 2
                    part = slice(s * n, (s + 1) * n)
                    if s == 0:
                        dve.wait_ge(loaded[i], (u - i) * 40 + 80)
                    for r in range(s * n, (s + 1) * n):
                        j, kind, h = r // (K3 * H), r // H % K3, r % H
                        src = (vf[i][:, j, D:], fl[i][:, j, :], dl[i][:, j, :])[kind][:, h * DK:(h + 1) * DK]
                        ins = dve.bn_stats(bs[:, r, :], src)
                    ins.then_inc(stat_done, 1)
                    dve.wait_ge(stat_done, u * 2 + (s + 1))
                    dve.tensor_tensor(tmp[:, 0, part], bs[:, part, 1], bs[:, part, 4], ALU.add).then_inc(var_step, 1)
                    dve.tensor_tensor(tmp[:, 1, part], bs[:, part, 1], bs[:, part, 4], ALU.subtract)\
                        .then_inc(var_step, 1)
                    dve.tensor_tensor(tmp[:, 2, part], bs[:, part, 2], bs[:, part, 5], ALU.add).then_inc(var_step, 1)
                    dve.wait_ge(var_step, u * 8 + (4 * s + 3))
                    mean = st[:, s * J // 2:(s + 1) * J // 2].rearrange("p j (k s h) -> p (j k) s h", k=K3, s=2)
                    dve.tensor_scalar(mean[:, :, 0, :], tmp[:, 0, part].rearrange("p (a h) -> p a h", h=H), 0.5, None,
                                      ALU.mult)
                    dve.scalar_tensor_tensor(out=tmp[:, 1, part], in0=tmp[:, 1, part], scalar=0.25,
                                             in1=tmp[:, 1, part], op0=ALU.mult, op1=ALU.mult).then_inc(var_step, 1)
                    dve.wait_ge(var_step, u * 8 + (4 * s + 4))
                    dve.scalar_tensor_tensor(out=tmp[:, 2, part], in0=tmp[:, 2, part], scalar=1.0 / DK,
                                             in1=tmp[:, 1, part], op0=ALU.mult, op1=ALU.add).then_inc(var_done, 1)
                if s == 15:
                    n = u * 5
                    dve.wait_ge(logit_done, u + 1)
                    dve.tensor_tensor(pr[:].rearrange("p (j h) c -> p j h c", h=H),
                                      M[1][:, 0:NH * 3].rearrange("p (j h c) -> p j h c", j=J, h=H),
                                      m.rtau[:].unsqueeze(1).unsqueeze(3).to_broadcast([P, J, H, 3]), ALU.mult)\
                        .then_inc(lg_done, 1)
                    dve.wait_ge(lg_done, u + 1)
                    dve.tensor_reduce(red[:], pr[:], AX_X, ALU.max).then_inc(soft_step, 1)
                    dve.wait_ge(soft_step, n + 1)
                    dve.tensor_tensor(pr[:], pr[:], red[:].unsqueeze(2).to_broadcast([P, NH, 3]), ALU.subtract)\
                        .then_inc(shifted_done, 1)
                    idg = m.gates[:, bass.ds(u * (J * 8), J * 8)].rearrange("p (j c) -> p j c", c=8)[:, :, H:]
                    dve.tensor_tensor(ids[:], idg, m.alpha[:].unsqueeze(1).to_broadcast([P, J, H]), ALU.mult)\
                        .then_inc(soft_step, 1)
                if s == 17:
                    n = u * 5
                    dve.wait_ge(exp_done, u + 1)
                    dve.tensor_reduce(red[:], pr[:], AX_X, ALU.add).then_inc(soft_step, 1)
                    dve.wait_ge(soft_step, n + 3)
                    dve.tensor_scalar(ids[:], ids[:], EPS_ID, None, ALU.add)
                    dve.reciprocal(red[:], red[:]).then_inc(soft_step, 1)
                    dve.wait_ge(soft_step, n + 4)
                    dve.tensor_tensor(pr[:], pr[:], red[:].unsqueeze(2).to_broadcast([P, NH, 3]), ALU.mult)\
                        .then_inc(soft_step, 1)
                    dve.wait_ge(soft_step, n + 5)
                    dve.tensor_scalar(pr[:], pr[:], 1.0 - 3.0 * R_EPS, R_EPS, ALU.mult, ALU.add)\
                        .then_inc(prob_done, 1)
                pc = pr[:].rearrange("p (j h) c -> p j h c", h=H)
                if s == 18:
                    dve.wait_ge(prob_done, u + 1)
                    dve.tensor_tensor(by_head(t2[:]), by_head(fl[i][:]), spread(pc[:, :, :, 1]), ALU.mult)\
                        .then_inc(mix_step, 1)
                    dve.tensor_tensor(by_head(t3[:]), by_head(dl[i][:]), spread(pc[:, :, :, 2]), ALU.mult)\
                        .then_inc(mix_step, 1)
                if s == 19:
                    dve.wait_ge(mix_step, u * 4 + 2)
                    dve.tensor_tensor(t2[:], t2[:], t3[:], ALU.add).then_inc(mix_step, 1)
                if s == 21:
                    dve.wait_ge(mix_step, u * 4 + 3)
                    dve.wait_ge(pool_mix, u * 2 + 2)
                    dve.tensor_tensor(t2[:], t2[:], t0[:], ALU.add).then_inc(mix_step, 1)
                    dve.wait_ge(mix_step, u * 4 + 4)
                    dve.tensor_tensor(t2[:], t2[:], t1[:], ALU.add).then_inc(mix_done, 1)
                if s == 23:
                    dve.wait_ge(sq_done, u + 1)
                    dve.tensor_reduce(rms[:], by_head(t0[:]).rearrange("p j h d -> p (j h) d"), AX_X, ALU.add)\
                        .then_inc(rms_step, 1)
                    dve.wait_ge(rms_step, u + 1)
                    dve.tensor_scalar(rms[:], rms[:], 1.0 / DK, RMS_EPS, ALU.mult, ALU.add).then_inc(ssum_done, 1)
                if s == 25:
                    dve.wait_ge(rms_done, u + 1)
                    dve.tensor_tensor(by_head(t3[:]), by_head(t2[:]),
                                      spread(rms[:].rearrange("p (j h) -> p j h", h=H)), ALU.mult)\
                        .then_inc(on_done, 1)
                if s == 29:
                    for jj in two:
                        dve.wait_ge(wo_done, u * 2 + (jj + 1))
                        if jj == 0:
                            dve.wait_ge(fin_done, u + 1)
                        dve.tensor_tensor(x2[i][:, 2 * jj:2 * jj + 2, :], xx[i][:, 2 * jj:2 * jj + 2, :],
                                          M[jj][:].rearrange("p (j d) -> p j d", d=D), ALU.add)\
                            .then_inc(x2_done, 1)
                if s == 31:
                    dve.wait_ge(x2_done, u * 2 + 6)
                    for j in range(J):
                        dve.bn_stats(st2[:, j, :], x2[i][:, j, :]).then_inc(ln_step, 1)
                    dve.wait_ge(ln_step, u * (2 * J) + J)
                    dve.memset(ws[:], 0.0)
                    for j in range(J):
                        dve.bn_aggr(mv[:, j, :], st2[:, j, :]).then_inc(ln_step, 1)
                    dve.wait_ge(ln_step, u * (2 * J) + 2 * J)
                    dve.tensor_scalar(mv[:, :, 1], mv[:, :, 1], LN_EPS, None, ALU.add).then_inc(ln_var_done, 1)
                if s == 33:
                    dve.wait_ge(rstd_done, u + 1)
                    for j in range(J):
                        ins = dve.tensor_scalar(t3[:, j, :], x2[i][:, j, :], mv[:, j, 0:1], rstd[:, j:j + 1],
                                                ALU.subtract, ALU.mult)
                    ins.then_inc(xn_done, 1)

            def route(u, i, s):
                n = u * 17
                flat = sc[:].rearrange("p j e -> p (j e)")
                quad = sc[:].rearrange("p j (g a b) -> p (j g) a b", g=NG, b=2)
                if s == 0:
                    dve.wait_ge(gexp_done, u + 2)
                    dve.tensor_scalar(flat, flat, 1.0, None, ALU.add).then_inc(route_step, 1)
                    dve.wait_ge(route_step, n + 1)
                    dve.reciprocal(flat, flat).then_inc(route_step, 1)
                    dve.wait_ge(route_step, n + 2)
                    dve.tensor_tensor(hi[:], quad[:, :, :, 0], quad[:, :, :, 1], ALU.max).then_inc(route_step, 1)
                    dve.tensor_tensor(lo[:], quad[:, :, :, 0], quad[:, :, :, 1], ALU.min).then_inc(route_step, 1)
                    dve.wait_ge(route_step, n + 4)
                    dve.tensor_tensor(gs[:, 0, :], hi[:, :, 0], hi[:, :, 1], ALU.max)
                    dve.tensor_tensor(gs[:, 1, :], hi[:, :, 0], hi[:, :, 1], ALU.min)
                    dve.tensor_tensor(gs[:, 2, :], lo[:, :, 0], lo[:, :, 1], ALU.max).then_inc(route_step, 1)
                    dve.wait_ge(route_step, n + 5)
                    dve.tensor_tensor(gs[:, 1, :], gs[:, 1, :], gs[:, 2, :], ALU.max).then_inc(route_step, 1)
                    dve.wait_ge(route_step, n + 6)
                    dve.tensor_tensor(gs[:, 3, :], gs[:, 0, :], gs[:, 1, :], ALU.add).then_inc(route_step, 1)
                if s == 1:
                    dve.wait_ge(route_step, n + 7)
                    g = gs[:, 3, :].rearrange("p (j g) -> p j g", g=NG)
                    other = g.unsqueeze(2).to_broadcast([P, J, NG, NG])
                    own = g.unsqueeze(3).to_broadcast([P, J, NG, NG])
                    dve.tensor_tensor(gq[:, 0], other, own, ALU.is_gt)
                    dve.tensor_tensor(gq[:, 1], other, own, ALU.is_equal).then_inc(route_step, 1)
                    dve.wait_ge(route_step, n + 8)
                    dve.tensor_tensor(gq[:, 1], gq[:, 1], gsel[:], ALU.mult).then_inc(route_step, 1)
                    dve.wait_ge(route_step, n + 9)
                    dve.tensor_tensor(gq[:, 0], gq[:, 0], gq[:, 1], ALU.add).then_inc(route_step, 1)
                    dve.wait_ge(route_step, n + 10)
                    dve.tensor_reduce(gm[:], gq[:, 0].rearrange("p j g h -> p (j g) h"), AX_X, ALU.add)\
                        .then_inc(route_step, 1)
                    dve.wait_ge(route_step, n + 11)
                    dve.tensor_scalar(gm[:], gm[:], 2.0, None, ALU.is_lt).then_inc(route_step, 1)
                    dve.wait_ge(route_step, n + 12)
                    dve.tensor_tensor(ms[:].rearrange("p j (g a) -> p (j g) a", g=NG),
                                      sc[:].rearrange("p j (g a) -> p (j g) a", g=NG),
                                      gm[:].unsqueeze(2).to_broadcast([P, J * NG, E // NG]), ALU.mult)\
                        .then_inc(route_step, 1)
                if s == 2:
                    dve.wait_ge(route_step, n + 13)
                    other = ms[:].unsqueeze(2).to_broadcast([P, J, E, E])
                    own = ms[:].unsqueeze(3).to_broadcast([P, J, E, E])
                    dve.tensor_tensor(rq[:, 0], other, own, ALU.is_gt)
                    dve.tensor_tensor(rq[:, 1], other, own, ALU.is_equal).then_inc(route_step, 1)
                    dve.wait_ge(route_step, n + 14)
                    dve.tensor_tensor(rq[:, 1], rq[:, 1], esel[:].unsqueeze(1).to_broadcast([P, J, E, E]), ALU.mult)\
                        .then_inc(route_step, 1)
                if s == 3:
                    dve.wait_ge(route_step, n + 15)
                    dve.tensor_tensor(rq[:, 0], rq[:, 0], rq[:, 1], ALU.add).then_inc(route_step, 1)
                    dve.wait_ge(route_step, n + 16)
                    dve.tensor_reduce(rk[:].rearrange("p j e -> p (j e)"), rq[:, 0].rearrange("p j a b -> p (j a) b"),
                                      AX_X, ALU.add).then_inc(route_step, 1)
                    dve.wait_ge(route_step, n + 17)
                    dve.scalar_tensor_tensor(out=ms[:].rearrange("p j e -> p (j e)"),
                                             in0=rk[:].rearrange("p j e -> p (j e)"), scalar=float(TOPK), in1=flat,
                                             op0=ALU.is_lt, op1=ALU.mult).then_inc(sel_step, 1)
                    dve.wait_ge(sel_step, u * 4 + 1)
                    dve.tensor_reduce(ws[:], ms[:], AX_X, ALU.add).then_inc(sel_step, 1)
                    dve.wait_ge(sel_step, u * 4 + 2)
                    dve.tensor_scalar(ws[:], ws[:], 1e-20, None, ALU.add).then_inc(sel_step, 1)
                    dve.wait_ge(sel_step, u * 4 + 3)
                    dve.reciprocal(ws[:], ws[:]).then_inc(sel_step, 1)
                    dve.wait_ge(sel_step, u * 4 + 4)
                    for j in range(J):
                        ins = dve.tensor_scalar(comb[i][:, j, :], ms[:, j, :], ws[:, j:j + 1], SCALING, ALU.mult,
                                                ALU.mult)
                    ins.then_inc(comb_done, 1)

            def expert(u, i, e):
                n = e + 1
                if e == 0:
                    dve.wait_ge(comb_done, u + 1)
                dve.wait_ge(dn_done, u * NX + (NS + e + 5))
                if e == 0:
                    dve.wait_ge(sh_ev, u + 1)
                else:
                    dve.wait_ge(dn_ev, u * E + (e + 2))
                for j in range(J):
                    ins = dve.scalar_tensor_tensor(out=acc[i][:, j, :], in0=dn_ps[(i + n) % 2][:, j, :],
                                                   scalar=comb[i][:, j, e:e + 1], in1=acc[i][:, j, :],
                                                   op0=ALU.mult, op1=ALU.add)
                ins.then_inc(dn_ev, 1)

            def front(u, g):
                for s in range(2 * NX):
                    mix(u, g % 2, s)

            def body(u, g, nxt):
                i = g % 2
                for x in range(NX):
                    if x >= NS:
                        expert(u, i, x - NS)
                    if nxt is not None:
                        mix(nxt, 1 - i, 2 * x)
                        mix(nxt, 1 - i, 2 * x + 1)
                    if x < NS:
                        route(u, i, x)

            dve.wait_ge(const_done, 4)
            units_ahead(dve, front, body)


def build(nc, x, Wq, Wk, Wv, Wb, conv_q, conv_k, conv_v, fir_short, fir_long, alpha_id, Wid, bid, Wr1, br1,
          Wr2, br2, log_tau_group, log_tau_head, o_norm_w, Wo, gate_weight, expert_up, expert_down, shared_up,
          shared_down, c, wmod, out):
    w = Bag()
    w.x, w.Wq, w.Wk, w.Wv = x, Wq, Wk, Wv
    w.Wb, w.conv_q, w.conv_k, w.conv_v = Wb, conv_q, conv_k, conv_v
    w.fir_short, w.fir_long, w.alpha_id, w.Wid = fir_short, fir_long, alpha_id, Wid
    w.bid, w.Wr1, w.br1, w.Wr2 = bid, Wr1, br1, Wr2
    w.br2, w.log_tau_group, w.log_tau_head, w.o_norm_w = br2, log_tau_group, log_tau_head, o_norm_w
    w.Wo, w.gate_weight, w.expert_up, w.expert_down = Wo, gate_weight, expert_up, expert_down
    w.shared_up, w.shared_down, w.c, w.wmod = shared_up, shared_down, c, wmod
    w.out = out
    m = Bag()

    def dram(name, shape):
        return nc.dram_tensor(name, shape, F32).ap()

    m.hT_d = dram("hT_d", (NU, P, KD, UT))
    m.vf_d = dram("vf_d", (NT, P, 2 * D))
    m.kq_d = dram("kq_d", (NT, P, 2 * D))
    m.kqT_d = dram("kqT_d", (NT, P, 4 * P))
    m.fl_d = dram("fl_d", (NT, P, D))
    m.o_d = dram("o_d", (NT, P, D))
    m.taps_d = dram("taps_d", (D, TAPROW))
    with ExitStack() as ctx:
        def sb(name, shape):
            return ctx.enter_context(nc.sbuf_tensor(name, shape, F32))
        m.levels = [2, 4, 8, 16, 32, 64]
        m.ident = sb("ident", [P, P])
        m.flip = sb("flip", [P, P])
        m.ones = sb("ones", [P, P])
        m.lower = sb("lower", [P, P])
        m.upper = sb("upper", [P, H, P])
        m.first_lower = sb("first_lower", [P, H, P])
        m.level_mask = [sb(f"level_mask{s}", [P, H, P // 2]) for s in m.levels]
        m.zeros = sb("zeros_small", [P, 32])
        m.half_pow = sb("half_pow", [P, 64])
        m.root_pow = sb("root_pow", [P, 64])
        m.l2_eps = sb("l2_eps", [P, 16])
        m.conv_w = sb("conv_w", [P, 6, CONV])
        m.alpha = sb("alpha", [P, H])
        m.rtau = sb("rtau", [P, H])
        m.mod = sb("mod", [P, 12, B])
        m.gbB = sb("gbB", [P, B, D])
        m.wog = sb("wog", [P, B, KD, D])
        m.diag_fs = sb("diag_fs", [P, KD, FIRS, P])
        m.wqkv = sb("wqkv", [P, KD, 3 * D])
        m.wgate = sb("wgate", [P, KD, 8])
        m.bid_row = sb("bid_row", [1, 8])
        m.wr1 = sb("wr1", [P, KD, RH])
        m.wr1s = sb("wr1s", [6 * H, RH])
        m.br1 = sb("br1", [P, RH // P])
        m.wr2 = sb("wr2", [P, RH // P, 3 * H])
        m.br2 = sb("br2", [1, 3 * H])
        m.wgT = sb("wgT", [P, KD, E])
        m.gates = sb("gates", [P, NT * 8])
        for stage in STAGES:
            stage(nc, m, w)


STAGES = [setup, norm_inputs, conv_heads, long_filter, delta_rule, mix_and_experts]

_INS = ['x', 'Wq', 'Wk', 'Wv', 'Wb', 'conv_q', 'conv_k', 'conv_v', 'fir_short', 'fir_long', 'alpha_id', 'Wid', 'bid',
        'Wr1', 'br1', 'Wr2', 'br2', 'log_tau_group', 'log_tau_head', 'o_norm_w', 'Wo', 'gate_weight', 'expert_up',
        'expert_down', 'shared_up', 'shared_down', 'c', 'wmod']
_INS = [("L0_attn_hidden_states" if n == 'x' else f"L0_{n}" if n in ('c', 'wmod') else
         f"L0_ffn_{n}" if n in ('gate_weight', 'expert_up', 'expert_down', 'shared_up', 'shared_down') else
         f"L0_attn_{n}") for n in _INS]
_OUTS = [((B, L, D), 'float32')]


def kernel(**inputs):
    import numpy as _np
    import concourse.bacc as _bacc
    from concourse import mybir as _mybir
    from concourse.bass_utils import run_bass_kernel_spmd as _run

    nc = _bacc.Bacc("TRN2", target_bir_lowering=False, num_devices=1)
    arrays, args = {}, []
    for name in _INS:
        a = _np.ascontiguousarray(inputs[name])
        arrays[f"in_{name}_dram"] = a
        args.append(nc.dram_tensor(f"in_{name}_dram", a.shape, _mybir.dt.from_np(a.dtype), kind="ExternalInput").ap())
    for i, (shape, dtype) in enumerate(_OUTS):
        dt = _mybir.dt.from_np(_np.dtype(dtype))
        args.append(nc.dram_tensor(f"out_{i}_dram", shape, dt, kind="ExternalOutput").ap())
    build(nc, *args)
    r = _run(nc, [arrays], core_ids=[0])
    got = tuple(r.results[0][f"out_{i}_dram"] for i in range(len(_OUTS)))
    return got[0]
```
